# Optimizing a Trainium2 kernel written in Bass

```python
import numpy as np
import jax
import jax.numpy as jnp

def _softmax(x, axis=-1):
    return jax.nn.softmax(x, axis=axis)

def _gelu(x):
    return jax.nn.gelu(x, approximate=True)

def _silu(x):
    return jax.nn.silu(x)

def _sigmoid(x):
    return jax.nn.sigmoid(x)

def _layernorm(x, axis=-1, eps=1e-05):
    m = jnp.mean(x, axis=axis, keepdims=True)
    v = jnp.var(x, axis=axis, keepdims=True)
    return (x - m) / jnp.sqrt(v + eps)

def _scatter_add(tgt, idx, src, axis=0):
    return tgt.at[idx].add(src)

def _segment_sum(src, seg, n):
    return jax.ops.segment_sum(src, seg, n)
kernel_name = 'mk_flamingo_gated_d4_seqx_r4_ad3fdd'

def setup_inputs(seed: int=0):
    np.random.seed(seed)
    _w = jnp.asarray

    def _rec_inputs():
        import jax
        import jax.numpy as jnp
        _rk = jax.random.key(seed)
        x = 0.0002417 + 0.9998 * jax.random.normal(jax.random.fold_in(_rk, 1), (2, 512, 256), jnp.float32)
        _lenS = 512 - jax.random.randint(jax.random.fold_in(_rk, 7), (2,), 0, max(1, 512 // 4) + 1, jnp.int32)
        _lenS2 = 1024 - jax.random.randint(jax.random.fold_in(_rk, 8), (2,), 0, max(1, 1024 // 4) + 1, jnp.int32)
        _ctx_1024P = jax.random.normal(jax.random.fold_in(_rk, 11), (2, 16, 256), jnp.float32)
        _ctx_1024c = jax.random.dirichlet(jax.random.fold_in(_rk, 511), 0.3 * jnp.ones((16,), jnp.float32), (2, 1024))
        _ctx_1024t = jnp.einsum('bsk,bkd->bsd', _ctx_1024c, _ctx_1024P)
        _ctx_1024t = _ctx_1024t * jax.lax.rsqrt(jnp.mean(jnp.square(_ctx_1024t)) + 1e-12) * 0.953939
        ctx_1024 = 7.22013e-05 + 1.00017 * (_ctx_1024t + 0.3 * jax.random.normal(jax.random.fold_in(_rk, 611), (2, 1024, 256), jnp.float32))
        _validS = jnp.arange(512)[None, :] < _lenS[:, None]
        _validS2 = jnp.arange(1024)[None, :] < _lenS2[:, None]
        _causal = jnp.tril(jnp.ones((512, 512), dtype=bool))
        mask_BxS2_if0 = jnp.where(jnp.ones((2, 1024), dtype=bool), 0, 1).astype(jnp.int32)
        _g = jax.random.normal(jax.random.fold_in(_rk, 9001), (2, 4), jnp.float32)
        _g = jnp.sign(_g) * jnp.maximum(jnp.abs(_g), 1.0) + (_g == 0) * 1.0
        g_xattn = _g[0]
        g_ffn = _g[1]
        return (x, ctx_1024, mask_BxS2_if0, g_xattn, g_ffn)
    x, ctx_1024, mask_BxS2_if0, g_xattn, g_ffn = _rec_inputs()

    def _L0_xattn_setup():
        import jax, jax.numpy as jnp
        import numpy as np
        import math
        B, M, D, H, NK = (4, 512, 256, 16, 5)
        HD = D // H

        def _gather_pad0(x, idx):
            Bx, Hx, W, hd = x.shape
            valid = (idx >= 0) & (idx < W)
            idxc = jnp.clip(idx, 0, W - 1).reshape(Bx, Hx, -1)
            g = jnp.take_along_axis(x, idxc[..., None], axis=2)
            g = g.reshape(idx.shape + (hd,))
            return g * valid[..., None].astype(x.dtype)
        key = jax.random.key(seed)
        ks = jax.random.split(key, 9)
        w = lambda k, shape: jax.random.normal(k, shape, jnp.float32) * 0.02
        return {'k': jax.random.normal(ks[0], (B, M, D), jnp.float32), 'v': jax.random.normal(ks[1], (B, M, D), jnp.float32), 'q': jax.random.normal(ks[2], (B, M, D), jnp.float32), 'mask': jnp.zeros((B, M), jnp.int32), 'Wk': w(ks[3], (D, D)), 'bk': jnp.zeros((D,), jnp.float32), 'Wv': w(ks[4], (D, D)), 'bv': jnp.zeros((D,), jnp.float32), 'Wq': w(ks[5], (D, D)), 'bq': jnp.zeros((D,), jnp.float32), 'Woff': w(ks[6], (H * NK, D)), 'boff': jnp.zeros((H * NK,), jnp.float32), 'Wo': w(ks[7], (D, D)), 'bo': jnp.zeros((D,), jnp.float32)}
    _L0_xattn_all = _L0_xattn_setup()
    _L0_xattn_in = {k: v for k, v in _L0_xattn_all.items() if k in ('Wk', 'bk', 'Wv', 'bv', 'Wq', 'bq', 'Woff', 'boff', 'Wo', 'bo')}
    del _L0_xattn_all

    def _L0_ffn_setup():
        import jax, jax.numpy as jnp
        import numpy as np
        INT8_MAX = 127.0

        def _absmax_scale(x, axes):
            amax = jnp.max(jnp.abs(x), axis=axes, keepdims=True)
            return jnp.maximum(amax, 1e-12) / INT8_MAX
        key = jax.random.key(seed)
        k1, k2 = jax.random.split(key)
        lhs = jax.random.normal(k1, (4, 2048, 256), dtype=jnp.float32)
        rhs = jax.random.normal(k2, (256, 256), dtype=jnp.float32)
        return {'lhs': lhs, 'rhs': rhs}
    _L0_ffn_all = _L0_ffn_setup()
    _L0_ffn_in = {k: v for k, v in _L0_ffn_all.items() if k in ('rhs',)}
    del _L0_ffn_all

    def _L1_xattn_setup():
        import jax, jax.numpy as jnp
        import numpy as np
        D_MODEL = 256
        N_HEADS = 16
        DH = D_MODEL // N_HEADS // 2
        B, S = (4, 512)
        key = jax.random.key(seed)
        ks = jax.random.split(key, 8)
        scale_in = 1.0
        q = jax.random.normal(ks[0], (B, S, D_MODEL), dtype=jnp.float32)
        k = jax.random.normal(ks[1], (B, S, D_MODEL), dtype=jnp.float32)
        v = jax.random.normal(ks[2], (B, S, D_MODEL), dtype=jnp.float32)
        w_std = (2.0 / (D_MODEL + DH)) ** 0.5
        Wq = jax.random.normal(ks[3], (N_HEADS, D_MODEL, DH), dtype=jnp.float32) * w_std
        Wk = jax.random.normal(ks[4], (N_HEADS, D_MODEL, DH), dtype=jnp.float32) * w_std
        Wv = jax.random.normal(ks[5], (N_HEADS, D_MODEL, DH), dtype=jnp.float32) * w_std
        wo_std = (2.0 / (N_HEADS * DH + D_MODEL)) ** 0.5
        Wo = jax.random.normal(ks[6], (N_HEADS * DH, D_MODEL), dtype=jnp.float32) * wo_std
        return {'q': q, 'k': k, 'v': v, 'Wq': Wq, 'Wk': Wk, 'Wv': Wv, 'Wo': Wo}
    _L1_xattn_all = _L1_xattn_setup()
    _L1_xattn_in = {k: v for k, v in _L1_xattn_all.items() if k in ('Wq', 'Wk', 'Wv', 'Wo')}
    del _L1_xattn_all

    def _L1_ffn_setup():
        import jax, jax.numpy as jnp
        import numpy as np
        DIM = 256
        INNER = 1024
        E = 8
        EPS = 1e-06
        key = jax.random.key(seed)
        k_x, k_wg, k_bg, k_w1, k_w2 = jax.random.split(key, 5)
        x = jax.random.normal(k_x, (4, 512, DIM), dtype=jnp.float32)
        Wg = jax.random.normal(k_wg, (DIM, E), dtype=jnp.float32) / np.sqrt(DIM)
        bg = jax.random.normal(k_bg, (E,), dtype=jnp.float32) * 0.01
        W1 = jax.random.normal(k_w1, (E, DIM, INNER), dtype=jnp.float32) / np.sqrt(DIM)
        W2 = jax.random.normal(k_w2, (E, INNER, DIM), dtype=jnp.float32) / np.sqrt(INNER)
        return {'x': x, 'Wg': Wg, 'bg': bg, 'W1': W1, 'W2': W2}
    _L1_ffn_all = _L1_ffn_setup()
    _L1_ffn_in = {k: v for k, v in _L1_ffn_all.items() if k in ('Wg', 'bg', 'W1', 'W2')}
    del _L1_ffn_all

    def _L2_xattn_setup():
        import jax, jax.numpy as jnp
        import numpy as np
        B, L, D_MODEL, N_HEADS = (4, 512, 256, 16)
        HEAD_DIM = D_MODEL // N_HEADS
        key = jax.random.key(seed)
        ks = jax.random.split(key, 11)
        s = 1.0 / np.sqrt(D_MODEL)
        return {'queries': jax.random.normal(ks[0], (B, L, D_MODEL), jnp.float32), 'keys': jax.random.normal(ks[1], (B, L, D_MODEL), jnp.float32), 'values': jax.random.normal(ks[2], (B, L, D_MODEL), jnp.float32), 'Wq': jax.random.normal(ks[3], (D_MODEL, D_MODEL), jnp.float32) * s, 'bq': jnp.zeros((D_MODEL,), jnp.float32), 'Wk': jax.random.normal(ks[4], (D_MODEL, D_MODEL), jnp.float32) * s, 'bk': jnp.zeros((D_MODEL,), jnp.float32), 'Wv': jax.random.normal(ks[5], (D_MODEL, D_MODEL), jnp.float32) * s, 'bv': jnp.zeros((D_MODEL,), jnp.float32), 'Wo': jax.random.normal(ks[6], (D_MODEL, D_MODEL), jnp.float32) * s, 'bo': jnp.zeros((D_MODEL,), jnp.float32)}
    _L2_xattn_all = _L2_xattn_setup()
    _L2_xattn_in = {k: v for k, v in _L2_xattn_all.items() if k in ('Wq', 'bq', 'Wk', 'bk', 'Wv', 'bv', 'Wo', 'bo')}
    del _L2_xattn_all

    def _L2_ffn_setup():
        import jax, jax.numpy as jnp
        import numpy as np
        D_IN, D_HID = (256, 1024)

        def _ternary(key, shape):
            return jax.random.randint(key, shape, -1, 2).astype(jnp.float32)

        def _tlin(x, w, s):
            return jnp.einsum('bsi,oi->bso', x, w) * s
        key = jax.random.key(seed)
        ks = jax.random.split(key, 12)
        inv = lambda fan: 1.0 / np.sqrt(fan).astype(np.float32)
        return {'x': jax.random.normal(ks[0], (4, 512, D_IN), dtype=jnp.float32), 'w1_w': _ternary(ks[1], (D_HID, D_IN)), 'w1_s': jax.random.uniform(ks[2], (D_HID,), dtype=jnp.float32) * inv(D_IN), 'w2_w': _ternary(ks[3], (D_HID, D_IN)), 'w2_s': jax.random.uniform(ks[4], (D_HID,), dtype=jnp.float32) * inv(D_IN), 'h1_w': _ternary(ks[5], (D_HID, D_HID)), 'h1_s': jax.random.uniform(ks[6], (D_HID,), dtype=jnp.float32) * inv(D_HID), 'h2_w': _ternary(ks[7], (D_HID, D_HID)), 'h2_s': jax.random.uniform(ks[8], (D_HID,), dtype=jnp.float32) * inv(D_HID), 'w3_w': _ternary(ks[9], (D_IN, D_HID)), 'w3_s': jax.random.uniform(ks[10], (D_IN,), dtype=jnp.float32) * inv(D_HID)}
    _L2_ffn_all = _L2_ffn_setup()
    _L2_ffn_in = {k: v for k, v in _L2_ffn_all.items() if k in ('w1_w', 'w1_s', 'w2_w', 'w2_s', 'h1_w', 'h1_s', 'h2_w', 'h2_s', 'w3_w', 'w3_s')}
    del _L2_ffn_all

    def _L3_xattn_setup():
        import jax, jax.numpy as jnp
        import numpy as np
        NUM_HEADS = 8
        D_MODEL = 256
        DIM = D_MODEL // NUM_HEADS
        HEAD_DIM = DIM // NUM_HEADS
        B, S = (4, 512)

        def _split_heads(x):
            b, s, _ = x.shape
            return x.reshape(b, s, NUM_HEADS, HEAD_DIM).transpose(0, 2, 1, 3)
        key = jax.random.key(seed)
        ks = jax.random.split(key, 11)
        sd_in = 1.0 / np.sqrt(D_MODEL)
        sd_o = 1.0 / np.sqrt(DIM)
        return {'queries': jax.random.normal(ks[0], (B, S, D_MODEL), jnp.float32), 'keys': jax.random.normal(ks[1], (B, S, D_MODEL), jnp.float32), 'values': jax.random.normal(ks[2], (B, S, D_MODEL), jnp.float32), 'Wq': jax.random.normal(ks[3], (D_MODEL, DIM), jnp.float32) * sd_in, 'bq': jnp.zeros((DIM,), jnp.float32), 'Wk': jax.random.normal(ks[4], (D_MODEL, DIM), jnp.float32) * sd_in, 'bk': jnp.zeros((DIM,), jnp.float32), 'Wv': jax.random.normal(ks[5], (D_MODEL, DIM), jnp.float32) * sd_in, 'bv': jnp.zeros((DIM,), jnp.float32), 'Wo': jax.random.normal(ks[6], (DIM, D_MODEL), jnp.float32) * sd_o, 'bo': jnp.zeros((D_MODEL,), jnp.float32)}
    _L3_xattn_all = _L3_xattn_setup()
    _L3_xattn_in = {k: v for k, v in _L3_xattn_all.items() if k in ('Wq', 'bq', 'Wk', 'bk', 'Wv', 'bv', 'Wo', 'bo')}
    del _L3_xattn_all

    def _L3_ffn_setup():
        import jax, jax.numpy as jnp
        import numpy as np
        DIM = 256

        def _reference_tuple_inner(x, W_r, W_k, W_v, mu_r, mu_k):
            B, T, C = x.shape
            x_prev = jnp.concatenate([jnp.zeros((B, 1, C), x.dtype), x[:, :-1, :]], axis=1)
            xr = mu_r * x + (1.0 - mu_r) * x_prev
            xk = mu_k * x + (1.0 - mu_k) * x_prev
            r = jax.nn.sigmoid(jnp.einsum('btc,dc->btd', xr, W_r))
            k = jnp.einsum('btc,dc->btd', xk, W_k)
            k_act = jnp.square(jax.nn.relu(k))
            out = r * jnp.einsum('btc,dc->btd', k_act, W_v)
            new_state = x[:, -1, :]
            return (out, new_state)
        key = jax.random.key(seed)
        ks = jax.random.split(key, 6)
        B, T, C = (8, 512, DIM)
        x = jax.random.normal(ks[0], (B, T, C), dtype=jnp.float32)
        s = 1.0 / np.sqrt(C)
        W_r = jax.random.uniform(ks[1], (C, C), jnp.float32, -s, s)
        W_k = jax.random.uniform(ks[2], (C, C), jnp.float32, -s, s)
        W_v = jax.random.uniform(ks[3], (C, C), jnp.float32, -s, s)
        mu_r = jax.random.uniform(ks[4], (C,), jnp.float32)
        mu_k = jax.random.uniform(ks[5], (C,), jnp.float32)
        return {'x': x, 'W_r': W_r, 'W_k': W_k, 'W_v': W_v, 'mu_r': mu_r, 'mu_k': mu_k}
    _L3_ffn_all = _L3_ffn_setup()
    _L3_ffn_in = {k: v for k, v in _L3_ffn_all.items() if k in ('W_r', 'W_k', 'W_v', 'mu_r', 'mu_k')}
    del _L3_ffn_all
    return {'x': x, 'ctx_1024': ctx_1024, 'mask_BxS2_if0': mask_BxS2_if0, 'g_xattn': g_xattn, 'g_ffn': g_ffn, 'L0_xattn_Wk': _L0_xattn_in['Wk'], 'L0_xattn_bk': _L0_xattn_in['bk'], 'L0_xattn_Wv': _L0_xattn_in['Wv'], 'L0_xattn_bv': _L0_xattn_in['bv'], 'L0_xattn_Wq': _L0_xattn_in['Wq'], 'L0_xattn_bq': _L0_xattn_in['bq'], 'L0_xattn_Woff': _L0_xattn_in['Woff'], 'L0_xattn_boff': _L0_xattn_in['boff'], 'L0_xattn_Wo': _L0_xattn_in['Wo'], 'L0_xattn_bo': _L0_xattn_in['bo'], 'L0_ffn_rhs': _L0_ffn_in['rhs'], 'L1_xattn_Wq': _L1_xattn_in['Wq'], 'L1_xattn_Wk': _L1_xattn_in['Wk'], 'L1_xattn_Wv': _L1_xattn_in['Wv'], 'L1_xattn_Wo': _L1_xattn_in['Wo'], 'L1_ffn_Wg': _L1_ffn_in['Wg'], 'L1_ffn_bg': _L1_ffn_in['bg'], 'L1_ffn_W1': _L1_ffn_in['W1'], 'L1_ffn_W2': _L1_ffn_in['W2'], 'L2_xattn_Wq': _L2_xattn_in['Wq'], 'L2_xattn_bq': _L2_xattn_in['bq'], 'L2_xattn_Wk': _L2_xattn_in['Wk'], 'L2_xattn_bk': _L2_xattn_in['bk'], 'L2_xattn_Wv': _L2_xattn_in['Wv'], 'L2_xattn_bv': _L2_xattn_in['bv'], 'L2_xattn_Wo': _L2_xattn_in['Wo'], 'L2_xattn_bo': _L2_xattn_in['bo'], 'L2_ffn_w1_w': _L2_ffn_in['w1_w'], 'L2_ffn_w1_s': _L2_ffn_in['w1_s'], 'L2_ffn_w2_w': _L2_ffn_in['w2_w'], 'L2_ffn_w2_s': _L2_ffn_in['w2_s'], 'L2_ffn_h1_w': _L2_ffn_in['h1_w'], 'L2_ffn_h1_s': _L2_ffn_in['h1_s'], 'L2_ffn_h2_w': _L2_ffn_in['h2_w'], 'L2_ffn_h2_s': _L2_ffn_in['h2_s'], 'L2_ffn_w3_w': _L2_ffn_in['w3_w'], 'L2_ffn_w3_s': _L2_ffn_in['w3_s'], 'L3_xattn_Wq': _L3_xattn_in['Wq'], 'L3_xattn_bq': _L3_xattn_in['bq'], 'L3_xattn_Wk': _L3_xattn_in['Wk'], 'L3_xattn_bk': _L3_xattn_in['bk'], 'L3_xattn_Wv': _L3_xattn_in['Wv'], 'L3_xattn_bv': _L3_xattn_in['bv'], 'L3_xattn_Wo': _L3_xattn_in['Wo'], 'L3_xattn_bo': _L3_xattn_in['bo'], 'L3_ffn_W_r': _L3_ffn_in['W_r'], 'L3_ffn_W_k': _L3_ffn_in['W_k'], 'L3_ffn_W_v': _L3_ffn_in['W_v'], 'L3_ffn_mu_r': _L3_ffn_in['mu_r'], 'L3_ffn_mu_k': _L3_ffn_in['mu_k']}

def reference(x, ctx_1024, mask_BxS2_if0, g_xattn, g_ffn, L0_xattn_Wk, L0_xattn_bk, L0_xattn_Wv, L0_xattn_bv, L0_xattn_Wq, L0_xattn_bq, L0_xattn_Woff, L0_xattn_boff, L0_xattn_Wo, L0_xattn_bo, L0_ffn_rhs, L1_xattn_Wq, L1_xattn_Wk, L1_xattn_Wv, L1_xattn_Wo, L1_ffn_Wg, L1_ffn_bg, L1_ffn_W1, L1_ffn_W2, L2_xattn_Wq, L2_xattn_bq, L2_xattn_Wk, L2_xattn_bk, L2_xattn_Wv, L2_xattn_bv, L2_xattn_Wo, L2_xattn_bo, L2_ffn_w1_w, L2_ffn_w1_s, L2_ffn_w2_w, L2_ffn_w2_s, L2_ffn_h1_w, L2_ffn_h1_s, L2_ffn_h2_w, L2_ffn_h2_s, L2_ffn_w3_w, L2_ffn_w3_s, L3_xattn_Wq, L3_xattn_bq, L3_xattn_Wk, L3_xattn_bk, L3_xattn_Wv, L3_xattn_bv, L3_xattn_Wo, L3_xattn_bo, L3_ffn_W_r, L3_ffn_W_k, L3_ffn_W_v, L3_ffn_mu_r, L3_ffn_mu_k):
    import jax
    import jax.numpy as jnp

    def _L0_xattn_ref(k, v, q, mask, Wk, bk, Wv, bv, Wq, bq, Woff, boff, Wo, bo):
        import jax, jax.numpy as jnp
        import numpy as np
        import math
        B, M, D, H, NK = (4, 512, 256, 16, 5)
        HD = D // H

        def _gather_pad0(x, idx):
            Bx, Hx, W, hd = x.shape
            valid = (idx >= 0) & (idx < W)
            idxc = jnp.clip(idx, 0, W - 1).reshape(Bx, Hx, -1)
            g = jnp.take_along_axis(x, idxc[..., None], axis=2)
            g = g.reshape(idx.shape + (hd,))
            return g * valid[..., None].astype(x.dtype)
        Bq, Q, _ = q.shape
        key_len = k.shape[1]
        K = jnp.einsum('bmd,ed->bme', k, Wk) + bk
        V = jnp.einsum('bmd,ed->bme', v, Wv) + bv
        Qp = jnp.einsum('bqd,ed->bqe', q, Wq) + bq
        off = jnp.einsum('bqd,ed->bqe', Qp, Woff) + boff
        off = off.reshape(Bq, Q, H, NK).transpose(0, 2, 1, 3)
        Kh = K.reshape(Bq, key_len, H, HD).transpose(0, 2, 1, 3)
        Vh = V.reshape(Bq, key_len, H, HD).transpose(0, 2, 1, 3)
        Qh = Qp.reshape(Bq, Q, H, HD).transpose(0, 2, 1, 3)
        loc = jnp.arange(Q, dtype=jnp.float32)[:, None]
        left = -NK // 2
        ref = jnp.arange(left, NK + left, dtype=jnp.float32)
        sign_lens = (1 - mask).sum(-1).astype(jnp.float32) - 1.0
        loc_x = jnp.mod(ref + off + loc, sign_lens[:, None, None, None])
        xg = loc_x / (key_len - 1) * 2.0 - 1.0
        ix = ((xg + 1.0) * key_len - 1.0) / 2.0
        x0 = jnp.floor(ix)
        dx = ix - x0
        i0 = x0.astype(jnp.int32)
        i1 = i0 + 1
        w0 = (1.0 - dx)[..., None]
        w1 = dx[..., None]
        sk = 0.5 * (w0 * _gather_pad0(Kh, i0) + w1 * _gather_pad0(Kh, i1))
        sv = 0.5 * (w0 * _gather_pad0(Vh, i0) + w1 * _gather_pad0(Vh, i1))
        scores = jnp.einsum('bhqd,bhqkd->bhqk', Qh / math.sqrt(HD), sk)
        attn = jax.nn.softmax(scores, axis=-1)
        ctx = jnp.einsum('bhqk,bhqkd->bhqd', attn, sv)
        ctx = ctx.transpose(0, 2, 1, 3).reshape(Bq, Q, H * HD)
        return jnp.einsum('bqd,ed->bqe', ctx, Wo) + bo

    def _L0_ffn_ref(lhs, rhs):
        import jax, jax.numpy as jnp
        import numpy as np
        INT8_MAX = 127.0

        def _absmax_scale(x, axes):
            amax = jnp.max(jnp.abs(x), axis=axes, keepdims=True)
            return jnp.maximum(amax, 1e-12) / INT8_MAX
        lhs_scale = _absmax_scale(lhs, (2,))
        rhs_scale = _absmax_scale(rhs, (0,))
        q_lhs = jnp.clip(jnp.round(lhs / lhs_scale), -INT8_MAX, INT8_MAX).astype(jnp.int8)
        q_rhs = jnp.clip(jnp.round(rhs / rhs_scale), -INT8_MAX, INT8_MAX).astype(jnp.int8)
        acc = jax.lax.dot_general(q_lhs, q_rhs, (((2,), (0,)), ((), ())), preferred_element_type=jnp.int32)
        return acc.astype(jnp.float32) * lhs_scale * rhs_scale

    def _L1_xattn_ref(q, k, v, Wq, Wk, Wv, Wo):
        import jax, jax.numpy as jnp
        import numpy as np
        D_MODEL = 256
        N_HEADS = 16
        DH = D_MODEL // N_HEADS // 2
        B, S = (4, 512)
        scale = D_MODEL ** (-0.5)
        Q = jnp.einsum('bsd,hde->bhse', q, Wq)
        K = jnp.einsum('btd,hde->bhte', k, Wk)
        V = jnp.einsum('btd,hde->bhte', v, Wv)
        attn = jnp.einsum('bhse,bhte->bhst', Q, K) * scale
        attn = jax.nn.softmax(attn, axis=-1)
        x = jnp.einsum('bhst,bhte->bhse', attn, V)
        x = jnp.transpose(x, (0, 2, 1, 3)).reshape(q.shape[0], q.shape[1], N_HEADS * DH)
        return x @ Wo

    def _L1_ffn_ref(x, Wg, bg, W1, W2):
        import jax, jax.numpy as jnp
        import numpy as np
        DIM = 256
        INNER = 1024
        E = 8
        EPS = 1e-06
        B, N, D = x.shape
        num_experts = Wg.shape[1]
        T = B * N
        xf = x.reshape(T, D)
        gate_scores = jax.nn.softmax(xf @ Wg + bg, axis=-1)
        top1 = jnp.argmax(gate_scores, axis=-1)
        mask = jax.nn.one_hot(top1, num_experts, dtype=gate_scores.dtype)
        masked = gate_scores * mask
        denom = masked.sum(axis=0, keepdims=True) + EPS
        gate = masked / denom * T
        gate = gate.reshape(B, N, num_experts)
        out = jnp.zeros((B, N, D), dtype=x.dtype)
        for e in range(num_experts):
            h = jax.nn.relu(jnp.einsum('bnd,dh->bnh', x, W1[e]))
            y = jnp.einsum('bnh,hd->bnd', h, W2[e])
            out = out + gate[..., e:e + 1] * y
        return out

    def _L2_xattn_ref(queries, keys, values, Wq, bq, Wk, bk, Wv, bv, Wo, bo):
        import jax, jax.numpy as jnp
        import numpy as np
        B, L, D_MODEL, N_HEADS = (4, 512, 256, 16)
        HEAD_DIM = D_MODEL // N_HEADS
        Bsz, Lq, _ = queries.shape
        S = keys.shape[1]
        H, E = (N_HEADS, HEAD_DIM)
        q = (queries @ Wq + bq).reshape(Bsz, Lq, H, E)
        k = (keys @ Wk + bk).reshape(Bsz, S, H, E)
        v = (values @ Wv + bv).reshape(Bsz, S, H, E)
        scale = 1.0 / np.sqrt(E)
        scores = jnp.einsum('blhe,bshe->bhls', q, k)
        A = jax.nn.softmax(scale * scores, axis=-1)
        ctx = jnp.einsum('bhls,bshd->blhd', A, v).reshape(Bsz, Lq, H * E)
        out = ctx @ Wo + bo
        return out

    def _L2_ffn_ref(x, w1_w, w1_s, w2_w, w2_s, h1_w, h1_s, h2_w, h2_s, w3_w, w3_s):
        import jax, jax.numpy as jnp
        import numpy as np
        D_IN, D_HID = (256, 1024)

        def _ternary(key, shape):
            return jax.random.randint(key, shape, -1, 2).astype(jnp.float32)

        def _tlin(x, w, s):
            return jnp.einsum('bsi,oi->bso', x, w) * s
        h = jax.nn.silu(_tlin(x, w1_w, w1_s)) * _tlin(x, w2_w, w2_s)
        h = jax.nn.gelu(_tlin(h, h1_w, h1_s), approximate=False)
        h = jax.nn.gelu(_tlin(h, h2_w, h2_s), approximate=False)
        return _tlin(h, w3_w, w3_s)

    def _L3_xattn_ref(queries, keys, values, Wq, bq, Wk, bk, Wv, bv, Wo, bo):
        import jax, jax.numpy as jnp
        import numpy as np
        NUM_HEADS = 8
        D_MODEL = 256
        DIM = D_MODEL // NUM_HEADS
        HEAD_DIM = DIM // NUM_HEADS
        B, S = (4, 512)

        def _split_heads(x):
            b, s, _ = x.shape
            return x.reshape(b, s, NUM_HEADS, HEAD_DIM).transpose(0, 2, 1, 3)
        q = _split_heads(queries @ Wq + bq)
        k = _split_heads(keys @ Wk + bk)
        v = _split_heads(values @ Wv + bv)
        scale = 1.0 / np.sqrt(D_MODEL / NUM_HEADS).astype(np.float32)
        scores = jnp.einsum('bhqd,bhkd->bhqk', q, k) * scale
        attn = jax.nn.softmax(scores, axis=-1)
        o = jnp.einsum('bhqk,bhkd->bhqd', attn, v)
        b, h, s, hd = o.shape
        o = o.transpose(0, 2, 1, 3).reshape(b, s, h * hd)
        return o @ Wo + bo

    def _L3_ffn_ref(x, W_r, W_k, W_v, mu_r, mu_k):
        import jax, jax.numpy as jnp
        import numpy as np
        DIM = 256

        def _reference_tuple_inner(x, W_r, W_k, W_v, mu_r, mu_k):
            B, T, C = x.shape
            x_prev = jnp.concatenate([jnp.zeros((B, 1, C), x.dtype), x[:, :-1, :]], axis=1)
            xr = mu_r * x + (1.0 - mu_r) * x_prev
            xk = mu_k * x + (1.0 - mu_k) * x_prev
            r = jax.nn.sigmoid(jnp.einsum('btc,dc->btd', xr, W_r))
            k = jnp.einsum('btc,dc->btd', xk, W_k)
            k_act = jnp.square(jax.nn.relu(k))
            out = r * jnp.einsum('btc,dc->btd', k_act, W_v)
            new_state = x[:, -1, :]
            return (out, new_state)
        return _reference_tuple_inner(x, W_r, W_k, W_v, mu_r, mu_k)[0]
    x = x + jnp.tanh(g_xattn[0]) * _L0_xattn_ref(ctx_1024, ctx_1024, _layernorm(x, axis=-1), mask_BxS2_if0, L0_xattn_Wk, L0_xattn_bk, L0_xattn_Wv, L0_xattn_bv, L0_xattn_Wq, L0_xattn_bq, L0_xattn_Woff, L0_xattn_boff, L0_xattn_Wo, L0_xattn_bo)
    x = x + jnp.tanh(g_ffn[0]) * _L0_ffn_ref(_layernorm(x, axis=-1), L0_ffn_rhs)
    x = x + jnp.tanh(g_xattn[1]) * _L1_xattn_ref(_layernorm(x, axis=-1), ctx_1024, ctx_1024, L1_xattn_Wq, L1_xattn_Wk, L1_xattn_Wv, L1_xattn_Wo)
    x = x + jnp.tanh(g_ffn[1]) * _L1_ffn_ref(_layernorm(x, axis=-1), L1_ffn_Wg, L1_ffn_bg, L1_ffn_W1, L1_ffn_W2)
    x = x + jnp.tanh(g_xattn[2]) * _L2_xattn_ref(_layernorm(x, axis=-1), ctx_1024, ctx_1024, L2_xattn_Wq, L2_xattn_bq, L2_xattn_Wk, L2_xattn_bk, L2_xattn_Wv, L2_xattn_bv, L2_xattn_Wo, L2_xattn_bo)
    x = x + jnp.tanh(g_ffn[2]) * _L2_ffn_ref(_layernorm(x, axis=-1), L2_ffn_w1_w, L2_ffn_w1_s, L2_ffn_w2_w, L2_ffn_w2_s, L2_ffn_h1_w, L2_ffn_h1_s, L2_ffn_h2_w, L2_ffn_h2_s, L2_ffn_w3_w, L2_ffn_w3_s)
    x = x + jnp.tanh(g_xattn[3]) * _L3_xattn_ref(_layernorm(x, axis=-1), ctx_1024, ctx_1024, L3_xattn_Wq, L3_xattn_bq, L3_xattn_Wk, L3_xattn_bk, L3_xattn_Wv, L3_xattn_bv, L3_xattn_Wo, L3_xattn_bo)
    x = x + jnp.tanh(g_ffn[3]) * _L3_ffn_ref(_layernorm(x, axis=-1), L3_ffn_W_r, L3_ffn_W_k, L3_ffn_W_v, L3_ffn_mu_r, L3_ffn_mu_k)
    return x

_drawn_inputs = setup_inputs


def setup_inputs(seed=0):
    import zlib

    import numpy as np

    out = dict(_drawn_inputs(seed))
    spreads = {'L0_xattn_bk': (0.0, 0.1),
     'L0_xattn_bv': (0.0, 0.1),
     'L0_xattn_bq': (0.0, 0.1),
     'L0_xattn_boff': (0.0, 0.1),
     'L0_xattn_bo': (0.0, 0.1),
     'L2_xattn_bq': (0.0, 0.1),
     'L2_xattn_bk': (0.0, 0.1),
     'L2_xattn_bv': (0.0, 0.1),
     'L2_xattn_bo': (0.0, 0.1),
     'L3_xattn_bq': (0.0, 0.1),
     'L3_xattn_bk': (0.0, 0.1),
     'L3_xattn_bv': (0.0, 0.1),
     'L3_xattn_bo': (0.0, 0.1)}
    factors = {}
    for name, (base, spread) in spreads.items():
        noise = np.random.default_rng([zlib.crc32(name.encode()), seed]).standard_normal(out[name].shape)
        drawn = base * np.exp(spread * noise) if base else spread * noise
        out[name] = jnp.asarray(drawn.astype(out[name].dtype))
    for name, factor in factors.items():
        out[name] = (out[name] * factor).astype(out[name].dtype)
    return out
```

```python
from contextlib import ExitStack

import concourse.bass as bass
from concourse import mybir

F32 = mybir.dt.float32
BF16 = mybir.dt.bfloat16
I32 = mybir.dt.int32
ALU = mybir.AluOpType
ACT = mybir.ActivationFunctionType
AX = mybir.AxisListType

P = 128
D = 256
DC = D // P
B = 2
S = 512
M = 1024
T = B * S
NT = T // P
QT = S // P
CT = B * M
NCT = CT // P
CH = 512
EPS_LN = 1e-5
MAGIC = 1.5 * 2.0**23

H0, HD0, NK = 16, 16, 5
HK = H0 * NK
LEFT = (-NK) // 2
WIN = 8
BACK = 5
ROWS = M + S + 8

ATT = {1: (16, 8, 256 ** -0.5), 2: (16, 16, 0.25), 3: (8, 4, 1.0 / float(32.0 ** 0.5))}
HG = 4
KT = M // P
PARTS_Q = (0, 0, 0, 1, 1, 2)
PARTS_K = (0, 1, 2, 0, 1, 0)
SHIFT_ROWS = 2

NGROUPS = {l: B * ATT[l][0] // HG for l in ATT}
GROUP0 = {l: sum(NGROUPS[i] for i in range(1, l)) for l in range(1, 5)}
EW = {l: ATT[l][0] * ATT[l][1] for l in ATT}
EC = {l: max(1, EW[l] // P) for l in ATT}
PREP0 = {l: sum(EC[i] * CT // CH for i in range(1, l)) for l in range(1, 5)}
QCH0 = {l: sum(EC[i] * T // CH for i in range(1, l)) for l in range(1, 5)}
GEN_STEPS = M // WIN - 1
GEN_LINKS = 10
LN_AT = {0: 0, 2: 1, 3: 2, 4: 3, 5: 4, 6: 5, 7: 6}
OUT_AT = {0: 0, 1: 1, 2: 2, 4: 3, 5: 4, 6: 5}
CTX_BANKS0 = {0: 0, 1: 2 * DC, 2: 2 * DC + 2 * EC[1], 3: 2 * DC + 2 * EC[1] + 2 * EC[2]}
HALVES = HG * QT * 2
LEAD = HALVES + 12

CTX_SLOT = 4
XN0 = {s: s * NT for s in range(8)}
LATE_LOADS = 2 + 3 * 2 + 2 * 2
PREP_MM = PREP0[4] + 3 * NCT


def schedule(l):
    steps, u, total = [], 0, NGROUPS[l] * HALVES

    def maxima(upto):
        nonlocal u
        while u < min(upto, total):
            steps.append(("max", u))
            u += 1
            if u % HALVES == 4 and u > HALVES or u == total:
                steps.append(("tr", (u - 1) // HALVES - (0 if u == total else 1)))

    for g in range(NGROUPS[l]):
        for kt in range(KT):
            maxima(LEAD + 4 * (g * KT + kt))
            steps.append(("slot", g, kt))
    return steps


E_MOE, F_MOE = 8, 1024
F_GLU = 1024


def build(nc, io):
    with ExitStack() as ctx:
        def sb(name, shape, dt=F32):
            return ctx.enter_context(nc.sbuf_tensor(name, shape, dt))

        def sem(name):
            return ctx.enter_context(nc.semaphore(name))

        st_bank = [ctx.enter_context(nc.psum_tensor(f"st_bank{i}", [P, 2, CH], F32)) for i in range(2)]
        bank = [st_bank[i // 2][:, i % 2, :] for i in range(4)]
        bank += [ctx.enter_context(nc.psum_tensor(f"bank{i}", [P, CH], F32))[:, :] for i in range(4, 8)]

        kv_table = nc.dram_tensor("kv_table", [B, ROWS, 2 * D], F32).ap()
        kparts = {l: nc.dram_tensor(f"kparts{l}", [3, ATT[l][0] * ATT[l][1], CT], BF16).ap() for l in ATT}
        qparts = {l: nc.dram_tensor(f"qparts{l}", [3, ATT[l][0] * ATT[l][1], T], BF16).ap() for l in ATT}

        x = sb("x", [P, NT, D])
        xn = sb("xn", [P, NT, D])
        xnT = sb("xnT", [P, DC, T])
        ctxT = sb("ctxT", [P, DC, CT])
        ident = sb("ident", [P, P])
        identb = sb("identb", [P, P], BF16)
        onesf = sb("onesf", [P, P])
        bnst = sb("bnst", [P, NT, 6])
        mv = sb("mv", [P, NT, 2])
        rstd = sb("rstd", [P, NT])
        minus_half = sb("minus_half", [P, NT])
        tgx = sb("tgx", [P, 4])
        tgf = sb("tgf", [P, 4])
        gx = sb("gx", [P, 4])
        gf = sb("gf", [P, 4])
        ARENA = 31 * 1024
        arena = sb("arena", [P, ARENA])

        class Region:
            def __init__(self, at=0):
                self.at = at

            def take(self, shape, dt=F32):
                n = 1
                for s in shape:
                    n *= s
                words = n if dt in (F32, I32) else (n + 1) // 2
                ap = arena[:, self.at:self.at + words]
                self.at += words
                assert self.at <= ARENA, self.at
                if dt != F32:
                    ap = ap.bitcast(dt)
                if len(shape) == 2:
                    ap = ap.rearrange("p (a b) -> p a b", a=shape[0])
                elif len(shape) == 3:
                    ap = ap.rearrange("p (a b c) -> p a b c", a=shape[0], b=shape[1])
                elif len(shape) == 4:
                    ap = ap.rearrange("p (a b c d) -> p a b c d", a=shape[0], b=shape[1], c=shape[2])
                return ap

        w = {}
        for l in ATT:
            e = ATT[l][0] * ATT[l][1]
            w[l] = dict(
                q=sb(f"wq{l}", [P, DC, e]), o=sb(f"wo{l}", [min(e, P), (e + P - 1) // P, D]),
                bq=sb(f"bq{l}", [min(e, P), (e + P - 1) // P]) if l > 1 else None,
                bo=sb(f"bo{l}", [1, D]) if l > 1 else None)
        vaug = {l: sb(f"vaug{l}", [P, NCT, ATT[l][0], ATT[l][1] + 1]) for l in ATT}
        wo0 = sb("wo0", [P, DC, D])
        bo0 = sb("bo0", [1, D])

        chain_dve, chain_act, chain_pool = sem("chain_dve"), sem("chain_act"), sem("chain_pool")
        ld_ctx, ld_x, ld_w0, ld_prep, ld_small, ld_late = (sem(n) for n in (
            "ld_ctx", "ld_x", "ld_w0", "ld_prep", "ld_small", "ld_late"))
        consts_ready, tanh_ready = sem("consts_ready"), sem("tanh_ready")
        kv0_mm, kv0_ready = sem("kv0_mm"), sem("kv0_ready")
        table_written = [sem(f"table_written{i}") for i in range(4)]
        xn_ready, xnT_mm, xnT_ready = sem("xn_ready"), sem("xnT_mm"), sem("xnT_ready")
        qT0_mm, qT0_ready, q0_mm, q0_ready, off_mm = (sem(n) for n in ("qT0_mm", "qT0_ready", "q0_mm", "q0_ready", "off_mm"))
        cov_ready, cov_mm, flag_ready = sem("cov_ready"), sem("cov_mm"), sem("flag_ready")
        winK_ld = [sem(f"winK_ld{i}") for i in range(2)]
        winV_ld = [sem(f"winV_ld{i}") for i in range(2)]
        prodK_ready, prodK_used, prodV_ready, prodV_used = (sem(n) for n in ("prodK_ready", "prodK_used", "prodV_ready", "prodV_used"))
        sub0_ready, exp0_ready, attw_ready = sem("sub0_ready"), sem("exp0_ready"), sem("attw_ready")
        gen_ld, gen_used, gen_chain = sem("gen_ld"), sem("gen_used"), sem("gen_chain")
        ctxn_ready, ctxT_mm, ctxT_ready = sem("ctxn_ready"), sem("ctxT_mm"), sem("ctxT_ready")
        out_mm, x_ready = sem("out_mm"), sem("x_ready")
        prep_mm, prep_evac, prep_split = sem("prep_mm"), sem("prep_evac"), sem("prep_split")
        prep_st = [sem(f"prep_st{i}") for i in range(2)]
        prep_hi = sem("prep_hi")
        qp_mm, qp_evac, qp_split = sem("qp_mm"), sem("qp_evac"), sem("qp_split")
        qp_st = [sem(f"qp_st{i}") for i in range(2)]
        kq_zero, kq_ld, shift_ld = sem("kq_zero"), [sem(f"kq_ld{i}") for i in range(3)], [sem(f"shift_ld{i}") for i in range(3)]
        ones_rows = sem("ones_rows")
        max_mm, max_red, max_fin, max_tr, max_hi, max_lo = (sem(n) for n in ("max_mm", "max_red", "max_fin", "max_tr", "max_hi", "max_lo"))
        st_mm, exp_ready, pv_mm, pv_done = sem("st_mm"), sem("exp_ready"), sem("pv_mm"), sem("pv_done")
        pv_evac, pv_tr, norm_ready = sem("pv_evac"), sem("pv_tr"), sem("norm_ready")
        i8_scale, i8_tr, i8_bc, i8_qT, i8_w = sem("i8_scale"), sem("i8_tr"), sem("i8_bc"), sem("i8_qT"), sem("i8_w")
        i8_wq, i8_xq = sem("i8_wq"), sem("i8_xq")
        moe_small = sem("moe_small")
        lg_mm, lg_exp_in, lg_exp, mask_ready, den_mm, gate_ready = (sem(n) for n in (
            "lg_mm", "lg_exp_in", "lg_exp", "mask_ready", "den_mm", "gate_ready"))
        moe_ld = [sem(f"moe_ld{i}") for i in range(2)]
        up_mm, up_act, down_mm, down_add = sem("up_mm"), sem("up_act"), sem("down_mm"), sem("down_add")
        glu_ld, glu_mm, glu_silu, glu_h, glu_out_ld = sem("glu_ld"), sem("glu_mm"), sem("glu_silu"), sem("glu_h"), sem("glu_out_ld")
        h1_ld = [sem(f"h1_ld{i}") for i in range(2)]
        h1_mm, h1_act = sem("h1_mm"), sem("h1_act")
        fin_ld, mix_ready, rk_mm, rk_act, rk_sq, fv_mm, rv_ready = (sem(n) for n in (
            "fin_ld", "mix_ready", "rk_mm", "rk_act", "rk_sq", "fv_mm", "rv_ready"))
        stored = sem("stored")
        var_ready, rstd_ready = sem("var_ready"), sem("rstd_ready")

        r = Region()
        a_wkv = {l: r.take([DC, 2 * ATT[l][0] * ATT[l][1]]) for l in ATT}
        a_bk = {l: r.take([max(1, ATT[l][0] * ATT[l][1] // P)]) for l in (2, 3)}
        a_bv = {l: r.take([ATT[l][0] * ATT[l][1]]) for l in (2, 3)}
        a_pf = [r.take([CH]) for _ in range(2)]
        a_pr = [r.take([CH]) for _ in range(2)]
        a_ph = [[r.take([CH], BF16) for _ in range(3)] for _ in range(2)]
        l0_from = r.at
        a_w0kv = r.take([DC, 2 * D])
        a_bkv = r.take([2 * D])
        a_w0q = r.take([DC, D])
        a_woff = r.take([DC, HK])
        a_boff = r.take([HK])
        a_bq0 = r.take([D])
        a_bq0T = r.take([DC])
        a_kv0 = [r.take([2 * D]) for _ in range(4)]
        a_q0 = r.take([NT, D])
        a_qT0 = r.take([DC, T])
        a_u = r.take([NT, HK])
        a_t = r.take([NT, HK])
        a_sc = r.take([NT, HK])
        a_small = r.take([256])
        a_mx, a_sm = r.take([NT * H0]), r.take([NT * H0])
        a_loc, a_pos, a_msum = r.take([NT]), r.take([NT, WIN]), r.take([B])
        a_rlen = r.take([B])
        a_cov, a_gpos, a_gwrap = r.take([4]), r.take([WIN]), r.take([WIN])
        ctx0 = xn
        end_l0 = r.at
        r2 = Region(end_l0)
        a_win = [r2.take([WIN, D]) for _ in range(2)]
        a_prod = [r2.take([WIN, D]) for _ in range(2)]
        a_W = r2.take([NT, HK, WIN])
        a_S = r2.take([WIN, H0])
        a_A = [r2.take([H0, WIN]) for _ in range(2)]
        a_tmp = r2.take([HK, WIN])
        a_gW = r2.take([HK, WIN])
        gwin = xnT[:, :, :].rearrange("p c t -> p (c t)").rearrange("p (j e) -> p j e", j=WIN)
        a_mask = a_prod[0]
        a_iref = a_W[:, 0].rearrange("p a j -> p (a j)").bitcast(I32)
        a_ref = a_W[:, 1].rearrange("p a j -> p (a j)")
        a_ipos = a_W[:, 2].rearrange("p a j -> p (a j)")[:, 0:NT * WIN + NT].bitcast(I32)
        a_wrap = a_W[:, 3].rearrange("p a j -> p (a j)")
        flag_i = sb("flag_i", [1, 1], I32)

        r = Region()
        Kc = [r.take([HG, M], BF16) for _ in range(3)]
        Qc = [r.take([HG, S], BF16) for _ in range(3)]
        prob = [r.take([HG, S]) for _ in range(3)]
        mxh = [r.take([HG * QT, 2]) for _ in range(2)]
        mxg = [r.take([HG * QT]) for _ in range(2)]
        shp = [[r.take([P], BF16) for _ in range(SHIFT_ROWS)] for _ in range(2)]
        pvs = r.take([CH])
        rsum = r.take([QT, HG])
        qf = [r.take([CH]) for _ in range(2)]
        qr = [r.take([CH]) for _ in range(2)]
        qph = [[r.take([CH], BF16) for _ in range(3)] for _ in range(2)]
        after_att = r.at
        i8w = r.take([DC, D])
        r = Region(after_att)
        mw1 = [r.take([DC, F_MOE]) for _ in range(2)]
        mw2 = [r.take([F_MOE // P, D]) for _ in range(2)]
        r = Region()
        hid = [r.take([F_MOE // P, CH]) for _ in range(2)]
        wg, bg = r.take([DC, E_MOE]), r.take([E_MOE])
        lgs, lge, mskd, gate = (r.take([NT, E_MOE]) for _ in range(4))
        lgm, lgz, idx2 = r.take([NT, 1]), r.take([NT, 1]), r.take([NT, 1])
        rank8 = r.take([E_MOE])
        rank8i = r.take([E_MOE], I32)
        assert r.at <= after_att
        r = Region()
        gw1, gw2 = r.take([DC, F_GLU]), r.take([DC, F_GLU])
        gh = [r.take([F_GLU // P, F_GLU]) for _ in range(2)]
        ha, hb = r.take([F_GLU // P, CH]), r.take([F_GLU // P, CH])
        gw3 = vaug[1][:].rearrange("p t h e -> p (t h e)")[:, 0:F_GLU // P * D].rearrange("p (f d) -> p f d", d=D)
        gsc = r.take([4, F_GLU // P])
        gs3 = r.take([D])
        gtmp = [ctxT[:, 0, 0:CH], ctxT[:, 0, CH:2 * CH]]
        r = Region()
        mwr, mwk, mwv = (r.take([DC, D]) for _ in range(3))
        mmu, mom = r.take([2, DC]), r.take([2, DC])
        xr, xk = r.take([DC, T]), r.take([DC, T])
        rv, kact = r.take([NT, D]), r.take([DC, T])

        def table_dmas(t):
            return sum(1 + (i % KT < QT) + (i % KT == KT - 1) for i in range(t % 4, t + 1, 4))

        r = Region(0)
        i8wq, i8wT = r.take([DC, D], BF16), r.take([DC, D], BF16)
        i8xq, i8xT = r.take([NT, D], BF16), r.take([DC, T], BF16)
        i8wr, i8xr = r.take([DC]), r.take([NT])
        i8wsc, i8xsc, i8sc_bc = r.take([DC]), r.take([NT]), r.take([D])

        block = ctx.enter_context(nc.Block())

        class Chain:
            def __init__(self, eng, s):
                self.eng, self.s, self.n = eng, s, 0

            def link(self, ins):
                self.n += 1
                ins.then_inc(self.s, 1)
                self.eng.wait_ge(self.s, self.n)

        def bc(ap, shape):
            return ap.to_broadcast(shape)

        @block.sync
        def _(sp):
            def ld(dst, src, s):
                sp.dma_start(dst, src).then_inc(s, 16)

            def rows(a):
                return a.rearrange("(c p) n -> p c n", p=P)

            def spread(a, n=P):
                return a.partition_broadcast(n)

            ld(a_w0kv, rows(io["w0kv"]), ld_w0)
            ld(a_bkv, spread(io["b0kv"]), ld_w0)
            for b in range(B):
                ld(ctxT[:, :, b * M:(b + 1) * M], rows(io["ctxT"])[:, :, b * M:(b + 1) * M], ld_ctx)
            ld(x[:], io["x"].rearrange("(t p) d -> p t d", p=P), ld_x)
            ld(a_w0q, rows(io["w0q"]), ld_small)
            ld(a_woff, rows(io["woff"]), ld_small)
            ld(a_boff, spread(io["boff"]), ld_small)
            ld(a_bq0, spread(io["b0q"]), ld_small)
            ld(a_bq0T, io["b0qT"], ld_small)
            ld(a_mask.rearrange("p a b -> p (a b)").bitcast(I32), spread(io["mask"].rearrange("b m -> (b m)")), ld_small)
            ld(gx[:], spread(io["g_xattn"]), ld_small)
            ld(gf[:], spread(io["g_ffn"]), ld_small)
            for l in ATT:
                ld(a_wkv[l], rows(io[f"wkv{l}"]), ld_prep)
            for l in (2, 3):
                e = ATT[l][0] * ATT[l][1]
                n = min(e, P)
                ld(a_bk[l][0:n, 0:e // n], io[f"bk{l}"], ld_prep)
                ld(a_bv[l][0:1, 0:e], io[f"bv{l}"].rearrange("(o n) -> o n", o=1), ld_prep)
            for t in range(NCT):
                b, i = t // KT, t % KT
                sp.wait_ge(kv0_ready, t + 1)
                src = a_kv0[t % 4]
                sp.dma_start(kv_table[b, BACK + i * P:BACK + (i + 1) * P, :], src).then_inc(table_written[t % 4], 16)
                if i < QT:
                    n = min(P, ROWS - (BACK + M + i * P))
                    sp.dma_start(kv_table[b, BACK + M + i * P:BACK + M + i * P + n, :], src[0:n]).then_inc(table_written[t % 4], 16)
                if i == KT - 1:
                    sp.dma_start(kv_table[b, 0:BACK, :], src[P - BACK:P]).then_inc(table_written[t % 4], 16)
            ld(wo0[:], rows(io["w0o"]), ld_late)
            ld(bo0[:], io["b0o"].rearrange("(o n) -> o n", o=1), ld_late)
            for l in ATT:
                e = ATT[l][0] * ATT[l][1]
                n = min(e, P)
                ld(w[l]["q"][:], rows(io[f"wq{l}"]), ld_late)
                ld(w[l]["o"][:], io[f"wo{l}"].rearrange("(c p) n -> p c n", p=n), ld_late)
                if l > 1:
                    ld(w[l]["bq"][:], io[f"bq{l}"], ld_late)
                    ld(w[l]["bo"][:], io[f"bo{l}"].rearrange("(o n) -> o n", o=1), ld_late)

            for i in range(4):
                sp.wait_ge(table_written[i], 16 * table_dmas(NCT - 4 + i))
            sp.wait_ge(flag_ready, 1)
            uncovered = sp.value_load(flag_i[0:1, 0:1], min_val=0, max_val=1)

            def window(t, col, shift):
                b, i = t // QT, t % QT
                return bass.AP(tensor=kv_table.tensor, offset=kv_table.offset + (b * ROWS + i * P) * 2 * D + col * D + shift * WIN * 2 * D,
                               ap=[[2 * D, P], [2 * D, WIN], [1, D]])

            for t in range(NT):
                if t >= 2:
                    sp.wait_ge(prodK_ready, t - 1)
                sp.dma_start(a_win[t % 2], window(t, 0, 0)).then_inc(winK_ld[t % 2], 16)

            def general_windows(col, loop0):
                with sp.If(uncovered):
                    for t in range(NT):
                        with sp.Fori(1, M // WIN) as s:
                            sp.wait_ge(gen_used, s + (loop0 + t) * GEN_STEPS)
                            sp.dma_start(gwin, window(t, col, s)).then_inc(gen_ld, 16)

            general_windows(0, 0)
            for t in range(NT):
                if t < 2:
                    sp.wait_ge(prodK_ready, NT - 1 + t)
                else:
                    sp.wait_ge(prodV_ready, t - 1)
                sp.dma_start(a_win[t % 2], window(t, 1, 0)).then_inc(winV_ld[t % 2], 16)

            general_windows(1, NT)

            def group_load(l, g):
                H, dh, _ = ATT[l]
                gi = GROUP0[l] + g
                b, h0 = g // (H // HG), (g % (H // HG)) * HG
                buf = gi % 3
                sp.wait_ge(kq_zero, gi + 1)
                for c in range(6):
                    rr = slice(SHIFT_ROWS + c * dh, SHIFT_ROWS + (c + 1) * dh)
                    heads = slice(h0 * dh, (h0 + HG) * dh)
                    sp.dma_start(Kc[buf][rr], kparts[l][PARTS_K[c], heads, b * M:(b + 1) * M].rearrange("(h d) t -> d h t", d=dh)).then_inc(kq_ld[buf], 16)
                    sp.dma_start(Qc[buf][rr], qparts[l][PARTS_Q[c], heads, b * S:(b + 1) * S].rearrange("(h d) t -> d h t", d=dh)).then_inc(kq_ld[buf], 16)

            def shift_load(l, g):
                gi = GROUP0[l] + g
                sp.wait_ge(max_hi, gi + 1)
                sp.wait_ge(max_lo, gi + 1)
                for i in range(SHIFT_ROWS):
                    sp.dma_start(Qc[gi % 3][i:i + 1].rearrange("o h (q n) -> o (h q) n", n=P), shp[gi % 2][i][0:HG * QT, :]).then_inc(shift_ld[gi % 3], 16)

            def attention_loads(l):
                ng = NGROUPS[l]
                sp.wait_ge(qp_st[0], 16 * 3 * (QCH0[l + 1] // 2))
                sp.wait_ge(qp_st[1], 16 * 3 * (QCH0[l + 1] // 2))
                for i in range(2):
                    sp.wait_ge(prep_st[i], 16 * 3 * (PREP0[l + 1] // 2))
                for g in range(min(3, ng)):
                    group_load(l, g)
                shift_load(l, 0)
                for g in range(ng):
                    if g + 1 < ng:
                        shift_load(l, g + 1)
                    if g + 3 < ng:
                        group_load(l, g + 3)

            def expert_load(e):
                ld(mw1[e % 2], rows(io["w1"][e]), moe_ld[e % 2])
                ld(mw2[e % 2], rows(io["w2"][e]), moe_ld[e % 2])

            def moe_loads():
                sp.wait_ge(x_ready, 3 * NT)
                ld(wg, rows(io["wg"]), moe_small)
                ld(bg[0:1, :], io["bg"].rearrange("(o n) -> o n", o=1), moe_small)
                for e in range(2, E_MOE):
                    sp.wait_ge(down_mm, (e - 1) * NT)
                    expert_load(e)

            def glu_loads():
                sp.wait_ge(x_ready, 5 * NT)
                ld(gw1, rows(io["glu1"]), glu_ld)
                ld(gw2, rows(io["glu2"]), glu_ld)
                for i, n in enumerate(("s1", "s2", "sh1", "sh2")):
                    ld(gsc[:, i], io[n], glu_ld)
                ld(gs3, spread(io["s3"]), glu_ld)
                ld(gw3, rows(io["glu3"]), glu_ld)
                ld(gh[0], rows(io["gluh1"]), h1_ld[0])
                ld(gh[1], rows(io["gluh2"]), h1_ld[1])

            def mix_loads():
                sp.wait_ge(x_ready, 7 * NT)
                for dst, n in ((mwr, "w_r"), (mwk, "w_k"), (mwv, "w_v")):
                    ld(dst, rows(io[n]), fin_ld)
                ld(mmu[:, 0], io["mu_r"], fin_ld)
                ld(mmu[:, 1], io["mu_k"], fin_ld)

            sp.wait_ge(x_ready, NT)
            ld(i8w, io["i8rhsT"].rearrange("(c p) n -> p c n", p=P), i8_w)
            sp.wait_ge(x_ready, 2 * NT)
            for e in range(2):
                expert_load(e)
            attention_loads(1)
            moe_loads()
            attention_loads(2)
            glu_loads()
            attention_loads(3)
            mix_loads()
            for t in range(NT):
                sp.wait_ge(x_ready, 8 * NT - NT + t + 1)
                sp.dma_start(io["out"][t * P:(t + 1) * P, :], x[:, t, :]).then_inc(stored, 16)
            sp.wait_ge(stored, 16 * NT)

        @block.gpsimd
        def _(pool):
            ch = Chain(pool, chain_pool)
            ch.link(pool.memset(ident[:], 0.0))
            ch.link(pool.affine_select(out=ident[:], in_=ident[:], compare_op=ALU.not_equal, fill=1.0, base=0,
                                       pattern=[[-1, P]], channel_multiplier=1))
            pool.tensor_copy(identb[:], ident[:]).then_inc(consts_ready, 1)
            pool.memset(onesf[:], 1.0).then_inc(consts_ready, 1)
            pool.iota(a_iref, pattern=[[0, NT * H0], [1, NK]], base=LEFT, channel_multiplier=0).then_inc(consts_ready, 1)
            pool.iota(a_ipos[:, 0:NT * WIN], pattern=[[0, B], [P, QT], [1, WIN]], base=-BACK, channel_multiplier=1).then_inc(consts_ready, 1)
            pool.iota(a_ipos[:, NT * WIN:], pattern=[[0, B], [P, QT]], base=0, channel_multiplier=1).then_inc(consts_ready, 1)
            for l in ATT:
                pool.memset(vaug[l][:].rearrange("p t h e -> p (t h) e")[:, :, ATT[l][1]], 1.0).then_inc(ones_rows, 1)

            def inverse_deviation(stage):
                pool.wait_ge(var_ready, stage + 1)
                ch.link(pool.tensor_scalar(rstd[:], mv[:, :, 1], EPS_LN, None, ALU.add))
                pool.tensor_tensor(rstd[:], rstd[:], minus_half[:], ALU.pow).then_inc(rstd_ready, 1)

            ch.link(pool.memset(minus_half[:], -0.5))
            inverse_deviation(0)

            def split_k(k):
                l = next(i for i in ATT if PREP0[i] <= k < PREP0[i + 1])
                n = min(P, EW[l])
                kf, kr, (hi, mid, lo) = a_pf[k % 2], a_pr[k % 2], a_ph[k % 2]
                pool.wait_ge(prep_hi, k + 1)
                ch.link(pool.tensor_tensor(kr[0:n], kf[0:n], hi[0:n], ALU.subtract))
                ch.link(pool.tensor_copy(mid[0:n], kr[0:n]))
                pool.tensor_tensor(lo[0:n], kr[0:n], mid[0:n], ALU.subtract).then_inc(prep_split, 1)

            for k in range(8):
                split_k(k)
            for t in range(NT):
                pool.wait_ge(winK_ld[t % 2], 16 * (t // 2 + 1))
                if t == 0:
                    pool.wait_ge(q0_ready, NT)
                if t >= 2:
                    pool.wait_ge(prodK_used, t - 1)
                pool.tensor_tensor(a_prod[t % 2], a_win[t % 2], bc(a_q0[:, t, :].unsqueeze(1), [P, WIN, D]), ALU.mult).then_inc(prodK_ready, 1)
            for k in range(8, PREP0[4]):
                split_k(k)
            for t in range(NT):
                pool.wait_ge(winV_ld[t % 2], 16 * (t // 2 + 1))
                pool.wait_ge(attw_ready, t + 1)
                pool.wait_ge(prodV_used, t - 1) if t >= 2 else pool.wait_ge(prodK_used, NT)
                pool.tensor_tensor(a_prod[t % 2].rearrange("p j (h d) -> p j h d", h=H0), a_win[t % 2].rearrange("p j (h d) -> p j h d", h=H0),
                                   bc(a_A[t % 2].rearrange("p h j -> p j h").unsqueeze(3), [P, WIN, H0, HD0]), ALU.mult).then_inc(prodV_ready, 1)

            def shift_rows(l):
                for g in range(NGROUPS[l]):
                    gi = GROUP0[l] + g
                    if g == 0:
                        pool.wait_ge(x_ready, 2 * l * NT)
                        if l == 1:
                            for i in range(2):
                                pool.wait_ge(prep_st[i], 16 * 3 * (PREP0[4] // 2))
                    if g >= 3:
                        pool.wait_ge(st_mm, 2 * KT * (gi - 2))
                    if g < 3:
                        ch.link(pool.memset(Kc[gi % 3][0:SHIFT_ROWS], 1.0))
                    pool.memset(Qc[gi % 3][0:SHIFT_ROWS], 0.0).then_inc(kq_zero, 1)

            inverse_deviation(1)
            for l in ATT:
                inverse_deviation(2 * l)
                shift_rows(l)
                inverse_deviation(2 * l + 1)

        @block.scalar
        def _(act):
            ch = Chain(act, chain_act)
            act.wait_ge(ld_small, 16 * 8)
            act.activation(tgx[:], gx[:], ACT.Tanh).then_inc(tanh_ready, 1)
            act.activation(tgf[:], gf[:], ACT.Tanh).then_inc(tanh_ready, 1)

            def transposed(ready, first, n, src_banks, done, count0, rows=P):
                pass

            def ln_evac(stage):
                for i in range(4):
                    c, h = i % 2, i // 2
                    act.wait_ge(xnT_mm, LN_AT[stage] * 4 + i + 1)
                    act.activation(xnT[:, c, h * CH:(h + 1) * CH], bank[i], ACT.Copy).then_inc(xnT_ready, 1)

            def ctx_evac(l, width):
                n, ec = min(P, width), max(1, width // P)
                for i in range(2 * ec):
                    c, h = i % ec, i // ec
                    act.wait_ge(ctxT_mm, CTX_BANKS0[l] + i + 1)
                    act.activation(xnT[0:n, c, h * CH:(h + 1) * CH], bank[i][0:n, :], ACT.Copy).then_inc(ctxT_ready, 1)

            ln_evac(0)
            for c in range(DC):
                for h in range(2):
                    act.wait_ge(qT0_mm, 2 * c + h + 1)
                    act.activation(a_qT0[:, c, h * CH:(h + 1) * CH], bank[h], ACT.Identity, bias=a_bq0T[:, c:c + 1]).then_inc(qT0_ready, 1)

            act.wait_ge(ld_prep, 16 * 7)
            n_mm = 0

            def store_parts(k):
                l = next(i for i in ATT if PREP0[i] <= k < PREP0[i + 1])
                n, j = min(P, EW[l]), k - PREP0[l]
                c, q = j // (CT // CH), j % (CT // CH)
                act.wait_ge(prep_split, k + 1)
                for i in range(3):
                    act.dma_start(kparts[l][i, c * P:c * P + n, q * CH:(q + 1) * CH], a_ph[k % 2][i][0:n]).then_inc(prep_st[k % 2], 16)

            for l in ATT:
                n = min(P, EW[l])
                for j in range(PREP0[l + 1] - PREP0[l]):
                    k = PREP0[l] + j
                    c = j // (CT // CH)
                    act.wait_ge(prep_mm, n_mm + 1)
                    if k >= 2:
                        act.wait_ge(prep_split, k - 1)
                        act.wait_ge(prep_st[k % 2], 16 * 3 * (k // 2))
                    src, dst = bank[6 + n_mm % 2][0:n, :], a_pf[k % 2][0:n]
                    if l == 1:
                        ins = act.activation(dst, src, ACT.Copy)
                    else:
                        ins = act.activation(dst, src, ACT.Identity, bias=a_bk[l][0:n, c:c + 1])
                    n_mm += 1
                    ins.then_inc(prep_evac, 1)
                    act.wait_ge(prep_evac, n_mm)
                    act.activation(a_ph[k % 2][0][0:n], dst, ACT.Copy).then_inc(prep_hi, 1)
                    if k >= 1:
                        store_parts(k - 1)
                for t in range(NCT):
                    act.wait_ge(prep_mm, n_mm + 1)
                    act.activation(vaug[l][:, t, :, 0:ATT[l][1]], bank[6 + n_mm % 2][:, 0:EW[l]].rearrange("p (h d) -> p h d", h=ATT[l][0]),
                                   ACT.Copy).then_inc(prep_evac, 1)
                    n_mm += 1
            store_parts(PREP0[4] - 1)

            act.wait_ge(sub0_ready, 1)
            act.activation(a_sc[:], a_sc[:], ACT.Exp, scale=0.5 * HD0 ** -0.5).then_inc(exp0_ready, 1)
            ctx_evac(0, D)

            act.wait_ge(i8_wq, 1)

            def i8_evac():
                for i in range(DC):
                    act.wait_ge(i8_tr, i + 1)
                    act.activation(i8wT[:, i, :], bank[i][:, 0:D // 2].bitcast(BF16), ACT.Copy).then_inc(i8_qT, 1)
                act.wait_ge(i8_bc, 1)
                act.activation(i8sc_bc, bank[4][:, 0:D], ACT.Copy).then_inc(i8_qT, 1)
                for i in range(4):
                    c, h = i % 2, i // 2
                    act.wait_ge(i8_tr, DC + i + 1)
                    act.activation(i8xT[:, c, h * CH:(h + 1) * CH], bank[i][:, 0:CH // 2].bitcast(BF16), ACT.Copy).then_inc(i8_qT, 1)

            i8_evac()

            def q_store(l, k):
                n, j = min(P, EW[l]), k - QCH0[l]
                c, q = j // 2, j % 2
                act.wait_ge(qp_split, k + 1)
                for i in range(3):
                    act.dma_start(qparts[l][i, c * P:c * P + n, q * CH:(q + 1) * CH], qph[k % 2][i][0:n]).then_inc(qp_st[k % 2], 16)

            def attention(l):
                H, dh, scale = ATT[l]
                n = min(P, EW[l])
                for j in range(QCH0[l + 1] - QCH0[l]):
                    k = QCH0[l] + j
                    act.wait_ge(qp_mm, k + 1)
                    if k >= 2:
                        act.wait_ge(qp_split, k - 1)
                        act.wait_ge(qp_st[k % 2], 16 * 3 * (k // 2))
                    if l == 1:
                        ins = act.activation(qf[k % 2][0:n], bank[4 + k % 2][0:n], ACT.Copy)
                    else:
                        ins = act.activation(qf[k % 2][0:n], bank[4 + k % 2][0:n], ACT.Identity, bias=w[l]["bq"][:, j // 2:j // 2 + 1])
                    ch.link(ins)
                    act.activation(qph[k % 2][0][0:n], qf[k % 2][0:n], ACT.Copy).then_inc(qp_evac, 1)
                    if j >= 1:
                        q_store(l, k - 1)
                q_store(l, QCH0[l + 1] - 1)

                def shift_high(g):
                    gi = GROUP0[l] + g
                    act.wait_ge(max_tr, gi + 1)
                    if gi >= 2:
                        act.wait_ge(shift_ld[(gi - 2) % 3], 16 * SHIFT_ROWS * ((gi - 2) // 3 + 1))
                    act.activation(shp[gi % 2][0][0:HG * QT, :], bank[6][0:HG * QT, 0:P], ACT.Copy, scale=-1.0).then_inc(max_hi, 1)

                def pv_copy(g):
                    gi = GROUP0[l] + g
                    act.wait_ge(pv_mm, KT * (gi + 1))
                    act.wait_ge(pv_tr, gi) if gi else None
                    act.activation(pvs, bank[7], ACT.Copy).then_inc(pv_evac, 1)

                sched = schedule(l)
                for step in sched:
                    if step[0] == "tr":
                        shift_high(step[1])
                    elif step[0] == "slot":
                        _, g, kt = step
                        sl = (GROUP0[l] + g) * KT + kt
                        if kt == 1 and g > 0:
                            pv_copy(g - 1)
                        if sl >= 3:
                            act.wait_ge(pv_mm, sl - 2)
                        for pair in range(2):
                            act.wait_ge(st_mm, 2 * sl + pair + 1)
                            act.activation(prob[sl % 3][:, 2 * pair:2 * pair + 2, :], st_bank[pair][:], ACT.Exp, scale=scale).then_inc(exp_ready, 1)
                pv_copy(NGROUPS[l] - 1)
                ctx_evac(l, EW[l])

            ln_evac(2)
            attention(1)

            ln_evac(3)
            act.wait_ge(lg_exp_in, 1)
            act.activation(lge, lgs, ACT.Exp).then_inc(lg_exp, 1)
            for e in range(E_MOE):
                for h in range(2):
                    for f in range(F_MOE // P):
                        n = (e * 2 + h) * (F_MOE // P) + f
                        act.wait_ge(up_mm, n + 1)
                        if e * 2 + h >= 2:
                            act.wait_ge(down_mm, (e * 2 + h - 1) * QT)
                        act.activation(hid[h][:, f, :], bank[n % 2], ACT.Relu).then_inc(up_act, 1)

            ln_evac(4)
            attention(2)

            ln_evac(5)
            for h in range(2):
                for f in range(F_GLU // P):
                    n = h * (F_GLU // P) + f
                    act.wait_ge(glu_mm, 2 * n + 1)
                    if n >= 2:
                        act.wait_ge(glu_h, n - 1)
                    act.activation(gtmp[n % 2], bank[n % 2], ACT.Silu, scale=gsc[:, 0, f:f + 1]).then_inc(glu_silu, 1)
                for i, dst in enumerate((hb, ha)):
                    for f in range(F_GLU // P):
                        n = (h * 2 + i) * (F_GLU // P) + f
                        act.wait_ge(h1_mm, n + 1)
                        act.activation(dst[:, f, :], bank[4 + n % 2], ACT.Gelu, scale=gsc[:, 2 + i, f:f + 1]).then_inc(h1_act, 1)

            ln_evac(6)
            attention(3)

            ln_evac(7)
            for t in range(NT):
                act.wait_ge(rk_mm, t + 1)
                act.activation(rv[:, t, :], bank[t % 2][:, 0:D], ACT.Sigmoid).then_inc(rk_act, 1)
            for i in range(2 * DC):
                c, h = i // 2, i % 2
                act.wait_ge(rk_mm, NT + i + 1)
                act.activation(kact[:, c, h * CH:(h + 1) * CH], bank[2 + i % 2], ACT.Relu).then_inc(rk_act, 1)

        @block.tensor
        def _(pe):
            def transposes(src, dst_sem, base, width, ready, ready0):
                n, ec = min(P, width), max(1, width // P)
                for t in range(NT):
                    if ready is not None:
                        pe.wait_ge(ready, ready0 + t + 1)
                    for c in range(ec):
                        ins = pe.transpose(bank[(t // QT) * ec + c][0:n, (t % QT) * P:(t % QT + 1) * P], src[:, t, c * P:c * P + n], ident[:])
                        if t % QT == QT - 1:
                            ins.then_inc(dst_sem, 1)

            def project_out(stage, wmat, width, bias, l):
                n, ec = min(P, width), max(1, width // P)
                for t in range(NT):
                    if t % QT == 0:
                        pe.wait_ge(ctxT_ready, CTX_BANKS0[l] + (t // QT + 1) * ec)
                    if t >= 2:
                        pe.wait_ge(x_ready, stage * NT + t - 1)
                    o = bank[4 + t % 2][:, 0:D]
                    for c in range(ec):
                        ins = pe.matmul(o, xnT[0:n, c, t * P:(t + 1) * P], wmat[:, c, :], start=(c == 0), stop=(c == ec - 1 and bias is None))
                    if bias is not None:
                        ins = pe.matmul(o, onesf[0:1, :], bias, start=False, stop=True)
                    ins.then_inc(out_mm, 1)

            pe.wait_ge(ld_w0, 32)
            pe.wait_ge(ld_ctx, 32)
            for t in range(NCT):
                if t >= 2:
                    pe.wait_ge(kv0_ready, t - 1)
                for c in range(DC):
                    ins = pe.matmul(bank[4 + t % 2], ctxT[:, c, t * P:(t + 1) * P], a_w0kv[:, c, :], start=(c == 0), stop=(c == DC - 1))
                ins.then_inc(kv0_mm, 1)
            pe.wait_ge(consts_ready, 2)
            transposes(xn, xnT_mm, 0, D, xn_ready, 0)
            pe.wait_ge(ld_small, 16 * 8)
            pe.wait_ge(xnT_ready, 4)
            for c in range(DC):
                for h in range(2):
                    if c:
                        pe.wait_ge(qT0_ready, h + 1)
                    for i in range(DC):
                        ins = pe.matmul(bank[h], a_w0q[:, i, c * P:(c + 1) * P], xnT[:, i, h * CH:(h + 1) * CH], start=(i == 0), stop=(i == DC - 1))
                    ins.then_inc(qT0_mm, 1)
            pe.wait_ge(kv0_ready, NCT)
            for t in range(NT):
                if t >= 2:
                    pe.wait_ge(q0_ready, t - 1)
                for i in range(DC):
                    ins = pe.matmul(bank[4 + t % 2][:, 0:D], xnT[:, i, t * P:(t + 1) * P], a_w0q[:, i, :], start=(i == 0), stop=(i == DC - 1))
                ins.then_inc(q0_mm, 1)
            pe.wait_ge(qT0_ready, 4)
            for t in range(NT):
                o = bank[2 + t // QT][:, (t % QT) * HK:(t % QT + 1) * HK]
                for i in range(DC):
                    ins = pe.matmul(o, a_qT0[:, i, t * P:(t + 1) * P], a_woff[:, i, :], start=(i == 0), stop=(i == DC - 1))
                ins.then_inc(off_mm, 1)

            pe.wait_ge(cov_ready, 1)
            pe.matmul(bank[0][0:1, 0:1], onesf[:, 0:1], a_cov[:, 0:1], start=True, stop=True).then_inc(cov_mm, 1)

            n_mm = 0
            pe.wait_ge(ld_prep, 16 * 7)
            for l in ATT:
                n = min(P, EW[l])
                for j in range(PREP0[l + 1] - PREP0[l]):
                    c, q = j // (CT // CH), j % (CT // CH)
                    if n_mm >= 2:
                        pe.wait_ge(prep_evac, n_mm - 1)
                    for i in range(DC):
                        ins = pe.matmul(bank[6 + n_mm % 2][0:n, :], a_wkv[l][:, i, c * P:c * P + n], ctxT[:, i, q * CH:(q + 1) * CH], start=(i == 0), stop=(i == DC - 1))
                    ins.then_inc(prep_mm, 1)
                    n_mm += 1
                for t in range(NCT):
                    if n_mm >= 2:
                        pe.wait_ge(prep_evac, n_mm - 1)
                    o = bank[6 + n_mm % 2][:, 0:EW[l]]
                    for i in range(DC):
                        ins = pe.matmul(o, ctxT[:, i, t * P:(t + 1) * P], a_wkv[l][:, i, EW[l]:2 * EW[l]], start=(i == 0), stop=(i == DC - 1 and l == 1))
                    if l > 1:
                        ins = pe.matmul(o, onesf[0:1, :], a_bv[l][0:1, 0:EW[l]], start=False, stop=True)
                    ins.then_inc(prep_mm, 1)
                    n_mm += 1

            pe.wait_ge(ld_late, 16 * LATE_LOADS)
            transposes(ctx0, ctxT_mm, 0, D, ctxn_ready, 0)
            project_out(0, wo0, D, bo0[:], 0)

            pe.wait_ge(i8_wq, 1)
            for c in range(DC):
                for i in range(DC):
                    ins = pe.transpose(bank[c][:, 0:D // 2].bitcast(BF16)[:, i * P:(i + 1) * P], i8wq[:, i, c * P:(c + 1) * P], identb[:])
                ins.then_inc(i8_tr, 1)
            pe.wait_ge(x_ready, NT)
            for i in range(DC):
                ins = pe.matmul(bank[4][:, i * P:(i + 1) * P], bc(i8wsc[:, i:i + 1], [P, P]), ident[:], start=True, stop=True)
            ins.then_inc(i8_bc, 1)
            for t in range(NT):
                pe.wait_ge(i8_xq, t + 1)
                if t == 0:
                    pe.wait_ge(i8_qT, DC)
                for c in range(DC):
                    ins = pe.transpose(bank[(t // QT) * DC + c][:, 0:CH // 2].bitcast(BF16)[:, (t % QT) * P:(t % QT + 1) * P], i8xq[:, t, c * P:(c + 1) * P], identb[:])
                    if t % QT == QT - 1:
                        ins.then_inc(i8_tr, 1)
            for t in range(NT):
                if t % QT == 0:
                    pe.wait_ge(i8_qT, DC + 1 + (t // QT + 1) * DC)
                if t >= 2:
                    pe.wait_ge(x_ready, NT + t - 1)
                for c in range(DC):
                    ins = pe.matmul(bank[4 + t % 2][:, 0:D], i8xT[:, c, t * P:(t + 1) * P], i8wT[:, c, :], start=(c == 0), stop=(c == DC - 1))
                ins.then_inc(out_mm, 1)

            def attention(l):
                H, dh, _ = ATT[l]
                R = SHIFT_ROWS + 6 * dh
                n = min(P, EW[l])
                stage = 2 * l
                pe.wait_ge(xnT_ready, (LN_AT[stage] + 1) * 4)
                for j in range(QCH0[l + 1] - QCH0[l]):
                    k = QCH0[l] + j
                    c, q = j // 2, j % 2
                    if j >= 2:
                        pe.wait_ge(qp_evac, k - 1)
                    for i in range(DC):
                        ins = pe.matmul(bank[4 + k % 2][0:n, :], w[l]["q"][:, i, c * P:c * P + n], xnT[:, i, q * CH:(q + 1) * CH], start=(i == 0), stop=(i == DC - 1))
                    ins.then_inc(qp_mm, 1)
                pe.wait_ge(qp_evac, QCH0[l + 1])

                def row_max(u):
                    g, hh, qt, half = u // HALVES, u // (2 * QT) % HG, u // 2 % QT, u % 2
                    gi = GROUP0[l] + g
                    un = GROUP0[l] * HALVES + u
                    if u % HALVES == 0:
                        pe.wait_ge(kq_ld[gi % 3], 16 * 12 * (gi // 3 + 1))
                    if un >= 2:
                        pe.wait_ge(max_red, un - 1)
                    pe.matmul(bank[4 + un % 2], Qc[gi % 3][0:R, hh, qt * P:(qt + 1) * P], Kc[gi % 3][0:R, hh, half * CH:(half + 1) * CH],
                              start=True, stop=True).then_inc(max_mm, 1)

                turned = {"max": GROUP0[l], "context": GROUP0[l]}

                def turn_max(g):
                    gi = GROUP0[l] + g
                    pe.wait_ge(max_fin, gi + 1)
                    if gi == 0:
                        pe.wait_ge(prep_evac, PREP_MM)
                    if turned["context"]:
                        pe.wait_ge(norm_ready, turned["context"])
                    if turned["max"]:
                        pe.wait_ge(max_lo, turned["max"])
                    turned["max"] += 1
                    pe.transpose(bank[6][0:HG * QT, 0:P], mxg[gi % 2], ident[:]).then_inc(max_tr, 1)

                def score(g, kt, pair):
                    gi = GROUP0[l] + g
                    sl = gi * KT + kt
                    if kt == 0 and pair == 0:
                        pe.wait_ge(shift_ld[gi % 3], 16 * SHIFT_ROWS * (gi // 3 + 1))
                    if sl >= 1:
                        pe.wait_ge(exp_ready, 2 * (sl - 1) + pair + 1)
                    for i in range(2):
                        hh = 2 * pair + i
                        ins = pe.matmul(st_bank[pair][:, i, :], Kc[gi % 3][0:R, hh, kt * P:(kt + 1) * P], Qc[gi % 3][0:R, hh, :], start=True, stop=True)
                    ins.then_inc(st_mm, 1)

                def values(g, kt):
                    gi = GROUP0[l] + g
                    sl = gi * KT + kt
                    b, h0 = g // (H // HG), (g % (H // HG)) * HG
                    pe.wait_ge(exp_ready, 2 * sl + 2)
                    if kt == 0:
                        pe.wait_ge(pv_evac, gi) if g else pe.wait_ge(pv_done, l)
                    for hh in range(HG):
                        ins = pe.matmul(bank[7][32 * hh:32 * hh + dh + 1, :], vaug[l][:, b * KT + kt, h0 + hh, :], prob[sl % 3][:, hh, :],
                                        start=(kt == 0), stop=(kt == KT - 1))
                    ins.then_inc(pv_mm, 1)

                def turn_context(g, last):
                    gi = GROUP0[l] + g
                    pe.wait_ge(pv_evac, gi + 1)
                    pe.wait_ge(max_lo, turned["max"])
                    if turned["context"]:
                        pe.wait_ge(norm_ready, turned["context"])
                    turned["context"] += 1
                    for qt in range(QT):
                        ins = pe.transpose(bank[6][:, qt * P:(qt + 1) * P], pvs[:, qt * P:(qt + 1) * P], ident[:])
                    ins.then_inc(pv_tr, 1)

                for step in schedule(l):
                    if step[0] == "max":
                        row_max(step[1])
                    elif step[0] == "tr":
                        turn_max(step[1])
                    else:
                        _, g, kt = step
                        score(g, kt, 0)
                        if kt:
                            values(g, kt - 1)
                        elif g:
                            values(g - 1, KT - 1)
                        score(g, kt, 1)
                        if kt == CTX_SLOT and g:
                            turn_context(g - 1, False)
                values(NGROUPS[l] - 1, KT - 1)
                turn_context(NGROUPS[l] - 1, True)
                pe.wait_ge(norm_ready, GROUP0[l + 1])
                transposes(xn, ctxT_mm, 0, EW[l], None, 0)
                project_out(stage, w[l]["o"], EW[l], w[l]["bo"][:] if w[l]["bo"] is not None else None, l)

            def ln_transposes(stage):
                transposes(xn, xnT_mm, 0, D, xn_ready, XN0[stage])

            ln_transposes(2)
            attention(1)

            ln_transposes(3)
            pe.wait_ge(xnT_ready, (LN_AT[3] + 1) * 4)
            pe.wait_ge(moe_small, 32)
            for t in range(NT):
                o = bank[6][:, t * E_MOE:(t + 1) * E_MOE]
                for i in range(DC):
                    pe.matmul(o, xnT[:, i, t * P:(t + 1) * P], wg[:, i, :], start=(i == 0), stop=False)
                ins = pe.matmul(o, onesf[0:1, :], bg[0:1, :], start=False, stop=True)
            ins.then_inc(lg_mm, 1)
            pe.wait_ge(mask_ready, 1)
            for t in range(NT):
                ins = pe.matmul(bank[7][:, 0:E_MOE], onesf[:], mskd[:, t, :], start=(t == 0), stop=(t == NT - 1))
            ins.then_inc(den_mm, 1)
            for e in range(E_MOE):
                pe.wait_ge(moe_ld[e % 2], 32 * (e // 2 + 1))
                for h in range(2):
                    for f in range(F_MOE // P):
                        n = (e * 2 + h) * (F_MOE // P) + f
                        if n >= 2:
                            pe.wait_ge(up_act, n - 1)
                        for i in range(DC):
                            ins = pe.matmul(bank[n % 2], mw1[e % 2][:, i, f * P:(f + 1) * P], xnT[:, i, h * CH:(h + 1) * CH], start=(i == 0), stop=(i == DC - 1))
                        ins.then_inc(up_mm, 1)
                    pe.wait_ge(up_act, (e * 2 + h + 1) * (F_MOE // P))
                    for q in range(QT):
                        n = (e * 2 + h) * QT + q
                        if n >= 2:
                            pe.wait_ge(down_add, n - 1)
                        for f in range(F_MOE // P):
                            ins = pe.matmul(bank[4 + n % 2][:, 0:D], hid[h][:, f, q * P:(q + 1) * P], mw2[e % 2][:, f, :], start=(f == 0), stop=(f == F_MOE // P - 1))
                        ins.then_inc(down_mm, 1)

            ln_transposes(4)
            attention(2)

            ln_transposes(5)
            pe.wait_ge(xnT_ready, (LN_AT[5] + 1) * 4)
            pe.wait_ge(glu_ld, 16 * 8)
            nf = F_GLU // P
            for h in range(2):
                for f in range(nf):
                    n = h * nf + f
                    if n >= 2:
                        pe.wait_ge(glu_h, n - 1)
                    for j, gw in enumerate((gw1, gw2)):
                        for i in range(DC):
                            ins = pe.matmul(bank[2 * j + n % 2], gw[:, i, f * P:(f + 1) * P], xnT[:, i, h * CH:(h + 1) * CH], start=(i == 0), stop=(i == DC - 1))
                        ins.then_inc(glu_mm, 1)
                pe.wait_ge(glu_h, (h + 1) * nf)
                for i, src in enumerate((ha, hb)):
                    if h == 0:
                        pe.wait_ge(h1_ld[i], 16)
                    if i:
                        pe.wait_ge(h1_act, (h * 2 + 1) * nf)
                    for f in range(nf):
                        n = (h * 2 + i) * nf + f
                        if n >= 2:
                            pe.wait_ge(h1_act, n - 1)
                        for j in range(nf):
                            ins = pe.matmul(bank[4 + n % 2], gh[i][:, j, f * P:(f + 1) * P], src[:, j, :], start=(j == 0), stop=(j == nf - 1))
                        ins.then_inc(h1_mm, 1)
                pe.wait_ge(h1_act, (h * 2 + 2) * nf)
                for q in range(QT):
                    t = h * QT + q
                    if t >= 2:
                        pe.wait_ge(x_ready, 5 * NT + t - 1)
                    for j in range(nf):
                        ins = pe.matmul(bank[6 + t % 2][:, 0:D], ha[:, j, q * P:(q + 1) * P], gw3[:, j, :], start=(j == 0), stop=(j == nf - 1))
                    ins.then_inc(out_mm, 1)

            ln_transposes(6)
            attention(3)

            ln_transposes(7)
            pe.wait_ge(fin_ld, 16 * 5)
            pe.wait_ge(mix_ready, 4)
            for t in range(NT):
                if t >= 2:
                    pe.wait_ge(rk_act, t - 1)
                for i in range(DC):
                    ins = pe.matmul(bank[t % 2][:, 0:D], xr[:, i, t * P:(t + 1) * P], mwr[:, i, :], start=(i == 0), stop=(i == DC - 1))
                ins.then_inc(rk_mm, 1)
            for j in range(2 * DC):
                c, h = j // 2, j % 2
                if j >= 2:
                    pe.wait_ge(rk_act, NT + j - 1)
                for i in range(DC):
                    ins = pe.matmul(bank[2 + j % 2], mwk[:, i, c * P:(c + 1) * P], xk[:, i, h * CH:(h + 1) * CH], start=(i == 0), stop=(i == DC - 1))
                ins.then_inc(rk_mm, 1)
            pe.wait_ge(rk_sq, 2 * DC)
            for t in range(NT):
                if t >= 2:
                    pe.wait_ge(rv_ready, t - 1)
                for i in range(DC):
                    ins = pe.matmul(bank[4 + t % 2][:, 0:D], kact[:, i, t * P:(t + 1) * P], mwv[:, i, :], start=(i == 0), stop=(i == DC - 1))
                ins.then_inc(fv_mm, 1)

        @block.vector
        def _(dve):
            ch = Chain(dve, chain_dve)

            def normalise(stage):
                if stage:
                    dve.wait_ge(x_ready, stage * NT)
                else:
                    dve.wait_ge(ld_x, 16)
                for t in range(NT):
                    ins = dve.bn_stats(bnst[:, t, :], x[:, t, :])
                ch.link(ins)
                for t in range(NT):
                    ins = dve.bn_aggr(mv[:, t, :], bnst[:, t, :])
                ins.then_inc(var_ready, 1)
                dve.wait_ge(var_ready, stage + 1)
                dve.wait_ge(rstd_ready, stage + 1)
                for t in range(NT):
                    dve.tensor_scalar(xn[:, t, :], x[:, t, :], mv[:, t, 0:1], rstd[:, t:t + 1], ALU.subtract, ALU.mult).then_inc(xn_ready, 1)

            def add_out(stage, tg, banks=4):
                for t in range(NT):
                    dve.wait_ge(out_mm, OUT_AT[stage] * NT + t + 1)
                    dve.scalar_tensor_tensor(x[:, t, :], bank[banks + t % 2][:, 0:D], tg, x[:, t, :], ALU.mult, ALU.add).then_inc(x_ready, 1)

            normalise(0)
            dve.wait_ge(ld_w0, 32)
            for t in range(NCT):
                dve.wait_ge(kv0_mm, t + 1)
                if t >= 4:
                    dve.wait_ge(table_written[t % 4], 16 * table_dmas(t - 4))
                dve.tensor_tensor(a_kv0[t % 4], bank[4 + t % 2], a_bkv, ALU.add).then_inc(kv0_ready, 1)
            dve.wait_ge(consts_ready, 5)
            dve.wait_ge(ld_small, 16 * 8)
            dve.tensor_copy(a_ref, a_iref)
            ch.link(dve.tensor_copy(a_pos.rearrange("p t j -> p (t j)"), a_ipos[:, 0:NT * WIN]))
            dve.tensor_scalar(a_wrap[:, 0:NT * WIN], a_pos.rearrange("p t j -> p (t j)"), 0.0, float(M), ALU.is_lt, ALU.mult)
            ch.link(dve.tensor_copy(a_loc, a_ipos[:, NT * WIN:]))
            ch.link(dve.tensor_tensor(a_pos.rearrange("p t j -> p (t j)"), a_pos.rearrange("p t j -> p (t j)"), a_wrap[:, 0:NT * WIN], ALU.add))
            mf = a_mask.rearrange("p j e -> p (j e)")
            ch.link(dve.tensor_scalar(mf, mf.bitcast(I32), -1.0, 1.0, ALU.mult, ALU.add))
            ch.link(dve.tensor_reduce(a_msum, mf.rearrange("p (b m) -> p b m", b=B), AX.X, ALU.add))
            ch.link(dve.tensor_scalar(a_msum, a_msum, -1.0, None, ALU.add))
            for t in range(NT):
                dve.wait_ge(q0_mm, t + 1)
                dve.tensor_tensor(a_q0[:, t, :], bank[4 + t % 2][:, 0:D], a_bq0, ALU.add).then_inc(q0_ready, 1)
            dve.wait_ge(off_mm, NT)
            u = a_u.rearrange("p t k -> p (t k)")
            tt = a_t.rearrange("p t k -> p (t k)")
            for b in range(B):
                ins = dve.tensor_tensor(a_u[:, b * QT:(b + 1) * QT, :], bank[2 + b][:, 0:QT * HK].rearrange("p (t k) -> p t k", t=QT),
                                        bc(a_boff.unsqueeze(1), [P, QT, HK]), ALU.add)
            ch.link(ins)
            ch.link(dve.tensor_tensor(u, u, a_ref, ALU.add))
            ch.link(dve.tensor_tensor(a_u, a_u, bc(a_loc.unsqueeze(2), [P, NT, HK]), ALU.add))
            half = QT * HK
            halves = [(b, slice(b * half, (b + 1) * half)) for b in range(B)]
            ch.link(dve.reciprocal(a_rlen, a_msum))
            for b, h in halves:
                ins = dve.tensor_scalar(tt[:, h], u[:, h], a_rlen[:, b:b + 1], MAGIC, ALU.mult, ALU.add)
            ch.link(ins)
            for b, h in halves:
                ins = dve.tensor_scalar(tt[:, h], tt[:, h], -MAGIC, a_msum[:, b:b + 1], ALU.add, ALU.mult)
            ch.link(ins)
            ch.link(dve.tensor_tensor(u, u, tt, ALU.subtract))
            for b, h in halves:
                ins = dve.tensor_scalar(tt[:, h], u[:, h], a_msum[:, b:b + 1], 0.0, ALU.mult, ALU.is_lt)
            ch.link(ins)
            for b, h in halves:
                ins = dve.scalar_tensor_tensor(u[:, h], tt[:, h], a_msum[:, b:b + 1], u[:, h], ALU.mult, ALU.add)
            ch.link(ins)
            ch.link(dve.tensor_scalar(u, u, 1.0 / float(M - 1), 2.0, ALU.mult, ALU.mult))
            ch.link(dve.tensor_scalar(u, u, -1.0, 1.0, ALU.add, ALU.add))
            ch.link(dve.tensor_scalar(u, u, float(M), -1.0, ALU.mult, ALU.add))
            ch.link(dve.tensor_scalar(u, u, 0.5, None, ALU.mult))
            ch.link(dve.tensor_tensor(a_t, a_u, bc(a_loc.unsqueeze(2), [P, NT, HK]), ALU.subtract))
            ch.link(dve.tensor_scalar(tt, tt, float(BACK), None, ALU.add))
            ch.link(dve.tensor_scalar(a_wrap, tt, float(M // 2), float(-M), ALU.is_ge, ALU.mult))
            ch.link(dve.tensor_tensor(tt, tt, a_wrap, ALU.add))
            ch.link(dve.tensor_scalar(a_wrap, tt, 0.0, None, ALU.is_ge))
            ch.link(dve.scalar_tensor_tensor(tt, tt, float(WIN - 1), a_wrap, ALU.is_le, ALU.mult))
            dve.tensor_reduce(a_cov[:, 0:1], tt, AX.X, ALU.add).then_inc(cov_ready, 1)
            dve.wait_ge(cov_mm, 1)
            dve.tensor_scalar(flag_i[:], bank[0][0:1, 0:1], float(P * NT * HK) - 0.5, None, ALU.is_lt).then_inc(flag_ready, 1)
            dve.wait_ge(flag_ready, 1)
            uncovered = dve.value_load(flag_i[0:1, 0:1], min_val=0, max_val=1)
            dve.wait_ge(cov_ready, 1)
            for t in range(NT):
                ins = dve.tensor_tensor(a_W[:, t], bc(a_u[:, t, :].unsqueeze(2), [P, HK, WIN]), bc(a_pos[:, t, :].unsqueeze(1), [P, HK, WIN]), ALU.subtract)
            ch.link(ins)
            Wf = a_W.rearrange("p t k j -> p (t k j)")
            ch.link(dve.scalar_tensor_tensor(Wf, Wf, -1.0, Wf, ALU.mult, ALU.min))
            ch.link(dve.tensor_scalar(Wf, Wf, 1.0, 0.0, ALU.add, ALU.max))

            def scores0(prod, S_out):
                return dve.tensor_reduce(S_out.rearrange("p h j -> p j h"), prod.rearrange("p j (h d) -> p j h d", h=H0), AX.X, ALU.add)

            def hkj(a):
                return a.rearrange("p (h k) j -> p h k j", h=H0)

            S_hj = a_S.rearrange("p j h -> p (j h)").rearrange("p (h j) -> p h j", h=H0)
            for t in range(NT):
                dve.wait_ge(prodK_ready, t + 1)
                ins = scores0(a_prod[t % 2], S_hj)
                ins.then_inc(prodK_used, 1)
                dve.wait_ge(prodK_used, t + 1)
                ch.link(dve.tensor_tensor(hkj(a_tmp), hkj(a_W[:, t]), bc(S_hj.unsqueeze(2), [P, H0, NK, WIN]), ALU.mult))
                ch.link(dve.tensor_reduce(a_sc[:, t, :], a_tmp, AX.X, ALU.add))

            gen_links = [0]

            def general(loop0, use):
                with dve.If(uncovered):
                    if loop0 == 0:
                        dve.sem_inc(gen_used, 1)
                    for t in range(NT):
                        def link(ins):
                            gen_links[0] += 1
                            ins.then_inc(gen_chain, 1)
                            dve.wait_ge(gen_chain, gen_links[0])

                        link(dve.tensor_copy(a_gpos, a_pos[:, t, :]))
                        first = gen_links[0]
                        with dve.Fori(1, M // WIN) as s:
                            done = [0]

                            def step(ins):
                                done[0] += 1
                                ins.then_inc(gen_chain, 1)
                                dve.wait_ge(gen_chain, (s - 1) * GEN_LINKS + (first + done[0]))

                            step(dve.tensor_scalar(a_gpos, a_gpos, float(WIN), None, ALU.add))
                            step(dve.tensor_scalar(a_gwrap, a_gpos, float(M), float(-M), ALU.is_ge, ALU.mult))
                            step(dve.tensor_tensor(a_gpos, a_gpos, a_gwrap, ALU.add))
                            step(dve.tensor_tensor(a_gW, bc(a_u[:, t, :].unsqueeze(2), [P, HK, WIN]), bc(a_gpos.unsqueeze(1), [P, HK, WIN]), ALU.subtract))
                            step(dve.scalar_tensor_tensor(a_gW, a_gW, -1.0, a_gW, ALU.mult, ALU.min))
                            step(dve.tensor_scalar(a_gW, a_gW, 1.0, 0.0, ALU.add, ALU.max))
                            use(t, step, lambda: dve.wait_ge(gen_ld, s * 16 + 16 * (loop0 + t) * GEN_STEPS),
                                lambda ins: (ins.then_inc(gen_used, 1), dve.wait_ge(gen_used, s + ((loop0 + t) * GEN_STEPS + 1))))
                            assert done[0] == GEN_LINKS, done
                        gen_links[0] += GEN_STEPS * GEN_LINKS

            def more_scores(t, step, loaded, used):
                loaded()
                step(dve.tensor_tensor(gwin, gwin, bc(a_q0[:, t, :].unsqueeze(1), [P, WIN, D]), ALU.mult))
                used(scores0(gwin, S_hj))
                step(dve.tensor_tensor(hkj(a_tmp), hkj(a_gW), bc(S_hj.unsqueeze(2), [P, H0, NK, WIN]), ALU.mult))
                step(dve.tensor_reduce(a_small[:, 0:HK], a_tmp, AX.X, ALU.add))
                step(dve.tensor_tensor(a_sc[:, t, :], a_sc[:, t, :], a_small[:, 0:HK], ALU.add))

            def more_context(t, step, loaded, used):
                step(dve.tensor_tensor(a_tmp, a_gW, bc(a_sc[:, t, :].unsqueeze(2), [P, HK, WIN]), ALU.mult))
                step(dve.tensor_reduce(a_A[0], a_tmp.rearrange("p (h k) j -> p h j k", h=H0), AX.X, ALU.add))
                loaded()
                step(dve.tensor_tensor(gwin.rearrange("p j (h d) -> p j h d", h=H0), gwin.rearrange("p j (h d) -> p j h d", h=H0),
                                       bc(a_A[0].rearrange("p h j -> p j h").unsqueeze(3), [P, WIN, H0, HD0]), ALU.mult))
                used(dve.tensor_reduce(a_small, gwin.rearrange("p j e -> p e j"), AX.X, ALU.add))
                step(dve.tensor_tensor(ctx0[:, t, :], ctx0[:, t, :], a_small, ALU.add))

            general(0, more_scores)
            sc = a_sc.rearrange("p t (h k) -> p (t h) k", h=H0)
            ch.link(dve.tensor_reduce(a_mx, sc, AX.X, ALU.max))
            dve.tensor_tensor(sc, sc, bc(a_mx.unsqueeze(2), [P, NT * H0, NK]), ALU.subtract).then_inc(sub0_ready, 1)
            dve.wait_ge(exp0_ready, 1)
            ch.link(dve.tensor_reduce(a_sm, sc, AX.X, ALU.add))
            ch.link(dve.reciprocal(a_sm, a_sm))
            ch.link(dve.scalar_tensor_tensor(sc, sc, 0.5, bc(a_sm.unsqueeze(2), [P, NT * H0, NK]), ALU.mult, ALU.mult))

            def sum_rows(t):
                dve.wait_ge(prodV_ready, t + 1)
                dve.tensor_reduce(ctx0[:, t, :], a_prod[t % 2].rearrange("p j e -> p e j"), AX.X, ALU.add).then_inc(prodV_used, 1)

            for t in range(NT):
                ch.link(dve.tensor_tensor(a_tmp, a_W[:, t], bc(a_sc[:, t, :].unsqueeze(2), [P, HK, WIN]), ALU.mult))
                if t >= 2:
                    dve.wait_ge(prodV_ready, t - 1)
                dve.tensor_reduce(a_A[t % 2], a_tmp.rearrange("p (h k) j -> p h j k", h=H0), AX.X, ALU.add).then_inc(attw_ready, 1)
                dve.wait_ge(attw_ready, t + 1)
                if t:
                    sum_rows(t - 1)
            sum_rows(NT - 1)
            dve.wait_ge(prodV_used, NT)
            general(NT, more_context)
            dve.sem_inc(ctxn_ready, NT)
            dve.wait_ge(tanh_ready, 2)
            add_out(0, tgx[:, 0:1])

            dve.wait_ge(i8_w, 16)
            ch.link(dve.tensor_reduce(i8wsc, i8w, AX.X, ALU.max, apply_absolute_value=True))
            ch.link(dve.tensor_scalar(i8wsc, i8wsc, 1e-12, 1.0 / 127.0, ALU.max, ALU.mult))
            ch.link(dve.reciprocal(i8wr, i8wsc))
            for i in range(DC):
                ch.link(dve.tensor_scalar(i8w[:, i], i8w[:, i], i8wr[:, i:i + 1], MAGIC, ALU.mult, ALU.add))
                ch.link(dve.tensor_scalar(i8w[:, i], i8w[:, i], -MAGIC, 127.0, ALU.add, ALU.min))
                ins = dve.tensor_scalar(i8wq[:, i], i8w[:, i], -127.0, None, ALU.max)
            ins.then_inc(i8_wq, 2)
            normalise(1)
            dve.wait_ge(xn_ready, 2 * NT)
            ch.link(dve.tensor_reduce(i8xsc, xn[:], AX.X, ALU.max, apply_absolute_value=True))
            ch.link(dve.tensor_scalar(i8xsc, i8xsc, 1e-12, 1.0 / 127.0, ALU.max, ALU.mult))
            ch.link(dve.reciprocal(i8xr, i8xsc))
            for t in range(NT):
                ins = dve.tensor_scalar(xn[:, t], xn[:, t], i8xr[:, t:t + 1], MAGIC, ALU.mult, ALU.add)
            ch.link(ins)
            ch.link(dve.tensor_scalar(xn[:], xn[:], -MAGIC, 127.0, ALU.add, ALU.min))
            for t in range(NT):
                dve.tensor_scalar(i8xq[:, t], xn[:, t], -127.0, None, ALU.max).then_inc(i8_xq, 1)
            dve.wait_ge(i8_qT, DC + 1)
            dve.wait_ge(i8_xq, NT)
            for t in range(NT):
                dve.wait_ge(out_mm, OUT_AT[1] * NT + t + 1)
                ch.link(dve.scalar_tensor_tensor(xn[:, t, :], bank[4 + t % 2][:, 0:D], i8xsc[:, t:t + 1], i8sc_bc, ALU.mult, ALU.mult))
                dve.scalar_tensor_tensor(x[:, t, :], xn[:, t, :], tgf[:, 0:1], x[:, t, :], ALU.mult, ALU.add).then_inc(x_ready, 1)

            def attention(l):
                H, dh, _ = ATT[l]
                n = min(P, EW[l])
                for j in range(QCH0[l + 1] - QCH0[l]):
                    k = QCH0[l] + j
                    dve.wait_ge(qp_evac, k + 1)
                    hi, mid, lo = qph[k % 2]
                    ch.link(dve.tensor_tensor(qr[k % 2][0:n], qf[k % 2][0:n], hi[0:n], ALU.subtract))
                    ch.link(dve.tensor_copy(mid[0:n], qr[k % 2][0:n]))
                    dve.tensor_tensor(lo[0:n], qr[k % 2][0:n], mid[0:n], ALU.subtract).then_inc(qp_split, 1)

                if l == 1:
                    dve.wait_ge(prep_evac, PREP_MM)
                dve.memset(bank[7], 0.0).then_inc(pv_done, 1)

                def reduce_half(uu):
                    g, col, hf = uu // HALVES, uu // 2 % (HG * QT), uu % 2
                    un = GROUP0[l] * HALVES + uu
                    gi = GROUP0[l] + g
                    dve.wait_ge(max_mm, un + 1)
                    if uu % HALVES == 0 and gi >= 2:
                        dve.wait_ge(max_fin, gi - 1)
                    dve.tensor_reduce(mxh[gi % 2][:, col, hf:hf + 1], bank[4 + un % 2], AX.X, ALU.max).then_inc(max_red, 1)
                    if uu % HALVES == HALVES - 1:
                        dve.wait_ge(max_red, un + 1)
                        if gi >= 2:
                            dve.wait_ge(max_tr, gi - 1)
                        dve.tensor_reduce(mxg[gi % 2], mxh[gi % 2], AX.X, ALU.max).then_inc(max_fin, 1)

                def shift_low(g):
                    gi = GROUP0[l] + g
                    dve.wait_ge(max_hi, gi + 1)
                    dve.scalar_tensor_tensor(shp[gi % 2][1][0:HG * QT, :], bank[6][0:HG * QT, 0:P], -1.0, shp[gi % 2][0][0:HG * QT, :],
                                             ALU.mult, ALU.subtract).then_inc(max_lo, 1)

                def normalise_context(g):
                    gi = GROUP0[l] + g
                    b, h0 = g // (H // HG), (g % (H // HG)) * HG
                    dve.wait_ge(pv_tr, gi + 1)
                    turned = bank[6].rearrange("p (q h e) -> p q h e", q=QT, h=HG)
                    ch.link(dve.reciprocal(rsum, turned[:, :, :, dh]))
                    dst = xn[:, b * QT:(b + 1) * QT, h0 * dh:(h0 + HG) * dh].rearrange("p q (h e) -> p q h e", h=HG)
                    dve.tensor_tensor(dst, turned[:, :, :, 0:dh], bc(rsum.unsqueeze(3), [P, QT, HG, dh]), ALU.mult).then_inc(norm_ready, 1)

                for step in schedule(l):
                    if step[0] == "max":
                        reduce_half(step[1])
                    elif step[0] == "tr":
                        shift_low(step[1])
                    elif step[2] == CTX_SLOT and step[1]:
                        normalise_context(step[1] - 1)
                normalise_context(NGROUPS[l] - 1)
                add_out(2 * l, tgx[:, l:l + 1])

            normalise(2)
            attention(1)

            normalise(3)
            dve.wait_ge(lg_mm, 1)
            lg = bank[6][:, 0:NT * E_MOE].rearrange("p (t e) -> p t e", t=NT)
            ch.link(dve.tensor_reduce(lgm, lg, AX.X, ALU.max))
            dve.tensor_tensor(lgs, lg, bc(lgm, [P, NT, E_MOE]), ALU.subtract).then_inc(lg_exp_in, 1)
            for e in range(E_MOE):
                ins = dve.memset(rank8[:, e:e + 1], float(E_MOE - e))
            ch.link(ins)
            dve.wait_ge(lg_exp, 1)
            ch.link(dve.tensor_reduce(lgz, lge, AX.X, ALU.add))
            ch.link(dve.reciprocal(lgz, lgz))
            ch.link(dve.tensor_tensor(lge, lge, bc(lgz, [P, NT, E_MOE]), ALU.mult))
            ch.link(dve.tensor_reduce(lgm, lge, AX.X, ALU.max))
            ch.link(dve.tensor_tensor(lgs, lge, bc(lgm, [P, NT, E_MOE]), ALU.is_ge))
            ch.link(dve.tensor_tensor(lgs, lgs, bc(rank8.unsqueeze(1), [P, NT, E_MOE]), ALU.mult))
            ch.link(dve.tensor_reduce(idx2, lgs, AX.X, ALU.max))
            ch.link(dve.tensor_tensor(lgs, lgs, bc(idx2, [P, NT, E_MOE]), ALU.is_equal))
            dve.tensor_tensor(mskd, lgs, lge, ALU.mult).then_inc(mask_ready, 1)
            dve.wait_ge(den_mm, 1)
            den = rank8
            ch.link(dve.tensor_scalar(den, bank[7][:, 0:E_MOE], 1e-6, None, ALU.add))
            ch.link(dve.reciprocal(den, den))
            ch.link(dve.tensor_tensor(gate, mskd, bc(den.unsqueeze(1), [P, NT, E_MOE]), ALU.mult))
            ch.link(dve.tensor_scalar(gate, gate, float(T), tgf[:, 1:2], ALU.mult, ALU.mult))
            for e in range(E_MOE):
                for t in range(NT):
                    n = e * NT + t
                    dve.wait_ge(down_mm, n + 1)
                    if e:
                        dve.wait_ge(down_add, n + 1 - NT)
                    ins = dve.scalar_tensor_tensor(x[:, t, :], bank[4 + n % 2][:, 0:D], gate[:, t, e:e + 1], x[:, t, :], ALU.mult, ALU.add)
                    ins.then_inc(down_add, 1)
            dve.wait_ge(down_add, E_MOE * NT)
            dve.sem_inc(x_ready, NT)

            normalise(4)
            attention(2)

            normalise(5)
            nf = F_GLU // P
            for h in range(2):
                for f in range(nf):
                    n = h * nf + f
                    dve.wait_ge(glu_mm, 2 * n + 2)
                    dve.wait_ge(glu_silu, n + 1)
                    if h and f == 0:
                        dve.wait_ge(out_mm, OUT_AT[5] * NT + QT)
                    dve.scalar_tensor_tensor(ha[:, f, :], bank[2 + n % 2], gsc[:, 1, f:f + 1], gtmp[n % 2], ALU.mult, ALU.mult).then_inc(glu_h, 1)
                for q in range(QT):
                    t = h * QT + q
                    dve.wait_ge(out_mm, OUT_AT[5] * NT + t + 1)
                    ch.link(dve.tensor_tensor(xn[:, t, :], bank[6 + t % 2][:, 0:D], gs3, ALU.mult))
                    dve.scalar_tensor_tensor(x[:, t, :], xn[:, t, :], tgf[:, 2:3], x[:, t, :], ALU.mult, ALU.add).then_inc(x_ready, 1)

            normalise(6)
            attention(3)

            normalise(7)
            dve.wait_ge(fin_ld, 16 * 5)
            ch.link(dve.tensor_scalar(mom, mmu, -1.0, 1.0, ALU.mult, ALU.add))
            dve.wait_ge(xnT_ready, (LN_AT[7] + 1) * 4)
            for c in range(DC):
                for i, dst in enumerate((xr, xk)):
                    ch.link(dve.tensor_scalar(dst[:, c, :], xnT[:, c, :], mmu[:, i, c:c + 1], None, ALU.mult))
                    for b in range(B):
                        lo, hi = b * S, (b + 1) * S
                        ins = dve.scalar_tensor_tensor(dst[:, c, lo + 1:hi], xnT[:, c, lo:hi - 1], mom[:, i, c:c + 1], dst[:, c, lo + 1:hi], ALU.mult, ALU.add)
                    ins.then_inc(mix_ready, 1)
            for i in range(2 * DC):
                c, h = i // 2, i % 2
                dve.wait_ge(rk_act, NT + i + 1)
                ka = kact[:, c, h * CH:(h + 1) * CH]
                dve.tensor_tensor(ka, ka, ka, ALU.mult).then_inc(rk_sq, 1)
            for t in range(NT):
                dve.wait_ge(fv_mm, t + 1)
                ch2 = dve.tensor_tensor(rv[:, t, :], rv[:, t, :], bank[4 + t % 2][:, 0:D], ALU.mult)
                ch2.then_inc(rv_ready, 1)
                dve.wait_ge(rv_ready, t + 1)
                dve.scalar_tensor_tensor(x[:, t, :], rv[:, t, :], tgf[:, 3:4], x[:, t, :], ALU.mult, ALU.add).then_inc(x_ready, 1)


def kernel(**inputs):
    import numpy as _np
    import concourse.bacc as _bacc
    from concourse import mybir as _mybir
    from concourse.bass_utils import run_bass_kernel_spmd as _run

    a = {k: _np.asarray(v) for k, v in inputs.items()}
    heads = lambda m: m.transpose(1, 0, 2).reshape(m.shape[1], -1)
    cat = lambda *m: _np.concatenate(m, axis=-1)
    cols = lambda v: v.reshape(-1, min(P, v.size)).T
    arrays = {
        "b0qT": cols(a["L0_xattn_bq"]),
        "x": a["x"].reshape(T, D), "ctxT": a["ctx_1024"].reshape(CT, D).T, "mask": a["mask_BxS2_if0"],
        "g_xattn": a["g_xattn"], "g_ffn": a["g_ffn"],
        "w0kv": cat(a["L0_xattn_Wk"].T, a["L0_xattn_Wv"].T), "b0kv": cat(a["L0_xattn_bk"], a["L0_xattn_bv"]),
        "w0q": a["L0_xattn_Wq"].T, "b0q": a["L0_xattn_bq"], "woff": a["L0_xattn_Woff"].T, "boff": a["L0_xattn_boff"],
        "w0o": a["L0_xattn_Wo"].T, "b0o": a["L0_xattn_bo"], "i8rhsT": a["L0_ffn_rhs"].T,
        "wq1": heads(a["L1_xattn_Wq"]), "wkv1": cat(heads(a["L1_xattn_Wk"]), heads(a["L1_xattn_Wv"])), "wo1": a["L1_xattn_Wo"],
        "wg": a["L1_ffn_Wg"], "bg": a["L1_ffn_bg"], "w1": a["L1_ffn_W1"], "w2": a["L1_ffn_W2"],
        "glu1": a["L2_ffn_w1_w"].T, "glu2": a["L2_ffn_w2_w"].T, "gluh1": a["L2_ffn_h1_w"].T, "gluh2": a["L2_ffn_h2_w"].T,
        "glu3": a["L2_ffn_w3_w"].T, "s1": cols(a["L2_ffn_w1_s"]), "s2": cols(a["L2_ffn_w2_s"]), "sh1": cols(a["L2_ffn_h1_s"]),
        "sh2": cols(a["L2_ffn_h2_s"]), "s3": a["L2_ffn_w3_s"],
        "w_r": a["L3_ffn_W_r"].T, "w_k": a["L3_ffn_W_k"].T, "w_v": a["L3_ffn_W_v"].T, "mu_r": cols(a["L3_ffn_mu_r"]), "mu_k": cols(a["L3_ffn_mu_k"]),
    }
    for l in (2, 3):
        p = f"L{l}_xattn_"
        arrays |= {f"wq{l}": a[p + "Wq"], f"wkv{l}": cat(a[p + "Wk"], a[p + "Wv"]), f"wo{l}": a[p + "Wo"], f"bq{l}": cols(a[p + "bq"]),
                   f"bk{l}": cols(a[p + "bk"]), f"bv{l}": a[p + "bv"], f"bo{l}": a[p + "bo"]}
    nc = _bacc.Bacc("TRN2", target_bir_lowering=False, num_devices=1)
    io, feed = {}, {}
    for name, v in arrays.items():
        feed[f"in_{name}"] = _np.ascontiguousarray(v)
        io[name] = nc.dram_tensor(f"in_{name}", feed[f"in_{name}"].shape, _mybir.dt.from_np(feed[f"in_{name}"].dtype), kind="ExternalInput").ap()
    io["out"] = nc.dram_tensor("out_0", (T, D), F32, kind="ExternalOutput").ap()
    build(nc, io)
    got = _run(nc, [feed], core_ids=[0]).results[0]["out_0"]
    return _np.asarray(got).reshape(B, S, D)
```

```python
from contextlib import ExitStack

import concourse.bass as bass
from concourse import mybir

F32 = mybir.dt.float32
BF16 = mybir.dt.bfloat16
I32 = mybir.dt.int32
ALU = mybir.AluOpType
ACT = mybir.ActivationFunctionType
AX = mybir.AxisListType

P = 128
D = 256
DC = D // P
B = 2
S = 512
M = 1024
T = B * S
NT = T // P
QT = S // P
CT = B * M
NCT = CT // P
CH = 512
EPS_LN = 1e-5
MAGIC = 1.5 * 2.0**23

H0, HD0, NK = 16, 16, 5
HK = H0 * NK
LEFT = (-NK) // 2
WIN = 8
BACK = 5
ROWS = M + S + 8

ATT = {1: (16, 8, 256 ** -0.5), 2: (16, 16, 0.25), 3: (8, 4, 1.0 / float(32.0 ** 0.5))}
HG = 4
KT = M // P
PARTS_Q = (0, 0, 0, 1, 1, 2, 1, 2, 2)
PARTS_K = (0, 1, 2, 0, 1, 0, 2, 1, 2)
NPAIRS = {1: 9, 2: 6, 3: 9}
MIN_ROWS = 66
SHIFT_ROWS = 2

NGROUPS = {l: B * ATT[l][0] // HG for l in ATT}
GROUP0 = {l: sum(NGROUPS[i] for i in range(1, l)) for l in range(1, 5)}
EW = {l: ATT[l][0] * ATT[l][1] for l in ATT}
EC = {l: max(1, EW[l] // P) for l in ATT}
PREP0 = {l: sum(EC[i] * CT // CH for i in range(1, l)) for l in range(1, 5)}
QCH0 = {l: sum(EC[i] * T // CH for i in range(1, l)) for l in range(1, 5)}
GEN_STEPS = M // WIN - 1
GEN_LINKS = 10


def keys_and_queries(gi):
    layer = lambda i: next(l for l in ATT if i < GROUP0[l + 1])
    return sum(16 * 2 * NPAIRS[layer(i)] for i in range(gi % 3, gi + 1, 3))


LN_AT = {0: 0, 2: 1, 3: 2, 4: 3, 5: 4, 6: 5, 7: 6}
OUT_AT = {0: 0, 1: 1, 2: 2, 4: 3, 5: 4, 6: 5}
CTX_BANKS0 = {0: 0, 1: 2 * DC, 2: 2 * DC + 2 * EC[1], 3: 2 * DC + 2 * EC[1] + 2 * EC[2]}
HALVES = HG * QT * 2
LEAD = HALVES + 12

TURN_LAG = 4
TURN_BANKS = (4, 5, 6)
CTX_SLOT = 4
XN0 = {s: s * NT for s in range(8)}
LATE_LOADS = 2 + 3 * 2 + 2 * 2
PREP_MM = PREP0[4] + 3 * NCT


def schedule(l):
    steps, turns, u, total = [], 0, 0, NGROUPS[l] * HALVES

    def turn(kind, *what):
        nonlocal turns
        steps.append((kind, *what, turns))
        turns += 1

    def maxima(upto):
        nonlocal u
        while u < min(upto, total):
            turn("max", u)
            u += 1
            if u > HALVES and u % HALVES == TURN_LAG:
                turn("turn", u // HALVES - 1)
            if u == total:
                turn("turn", NGROUPS[l] - 1)

    for g in range(NGROUPS[l]):
        for kt in range(KT):
            sl = g * KT + kt
            maxima(LEAD + 4 * sl)
            steps.append(("score", g, kt, 0))
            maxima(LEAD + 4 * sl + 2)
            if sl:
                steps.append(("values", (sl - 1) // KT, (sl - 1) % KT))
            steps.append(("score", g, kt, 1))
            if kt == 0 and g:
                steps.append(("copy", g - 1))
            if kt == CTX_SLOT and g:
                turn("context", g - 1)
    steps += [("values", NGROUPS[l] - 1, KT - 1), ("copy", NGROUPS[l] - 1)]
    turn("context", NGROUPS[l] - 1)
    return steps


E_MOE, F_MOE = 8, 1024
FM = F_MOE // P
CAP = 192
SUB = CAP // 2
OVER = (T - 1) // CAP
SLOT_ROWS = -(-(E_MOE + OVER) * CAP // P) * P
UP_PER_BANK = CH // CAP
MOE_BUFS = 3
F_GLU = 1024


def build(nc, io):
    with ExitStack() as ctx:
        def sb(name, shape, dt=F32):
            return ctx.enter_context(nc.sbuf_tensor(name, shape, dt))

        def sem(name):
            return ctx.enter_context(nc.semaphore(name))

        st_bank = [ctx.enter_context(nc.psum_tensor(f"st_bank{i}", [P, 2, CH], F32)) for i in range(2)]
        bank = [st_bank[i // 2][:, i % 2, :] for i in range(4)]
        bank += [ctx.enter_context(nc.psum_tensor(f"bank{i}", [P, CH], F32))[:, :] for i in range(4, 8)]

        kv_table = nc.dram_tensor("kv_table", [B, ROWS, 2 * D], F32).ap()
        kparts = {l: nc.dram_tensor(f"kparts{l}", [3, ATT[l][0] * ATT[l][1], CT], BF16).ap() for l in ATT}
        qparts = {l: nc.dram_tensor(f"qparts{l}", [3, ATT[l][0] * ATT[l][1], T], BF16).ap() for l in ATT}

        slot_in = nc.dram_tensor("slot_in", [SLOT_ROWS, D], F32).ap()
        slot_out = nc.dram_tensor("slot_out", [SLOT_ROWS, D], F32).ap()

        x = sb("x", [P, NT, D])
        xn = sb("xn", [P, NT, D])
        xnT = sb("xnT", [P, DC, T])
        ctxT = sb("ctxT", [P, DC, CT])
        ident = sb("ident", [P, P])
        identb = sb("identb", [P, P], BF16)
        onesf = sb("onesf", [P, P])
        zero_row = sb("zero_row", [P, D // 2])
        before = sb("before", [P, P])
        bnst = sb("bnst", [P, NT, 6])
        mv = sb("mv", [P, NT, 2])
        rstd = sb("rstd", [P, NT])
        minus_half = sb("minus_half", [P, NT])
        tgx = sb("tgx", [P, 4])
        tgf = sb("tgf", [P, 4])
        gx = sb("gx", [P, 4])
        gf = sb("gf", [P, 4])
        ARENA = 31 * 1024
        arena = sb("arena", [P, ARENA])

        class Region:
            def __init__(self, at=0):
                self.at = at

            def take(self, shape, dt=F32):
                n = 1
                for s in shape:
                    n *= s
                words = n if dt in (F32, I32) else (n + 1) // 2
                ap = arena[:, self.at:self.at + words]
                self.at += words
                assert self.at <= ARENA, self.at
                if dt != F32:
                    ap = ap.bitcast(dt)
                if len(shape) == 2:
                    ap = ap.rearrange("p (a b) -> p a b", a=shape[0])
                elif len(shape) == 3:
                    ap = ap.rearrange("p (a b c) -> p a b c", a=shape[0], b=shape[1])
                elif len(shape) == 4:
                    ap = ap.rearrange("p (a b c d) -> p a b c d", a=shape[0], b=shape[1], c=shape[2])
                return ap

        w = {}
        for l in ATT:
            e = ATT[l][0] * ATT[l][1]
            w[l] = dict(
                q=sb(f"wq{l}", [P, DC, e]), o=sb(f"wo{l}", [min(e, P), (e + P - 1) // P, D]),
                bq=sb(f"bq{l}", [min(e, P), (e + P - 1) // P]) if l > 1 else None,
                bo=sb(f"bo{l}", [1, D]) if l > 1 else None)
        vaug = {l: sb(f"vaug{l}", [P, NCT, ATT[l][0], ATT[l][1] + 1]) for l in ATT}
        wo0 = sb("wo0", [P, DC, D])
        bo0 = sb("bo0", [1, D])

        chain_dve, chain_act, chain_pool = sem("chain_dve"), sem("chain_act"), sem("chain_pool")
        ld_ctx, ld_x, ld_w0, ld_prep, ld_small, ld_late = (sem(n) for n in (
            "ld_ctx", "ld_x", "ld_w0", "ld_prep", "ld_small", "ld_late"))
        consts_ready, tanh_ready = sem("consts_ready"), sem("tanh_ready")
        kv0_mm, kv0_ready = sem("kv0_mm"), sem("kv0_ready")
        table_written = [sem(f"table_written{i}") for i in range(4)]
        xn_ready, xnT_mm, xnT_ready = sem("xn_ready"), sem("xnT_mm"), sem("xnT_ready")
        qT0_mm, qT0_ready, q0_mm, q0_ready, off_mm = (sem(n) for n in ("qT0_mm", "qT0_ready", "q0_mm", "q0_ready", "off_mm"))
        cov_ready, cov_mm, flag_ready = sem("cov_ready"), sem("cov_mm"), sem("flag_ready")
        winK_ld = [sem(f"winK_ld{i}") for i in range(2)]
        winV_ld = [sem(f"winV_ld{i}") for i in range(2)]
        prodK_ready, prodK_used, prodV_ready, prodV_used = (sem(n) for n in ("prodK_ready", "prodK_used", "prodV_ready", "prodV_used"))
        sub0_ready, exp0_ready, attw_ready = sem("sub0_ready"), sem("exp0_ready"), sem("attw_ready")
        gen_ld, gen_used, gen_chain = sem("gen_ld"), sem("gen_used"), sem("gen_chain")
        ctxn_ready, ctxT_mm, ctxT_ready = sem("ctxn_ready"), sem("ctxT_mm"), sem("ctxT_ready")
        out_mm, x_ready = sem("out_mm"), sem("x_ready")
        prep_mm, prep_evac, prep_split = sem("prep_mm"), sem("prep_evac"), sem("prep_split")
        prep_st = [sem(f"prep_st{i}") for i in range(2)]
        prep_hi = sem("prep_hi")
        qp_mm, qp_evac, qp_split = sem("qp_mm"), sem("qp_evac"), sem("qp_split")
        qp_st = [sem(f"qp_st{i}") for i in range(2)]
        kq_zero, kq_ld, shift_ld = sem("kq_zero"), [sem(f"kq_ld{i}") for i in range(3)], [sem(f"shift_ld{i}") for i in range(3)]
        ones_rows = sem("ones_rows")
        max_mm, max_red, max_fin, max_tr, max_hi, max_lo = (sem(n) for n in ("max_mm", "max_red", "max_fin", "max_tr", "max_hi", "max_lo"))
        st_mm, exp_ready, pv_mm, pv_done = sem("st_mm"), sem("exp_ready"), sem("pv_mm"), sem("pv_done")
        pv_evac, pv_tr, norm_ready = sem("pv_evac"), sem("pv_tr"), sem("norm_ready")
        i8_scale, i8_tr, i8_bc, i8_qT, i8_w = sem("i8_scale"), sem("i8_tr"), sem("i8_bc"), sem("i8_qT"), sem("i8_w")
        i8_wq, i8_xq = sem("i8_wq"), sem("i8_xq")
        moe_small = sem("moe_small")
        lg_mm, lg_exp_in, lg_exp, mask_ready, den_mm, gate_ready = (sem(n) for n in (
            "lg_mm", "lg_exp_in", "lg_exp", "mask_ready", "den_mm", "gate_ready"))
        zero_ready, slots_zeroed = sem("zero_ready"), sem("slots_zeroed")
        onehot_ready, rank_mm, slots_ready, scattered, over_ready = (sem(n) for n in (
            "onehot_ready", "rank_mm", "slots_ready", "scattered", "over_ready"))
        units_done, gathered = sem("units_done"), [sem(f"gathered{t}") for t in range(NT)]
        unit_w = [sem(f"unit_w{i}") for i in range(MOE_BUFS)]
        unit_x, unit_tr, unit_xT, unit_up, unit_hid, unit_down, unit_y = (sem(n) for n in (
            "unit_x", "unit_tr", "unit_xT", "unit_up", "unit_hid", "unit_down", "unit_y"))
        unit_st = [sem(f"unit_st{i}") for i in range(2)]
        over_w, over_tr, over_xT, over_up, over_hid, over_down, over_y, over_st = (sem(n) for n in (
            "over_w", "over_tr", "over_xT", "over_up", "over_hid", "over_down", "over_y", "over_st"))
        glu_ld, glu_mm, glu_silu, glu_h, glu_out_ld = sem("glu_ld"), sem("glu_mm"), sem("glu_silu"), sem("glu_h"), sem("glu_out_ld")
        h1_ld = [sem(f"h1_ld{i}") for i in range(2)]
        h1_mm, h1_act = sem("h1_mm"), sem("h1_act")
        fin_ld, mix_ready, rk_mm, rk_act, rk_sq, fv_mm, rv_ready = (sem(n) for n in (
            "fin_ld", "mix_ready", "rk_mm", "rk_act", "rk_sq", "fv_mm", "rv_ready"))
        stored = sem("stored")
        var_ready, rstd_ready = sem("var_ready"), sem("rstd_ready")

        r = Region()
        a_wkv = {l: r.take([DC, 2 * ATT[l][0] * ATT[l][1]]) for l in ATT}
        a_bk = {l: r.take([max(1, ATT[l][0] * ATT[l][1] // P)]) for l in (2, 3)}
        a_bv = {l: r.take([ATT[l][0] * ATT[l][1]]) for l in (2, 3)}
        a_pf = [r.take([CH]) for _ in range(2)]
        a_pr = [r.take([CH]) for _ in range(2)]
        a_ph = [[r.take([CH], BF16) for _ in range(3)] for _ in range(2)]
        l0_from = r.at
        a_w0kv = r.take([DC, 2 * D])
        a_bkv = r.take([2 * D])
        a_w0q = r.take([DC, D])
        a_woff = r.take([DC, HK])
        a_boff = r.take([HK])
        a_bq0 = r.take([D])
        a_bq0T = r.take([DC])
        a_kv0 = [r.take([2 * D]) for _ in range(4)]
        a_q0 = r.take([NT, D])
        a_qT0 = r.take([DC, T])
        a_u = r.take([NT, HK])
        a_t = r.take([NT, HK])
        a_sc = r.take([NT, HK])
        a_small = r.take([256])
        a_mx, a_sm = r.take([NT * H0]), r.take([NT * H0])
        a_loc, a_pos, a_msum = r.take([NT]), r.take([NT, WIN]), r.take([B])
        a_rlen = r.take([B])
        a_cov, a_gpos, a_gwrap = r.take([4]), r.take([WIN]), r.take([WIN])
        ctx0 = xn
        end_l0 = r.at
        r2 = Region(end_l0)
        a_win = [r2.take([WIN, D]) for _ in range(2)]
        a_prod = [r2.take([WIN, D]) for _ in range(2)]
        a_W = r2.take([NT, HK, WIN])
        a_S = r2.take([WIN, H0])
        a_A = [r2.take([H0, WIN]) for _ in range(2)]
        a_tmp = r2.take([HK, WIN])
        a_gW = r2.take([HK, WIN])
        gwin = xnT[:, :, :].rearrange("p c t -> p (c t)").rearrange("p (j e) -> p j e", j=WIN)
        a_mask = a_prod[0]
        a_iref = a_W[:, 0].rearrange("p a j -> p (a j)").bitcast(I32)
        a_ref = a_W[:, 1].rearrange("p a j -> p (a j)")
        a_ipos = a_W[:, 2].rearrange("p a j -> p (a j)")[:, 0:NT * WIN + NT].bitcast(I32)
        a_wrap = a_W[:, 3].rearrange("p a j -> p (a j)")
        flag_i = sb("flag_i", [1, 1], I32)

        r = Region()
        Kc = [r.take([HG, M], BF16) for _ in range(3)]
        Qc = [r.take([HG, S], BF16) for _ in range(3)]
        prob = [r.take([HG, S]) for _ in range(3)]
        mxh = [r.take([HG * QT, 2]) for _ in range(2)]
        mxg = [r.take([HG * QT]) for _ in range(2)]
        shp = [[r.take([P], BF16) for _ in range(SHIFT_ROWS)] for _ in range(2)]
        pvs = xnT[:, 1, 0:CH]
        rsum = r.take([QT, HG])
        qf = [r.take([CH]) for _ in range(2)]
        qr = [r.take([CH]) for _ in range(2)]
        qph = [[r.take([CH], BF16) for _ in range(3)] for _ in range(2)]
        after_att = r.at
        i8w = r.take([DC, D])
        r = Region(after_att)
        mw1 = [r.take([DC, F_MOE]) for _ in range(MOE_BUFS)]
        mw2 = [r.take([FM, D]) for _ in range(MOE_BUFS)]
        r = Region()
        unit_in = r.take([E_MOE, 2, D])
        unit_inT = [r.take([DC, CAP]) for _ in range(2)]
        hid = [r.take([FM, CAP]) for _ in range(2)]
        unit_out = [r.take([2, D]) for _ in range(2)]
        wg, bg = r.take([DC, E_MOE]), r.take([E_MOE])
        lgs, lge, mskd, gate, pick = (r.take([NT, E_MOE]) for _ in range(5))
        lgm, lgz, idx2 = r.take([NT, 1]), r.take([NT, 1]), r.take([NT, 1])
        gate_tok, rank_tok, base_tok, over_tok, is_over = (r.take([NT]) for _ in range(5))
        first_best, den, unit_base, over_base, over_end, over_n, counts = (r.take([E_MOE]) for _ in range(7))
        over_cmp, over_f = r.take([OVER, E_MOE]), r.take([OVER + 1])
        slot_i = r.take([NT], I32)
        over_i = r.take([OVER + 1], I32)
        assert r.at <= after_att
        r = Region()
        gw1, gw2 = r.take([DC, F_GLU]), r.take([DC, F_GLU])
        gh = [r.take([F_GLU // P, F_GLU]) for _ in range(2)]
        ha, hb = r.take([F_GLU // P, CH]), r.take([F_GLU // P, CH])
        gw3 = vaug[1][:].rearrange("p t h e -> p (t h e)")[:, 0:F_GLU // P * D].rearrange("p (f d) -> p f d", d=D)
        gsc = r.take([4, F_GLU // P])
        gs3 = r.take([D])
        gtmp = [ctxT[:, 0, 0:CH], ctxT[:, 0, CH:2 * CH]]
        r = Region()
        mwr, mwk, mwv = (r.take([DC, D]) for _ in range(3))
        mmu, mom = r.take([2, DC]), r.take([2, DC])
        xr, xk = r.take([DC, T]), r.take([DC, T])
        rv, kact = r.take([NT, D]), r.take([DC, T])

        def table_dmas(t):
            return sum(1 + (i % KT < QT) + (i % KT == KT - 1) for i in range(t % 4, t + 1, 4))

        r = Region(0)
        i8wq, i8wT = r.take([DC, D], BF16), r.take([DC, D], BF16)
        i8xq, i8xT = r.take([NT, D], BF16), r.take([DC, T], BF16)
        i8wr, i8xr = r.take([DC]), r.take([NT])
        i8wsc, i8xsc, i8sc_bc = r.take([DC]), r.take([NT]), r.take([D])

        block = ctx.enter_context(nc.Block())

        class Chain:
            def __init__(self, eng, s):
                self.eng, self.s, self.n = eng, s, 0

            def link(self, ins):
                self.n += 1
                ins.then_inc(self.s, 1)
                self.eng.wait_ge(self.s, self.n)

        def bc(ap, shape):
            return ap.to_broadcast(shape)

        @block.sync
        def _(sp):
            def ld(dst, src, s):
                sp.dma_start(dst, src).then_inc(s, 16)

            def rows(a):
                return a.rearrange("(c p) n -> p c n", p=P)

            def spread(a, n=P):
                return a.partition_broadcast(n)

            ld(a_w0kv, rows(io["w0kv"]), ld_w0)
            ld(a_bkv, spread(io["b0kv"]), ld_w0)
            for b in range(B):
                ld(ctxT[:, :, b * M:(b + 1) * M], rows(io["ctxT"])[:, :, b * M:(b + 1) * M], ld_ctx)
            ld(x[:], io["x"].rearrange("(t p) d -> p t d", p=P), ld_x)
            ld(a_w0q, rows(io["w0q"]), ld_small)
            ld(a_woff, rows(io["woff"]), ld_small)
            ld(a_boff, spread(io["boff"]), ld_small)
            ld(a_bq0, spread(io["b0q"]), ld_small)
            ld(a_bq0T, io["b0qT"], ld_small)
            ld(a_mask.rearrange("p a b -> p (a b)").bitcast(I32), spread(io["mask"].rearrange("b m -> (b m)")), ld_small)
            ld(gx[:], spread(io["g_xattn"]), ld_small)
            ld(gf[:], spread(io["g_ffn"]), ld_small)
            for l in ATT:
                ld(a_wkv[l], rows(io[f"wkv{l}"]), ld_prep)
            for l in (2, 3):
                e = ATT[l][0] * ATT[l][1]
                n = min(e, P)
                ld(a_bk[l][0:n, 0:e // n], io[f"bk{l}"], ld_prep)
                ld(a_bv[l][0:1, 0:e], io[f"bv{l}"].rearrange("(o n) -> o n", o=1), ld_prep)
            for t in range(NCT):
                b, i = t // KT, t % KT
                sp.wait_ge(kv0_ready, t + 1)
                src = a_kv0[t % 4]
                sp.dma_start(kv_table[b, BACK + i * P:BACK + (i + 1) * P, :], src).then_inc(table_written[t % 4], 16)
                if i < QT:
                    n = min(P, ROWS - (BACK + M + i * P))
                    sp.dma_start(kv_table[b, BACK + M + i * P:BACK + M + i * P + n, :], src[0:n]).then_inc(table_written[t % 4], 16)
                if i == KT - 1:
                    sp.dma_start(kv_table[b, 0:BACK, :], src[P - BACK:P]).then_inc(table_written[t % 4], 16)
            ld(wo0[:], rows(io["w0o"]), ld_late)
            ld(bo0[:], io["b0o"].rearrange("(o n) -> o n", o=1), ld_late)
            for l in ATT:
                e = ATT[l][0] * ATT[l][1]
                n = min(e, P)
                ld(w[l]["q"][:], rows(io[f"wq{l}"]), ld_late)
                ld(w[l]["o"][:], io[f"wo{l}"].rearrange("(c p) n -> p c n", p=n), ld_late)
                if l > 1:
                    ld(w[l]["bq"][:], io[f"bq{l}"], ld_late)
                    ld(w[l]["bo"][:], io[f"bo{l}"].rearrange("(o n) -> o n", o=1), ld_late)

            sp.wait_ge(zero_ready, 1)
            for slots in (slot_in, slot_out):
                sp.dma_start(slots.rearrange("(p a) d -> p (a d)", p=P).rearrange("p (k d) -> p k d", d=D // 2),
                             bc(zero_row[:].unsqueeze(1), [P, SLOT_ROWS // P * 2, D // 2])).then_inc(slots_zeroed, 16)

            for i in range(4):
                sp.wait_ge(table_written[i], 16 * table_dmas(NCT - 4 + i))
            sp.wait_ge(flag_ready, 1)
            uncovered = sp.value_load(flag_i[0:1, 0:1], min_val=0, max_val=1)

            def window(t, col, shift):
                b, i = t // QT, t % QT
                return bass.AP(tensor=kv_table.tensor, offset=kv_table.offset + (b * ROWS + i * P) * 2 * D + col * D + shift * WIN * 2 * D,
                               ap=[[2 * D, P], [2 * D, WIN], [1, D]])

            for t in range(NT):
                if t >= 2:
                    sp.wait_ge(prodK_ready, t - 1)
                sp.dma_start(a_win[t % 2], window(t, 0, 0)).then_inc(winK_ld[t % 2], 16)

            def general_windows(col, loop0):
                with sp.If(uncovered):
                    for t in range(NT):
                        with sp.Fori(1, M // WIN) as s:
                            sp.wait_ge(gen_used, s + (loop0 + t) * GEN_STEPS)
                            sp.dma_start(gwin, window(t, col, s)).then_inc(gen_ld, 16)

            general_windows(0, 0)
            for t in range(NT):
                if t < 2:
                    sp.wait_ge(prodK_ready, NT - 1 + t)
                else:
                    sp.wait_ge(prodV_ready, t - 1)
                sp.dma_start(a_win[t % 2], window(t, 1, 0)).then_inc(winV_ld[t % 2], 16)

            general_windows(1, NT)

            def group_rows(l, g, c):
                H, dh, _ = ATT[l]
                h0 = (g % (H // HG)) * HG
                return slice(SHIFT_ROWS + c * dh, SHIFT_ROWS + (c + 1) * dh), slice(h0 * dh, (h0 + HG) * dh), g // (H // HG)

            def keys_load(l, g):
                gi = GROUP0[l] + g
                sp.wait_ge(kq_zero, gi + 1)
                for c in range(NPAIRS[l]):
                    rr, heads, b = group_rows(l, g, c)
                    sp.dma_start(Kc[gi % 3][rr], kparts[l][PARTS_K[c], heads, b * M:(b + 1) * M].rearrange("(h d) t -> d h t", h=HG)).then_inc(kq_ld[gi % 3], 16)

            def queries_load(l, g):
                gi = GROUP0[l] + g
                for c in range(NPAIRS[l]):
                    rr, heads, b = group_rows(l, g, c)
                    sp.dma_start(Qc[gi % 3][rr], qparts[l][PARTS_Q[c], heads, b * S:(b + 1) * S].rearrange("(h d) t -> d h t", h=HG)).then_inc(kq_ld[gi % 3], 16)

            def shift_load(l, g):
                gi = GROUP0[l] + g
                sp.wait_ge(max_hi, gi + 1)
                sp.wait_ge(max_lo, gi + 1)
                for i in range(SHIFT_ROWS):
                    sp.dma_start(Qc[gi % 3][i:i + 1].rearrange("o h (q n) -> o (h q) n", n=P), shp[gi % 2][i][0:HG * QT, :]).then_inc(shift_ld[gi % 3], 16)

            def attention_loads(l):
                ng = NGROUPS[l]
                for i in range(2):
                    sp.wait_ge(prep_st[i], 16 * 3 * (PREP0[l + 1] // 2))
                for g in range(min(3, ng)):
                    keys_load(l, g)
                for i in range(2):
                    sp.wait_ge(qp_st[i], 16 * 3 * (QCH0[l + 1] // 2))
                for g in range(min(3, ng)):
                    queries_load(l, g)
                shift_load(l, 0)
                for g in range(ng):
                    if g + 1 < ng:
                        shift_load(l, g + 1)
                    if g + 3 < ng:
                        keys_load(l, g + 3)
                        queries_load(l, g + 3)

            def expert_load(e):
                i = e % MOE_BUFS
                ld(mw1[i], rows(io["w1"][e]), unit_w[i])
                ld(mw2[i], rows(io["w2"][e]), unit_w[i])

            def unit_rows(dram, n):
                return dram[n * CAP:(n + 1) * CAP, :].rearrange("(s p) d -> p s d", p=SUB)

            def moe_loads():
                sp.wait_ge(x_ready, 3 * NT)
                ld(wg, rows(io["wg"]), moe_small)
                ld(bg[0:1, :], io["bg"].rearrange("(o n) -> o n", o=1), moe_small)
                sp.wait_ge(slots_zeroed, 32)
                sp.wait_ge(scattered, 16 * NT)
                for e in range(E_MOE):
                    ld(unit_in[0:SUB, e], unit_rows(slot_in, e), unit_x)
                for e in range(E_MOE):
                    sp.wait_ge(unit_y, e + 1)
                    sp.dma_start(unit_rows(slot_out, e), unit_out[e % 2][0:SUB]).then_inc(unit_st[e % 2], 16)
                    if e + MOE_BUFS < E_MOE:
                        expert_load(e + MOE_BUFS)
                for i in range(2):
                    sp.wait_ge(unit_st[i], 16 * E_MOE // 2)
                sp.wait_ge(over_ready, 1)
                over = sp.value_load(over_i[0:1, OVER:OVER + 1], min_val=0, max_val=1)
                with sp.If(over):
                    for j in range(OVER):
                        if j:
                            sp.wait_ge(over_y, j)
                        e = sp.value_load(over_i[0:1, j:j + 1], min_val=0, max_val=E_MOE - 1)
                        sp.dma_start(mw1[0], io["w1"][bass.ds(e, 1)].rearrange("o (c p) n -> p (o c) n", p=P)).then_inc(over_w, 16)
                        sp.dma_start(mw2[0], io["w2"][bass.ds(e, 1)].rearrange("o (c p) n -> p (o c) n", p=P)).then_inc(over_w, 16)
                        sp.dma_start(unit_in[0:SUB, 0], unit_rows(slot_in, E_MOE + j)).then_inc(over_w, 16)
                        sp.wait_ge(over_y, j + 1)
                        sp.dma_start(unit_rows(slot_out, E_MOE + j), unit_out[0][0:SUB]).then_inc(over_st, 16)
                        sp.wait_ge(over_st, 16 * (j + 1))
                sp.sem_inc(units_done, 1)

            def glu_loads():
                sp.wait_ge(x_ready, 5 * NT)
                ld(gw1, rows(io["glu1"]), glu_ld)
                ld(gw2, rows(io["glu2"]), glu_ld)
                for i, n in enumerate(("s1", "s2", "sh1", "sh2")):
                    ld(gsc[:, i], io[n], glu_ld)
                ld(gs3, spread(io["s3"]), glu_ld)
                ld(gw3, rows(io["glu3"]), glu_ld)
                ld(gh[0], rows(io["gluh1"]), h1_ld[0])
                ld(gh[1], rows(io["gluh2"]), h1_ld[1])

            def mix_loads():
                sp.wait_ge(x_ready, 7 * NT)
                for dst, n in ((mwr, "w_r"), (mwk, "w_k"), (mwv, "w_v")):
                    ld(dst, rows(io[n]), fin_ld)
                ld(mmu[:, 0], io["mu_r"], fin_ld)
                ld(mmu[:, 1], io["mu_k"], fin_ld)

            sp.wait_ge(x_ready, NT)
            ld(i8w, io["i8rhsT"].rearrange("(c p) n -> p c n", p=P), i8_w)
            sp.wait_ge(x_ready, 2 * NT)
            for e in range(MOE_BUFS):
                expert_load(e)
            attention_loads(1)
            moe_loads()
            attention_loads(2)
            glu_loads()
            attention_loads(3)
            mix_loads()
            for t in range(NT):
                sp.wait_ge(x_ready, 8 * NT - NT + t + 1)
                sp.dma_start(io["out"][t * P:(t + 1) * P, :], x[:, t, :]).then_inc(stored, 16)
            sp.wait_ge(stored, 16 * NT)

        @block.gpsimd
        def _(pool):
            ch = Chain(pool, chain_pool)
            ch.link(pool.memset(ident[:], 0.0))
            ch.link(pool.affine_select(out=ident[:], in_=ident[:], compare_op=ALU.not_equal, fill=1.0, base=0,
                                       pattern=[[-1, P]], channel_multiplier=1))
            pool.tensor_copy(identb[:], ident[:]).then_inc(consts_ready, 1)
            pool.memset(onesf[:], 1.0).then_inc(consts_ready, 1)
            pool.iota(a_iref, pattern=[[0, NT * H0], [1, NK]], base=LEFT, channel_multiplier=0).then_inc(consts_ready, 1)
            pool.iota(a_ipos[:, 0:NT * WIN], pattern=[[0, B], [P, QT], [1, WIN]], base=-BACK, channel_multiplier=1).then_inc(consts_ready, 1)
            pool.iota(a_ipos[:, NT * WIN:], pattern=[[0, B], [P, QT]], base=0, channel_multiplier=1).then_inc(consts_ready, 1)
            for l in ATT:
                pool.memset(vaug[l][:].rearrange("p t h e -> p (t h) e")[:, :, ATT[l][1]], 1.0).then_inc(ones_rows, 1)

            def inverse_deviation(stage):
                pool.wait_ge(var_ready, stage + 1)
                ch.link(pool.tensor_scalar(rstd[:], mv[:, :, 1], EPS_LN, None, ALU.add))
                pool.tensor_tensor(rstd[:], rstd[:], minus_half[:], ALU.pow).then_inc(rstd_ready, 1)

            pool.memset(zero_row[:], 0.0).then_inc(zero_ready, 1)
            pool.wait_ge(consts_ready, 5)
            pool.affine_select(out=before[:], in_=onesf[:], compare_op=ALU.is_gt, fill=0.0, base=0,
                               pattern=[[1, P]], channel_multiplier=-1).then_inc(consts_ready, 1)
            ch.link(pool.memset(minus_half[:], -0.5))
            inverse_deviation(0)

            def split_k(k):
                l = next(i for i in ATT if PREP0[i] <= k < PREP0[i + 1])
                n = min(P, EW[l])
                kf, kr, (hi, mid, lo) = a_pf[k % 2], a_pr[k % 2], a_ph[k % 2]
                pool.wait_ge(prep_hi, k + 1)
                ch.link(pool.tensor_tensor(kr[0:n], kf[0:n], hi[0:n], ALU.subtract))
                ch.link(pool.tensor_copy(mid[0:n], kr[0:n]))
                pool.tensor_tensor(lo[0:n], kr[0:n], mid[0:n], ALU.subtract).then_inc(prep_split, 1)

            for k in range(8):
                split_k(k)
            for t in range(NT):
                pool.wait_ge(winK_ld[t % 2], 16 * (t // 2 + 1))
                if t == 0:
                    pool.wait_ge(q0_ready, NT)
                if t >= 2:
                    pool.wait_ge(prodK_used, t - 1)
                pool.tensor_tensor(a_prod[t % 2], a_win[t % 2], bc(a_q0[:, t, :].unsqueeze(1), [P, WIN, D]), ALU.mult).then_inc(prodK_ready, 1)
            for k in range(8, PREP0[4]):
                split_k(k)
            for t in range(NT):
                pool.wait_ge(winV_ld[t % 2], 16 * (t // 2 + 1))
                pool.wait_ge(attw_ready, t + 1)
                pool.wait_ge(prodV_used, t - 1) if t >= 2 else pool.wait_ge(prodK_used, NT)
                pool.tensor_tensor(a_prod[t % 2].rearrange("p j (h d) -> p j h d", h=H0), a_win[t % 2].rearrange("p j (h d) -> p j h d", h=H0),
                                   bc(a_A[t % 2].rearrange("p h j -> p j h").unsqueeze(3), [P, WIN, H0, HD0]), ALU.mult).then_inc(prodV_ready, 1)

            def shift_rows(l):
                for g in range(NGROUPS[l]):
                    gi = GROUP0[l] + g
                    if g == 0:
                        pool.wait_ge(x_ready, 2 * l * NT)
                        if l == 1:
                            for i in range(2):
                                pool.wait_ge(prep_st[i], 16 * 3 * (PREP0[4] // 2))
                    if g >= 3:
                        pool.wait_ge(st_mm, 2 * KT * (gi - 2))
                    if g < 3:
                        if SHIFT_ROWS + NPAIRS[l] * ATT[l][1] < MIN_ROWS:
                            pool.memset(Qc[gi % 3][0:MIN_ROWS], 0.0)
                            ch.link(pool.memset(Kc[gi % 3][0:MIN_ROWS], 0.0))
                        ch.link(pool.memset(Kc[gi % 3][0:SHIFT_ROWS], 1.0))
                    pool.memset(Qc[gi % 3][0:SHIFT_ROWS], 0.0).then_inc(kq_zero, 1)

            inverse_deviation(1)
            for l in ATT:
                inverse_deviation(2 * l)
                shift_rows(l)
                inverse_deviation(2 * l + 1)
                if l == 1:
                    pool.wait_ge(slots_zeroed, 32)
                    pool.wait_ge(xn_ready, XN0[3] + NT)
                    pool.wait_ge(slots_ready, 1)
                    for t in range(NT):
                        pool.indirect_dma_start(slot_in, bass.IndirectOffsetOnAxis(slot_i[:, t:t + 1], 0), xn[:, t, :], None).then_inc(scattered, 16)
                    pool.wait_ge(units_done, 1)
                    for t in range(NT):
                        pool.indirect_dma_start(xn[:, t, :], None, slot_out, bass.IndirectOffsetOnAxis(slot_i[:, t:t + 1], 0)).then_inc(gathered[t], 16)

        @block.scalar
        def _(act):
            ch = Chain(act, chain_act)
            act.wait_ge(ld_small, 16 * 8)
            act.activation(tgx[:], gx[:], ACT.Tanh).then_inc(tanh_ready, 1)
            act.activation(tgf[:], gf[:], ACT.Tanh).then_inc(tanh_ready, 1)

            def transposed(ready, first, n, src_banks, done, count0, rows=P):
                pass

            def ln_evac(stage):
                for i in range(4):
                    c, h = i % 2, i // 2
                    act.wait_ge(xnT_mm, LN_AT[stage] * 4 + i + 1)
                    act.activation(xnT[:, c, h * CH:(h + 1) * CH], bank[i], ACT.Copy).then_inc(xnT_ready, 1)

            def ctx_evac(l, width):
                n, ec = min(P, width), max(1, width // P)
                for i in range(2 * ec):
                    c, h = i % ec, i // ec
                    act.wait_ge(ctxT_mm, CTX_BANKS0[l] + i + 1)
                    act.activation(xnT[0:n, c, h * CH:(h + 1) * CH], bank[i][0:n, :], ACT.Copy).then_inc(ctxT_ready, 1)

            ln_evac(0)
            for c in range(DC):
                for h in range(2):
                    act.wait_ge(qT0_mm, 2 * c + h + 1)
                    act.activation(a_qT0[:, c, h * CH:(h + 1) * CH], bank[h], ACT.Identity, bias=a_bq0T[:, c:c + 1]).then_inc(qT0_ready, 1)

            act.wait_ge(ld_prep, 16 * 7)
            n_mm = 0

            def store_parts(k):
                l = next(i for i in ATT if PREP0[i] <= k < PREP0[i + 1])
                n, j = min(P, EW[l]), k - PREP0[l]
                c, q = j // (CT // CH), j % (CT // CH)
                act.wait_ge(prep_split, k + 1)
                for i in range(3):
                    act.dma_start(kparts[l][i, c * P:c * P + n, q * CH:(q + 1) * CH], a_ph[k % 2][i][0:n]).then_inc(prep_st[k % 2], 16)

            for l in ATT:
                n = min(P, EW[l])
                for j in range(PREP0[l + 1] - PREP0[l]):
                    k = PREP0[l] + j
                    c = j // (CT // CH)
                    act.wait_ge(prep_mm, n_mm + 1)
                    if k >= 2:
                        act.wait_ge(prep_split, k - 1)
                        act.wait_ge(prep_st[k % 2], 16 * 3 * (k // 2))
                    src, dst = bank[6 + n_mm % 2][0:n, :], a_pf[k % 2][0:n]
                    if l == 1:
                        ins = act.activation(dst, src, ACT.Copy)
                    else:
                        ins = act.activation(dst, src, ACT.Identity, bias=a_bk[l][0:n, c:c + 1])
                    n_mm += 1
                    ins.then_inc(prep_evac, 1)
                    act.wait_ge(prep_evac, n_mm)
                    act.activation(a_ph[k % 2][0][0:n], dst, ACT.Copy).then_inc(prep_hi, 1)
                    if k >= 1:
                        store_parts(k - 1)
                for t in range(NCT):
                    act.wait_ge(prep_mm, n_mm + 1)
                    act.activation(vaug[l][:, t, :, 0:ATT[l][1]], bank[6 + n_mm % 2][:, 0:EW[l]].rearrange("p (h d) -> p h d", h=ATT[l][0]),
                                   ACT.Copy).then_inc(prep_evac, 1)
                    n_mm += 1
            store_parts(PREP0[4] - 1)

            act.wait_ge(sub0_ready, 1)
            act.activation(a_sc[:], a_sc[:], ACT.Exp, scale=0.5 * HD0 ** -0.5).then_inc(exp0_ready, 1)
            ctx_evac(0, D)

            act.wait_ge(i8_wq, 1)

            def i8_evac():
                for i in range(DC):
                    act.wait_ge(i8_tr, i + 1)
                    act.activation(i8wT[:, i, :], bank[i][:, 0:D // 2].bitcast(BF16), ACT.Copy).then_inc(i8_qT, 1)
                act.wait_ge(i8_bc, 1)
                act.activation(i8sc_bc, bank[4][:, 0:D], ACT.Copy).then_inc(i8_qT, 1)
                for i in range(4):
                    c, h = i % 2, i // 2
                    act.wait_ge(i8_tr, DC + i + 1)
                    act.activation(i8xT[:, c, h * CH:(h + 1) * CH], bank[i][:, 0:CH // 2].bitcast(BF16), ACT.Copy).then_inc(i8_qT, 1)

            i8_evac()

            def q_store(l, k):
                n, j = min(P, EW[l]), k - QCH0[l]
                c, q = j // 2, j % 2
                act.wait_ge(qp_split, k + 1)
                for i in range(3):
                    act.dma_start(qparts[l][i, c * P:c * P + n, q * CH:(q + 1) * CH], qph[k % 2][i][0:n]).then_inc(qp_st[k % 2], 16)

            def attention(l):
                H, dh, scale = ATT[l]
                n = min(P, EW[l])
                for j in range(QCH0[l + 1] - QCH0[l]):
                    k = QCH0[l] + j
                    act.wait_ge(qp_mm, k + 1)
                    if k >= 2:
                        act.wait_ge(qp_split, k - 1)
                        act.wait_ge(qp_st[k % 2], 16 * 3 * (k // 2))
                    if l == 1:
                        ins = act.activation(qf[k % 2][0:n], bank[4 + k % 2][0:n], ACT.Copy)
                    else:
                        ins = act.activation(qf[k % 2][0:n], bank[4 + k % 2][0:n], ACT.Identity, bias=w[l]["bq"][:, j // 2:j // 2 + 1])
                    ch.link(ins)
                    act.activation(qph[k % 2][0][0:n], qf[k % 2][0:n], ACT.Copy).then_inc(qp_evac, 1)
                    if j >= 1:
                        q_store(l, k - 1)
                q_store(l, QCH0[l + 1] - 1)

                for step in schedule(l):
                    if step[0] == "turn":
                        _, g, place = step
                        gi = GROUP0[l] + g
                        act.wait_ge(max_tr, gi + 1)
                        if gi >= 2:
                            act.wait_ge(shift_ld[(gi - 2) % 3], 16 * SHIFT_ROWS * ((gi - 2) // 3 + 1))
                        act.activation(shp[gi % 2][0][0:HG * QT, :], bank[TURN_BANKS[place % 3]][0:HG * QT, 0:P], ACT.Copy, scale=-1.0).then_inc(max_hi, 1)
                    elif step[0] == "score":
                        _, g, kt, pair = step
                        sl = (GROUP0[l] + g) * KT + kt
                        if sl >= 3:
                            act.wait_ge(pv_mm, sl - 2)
                        act.wait_ge(st_mm, 2 * sl + pair + 1)
                        act.activation(prob[sl % 3][:, 2 * pair:2 * pair + 2, :], st_bank[pair][:], ACT.Exp, scale=scale).then_inc(exp_ready, 1)
                    elif step[0] == "copy":
                        gi = GROUP0[l] + step[1]
                        act.wait_ge(pv_mm, KT * (gi + 1))
                        if gi:
                            act.wait_ge(pv_tr, gi)
                        act.activation(pvs, bank[7], ACT.Copy).then_inc(pv_evac, 1)
                ctx_evac(l, EW[l])

            ln_evac(2)
            attention(1)

            ln_evac(3)
            act.wait_ge(lg_exp_in, 1)
            act.activation(lge, lgs, ACT.Exp).then_inc(lg_exp, 1)
            ups = FM // UP_PER_BANK

            def hidden(n, up, ready, down):
                for i in range(ups):
                    act.wait_ge(up, n * ups + i + 1)
                    if n >= 2 and i == 0:
                        act.wait_ge(down, 2 * (n - 1))
                    act.activation(hid[n % 2][:, i * UP_PER_BANK:(i + 1) * UP_PER_BANK, :],
                                   bank[i % 4][:, 0:UP_PER_BANK * CAP].rearrange("p (f s) -> p f s", s=CAP), ACT.Relu).then_inc(ready, 1)

            for e in range(E_MOE):
                hidden(e, unit_up, unit_hid, unit_down)
            act.wait_ge(over_ready, 1)
            over = act.value_load(over_i[0:1, OVER:OVER + 1], min_val=0, max_val=1)
            with act.If(over):
                for j in range(OVER):
                    hidden(j, over_up, over_hid, over_down)

            ln_evac(4)
            attention(2)

            ln_evac(5)
            for h in range(2):
                for f in range(F_GLU // P):
                    n = h * (F_GLU // P) + f
                    act.wait_ge(glu_mm, 2 * n + 1)
                    if n >= 2:
                        act.wait_ge(glu_h, n - 1)
                    act.activation(gtmp[n % 2], bank[n % 2], ACT.Silu, scale=gsc[:, 0, f:f + 1]).then_inc(glu_silu, 1)
                for i, dst in enumerate((hb, ha)):
                    for f in range(F_GLU // P):
                        n = (h * 2 + i) * (F_GLU // P) + f
                        act.wait_ge(h1_mm, n + 1)
                        act.activation(dst[:, f, :], bank[4 + n % 2], ACT.Gelu, scale=gsc[:, 2 + i, f:f + 1]).then_inc(h1_act, 1)

            ln_evac(6)
            attention(3)

            ln_evac(7)
            for t in range(NT):
                act.wait_ge(rk_mm, t + 1)
                act.activation(rv[:, t, :], bank[t % 2][:, 0:D], ACT.Sigmoid).then_inc(rk_act, 1)
            for i in range(2 * DC):
                c, h = i // 2, i % 2
                act.wait_ge(rk_mm, NT + i + 1)
                act.activation(kact[:, c, h * CH:(h + 1) * CH], bank[2 + i % 2], ACT.Relu).then_inc(rk_act, 1)

        @block.tensor
        def _(pe):
            def transposes(src, dst_sem, base, width, ready, ready0):
                n, ec = min(P, width), max(1, width // P)
                for t in range(NT):
                    if ready is not None:
                        pe.wait_ge(ready, ready0 + t + 1)
                    for c in range(ec):
                        ins = pe.transpose(bank[(t // QT) * ec + c][0:n, (t % QT) * P:(t % QT + 1) * P], src[:, t, c * P:c * P + n], ident[:])
                        if t % QT == QT - 1:
                            ins.then_inc(dst_sem, 1)

            def project_out(stage, wmat, width, bias, l):
                n, ec = min(P, width), max(1, width // P)
                for t in range(NT):
                    if t % QT == 0:
                        pe.wait_ge(ctxT_ready, CTX_BANKS0[l] + (t // QT + 1) * ec)
                    if t >= 2:
                        pe.wait_ge(x_ready, stage * NT + t - 1)
                    o = bank[4 + t % 2][:, 0:D]
                    for c in range(ec):
                        ins = pe.matmul(o, xnT[0:n, c, t * P:(t + 1) * P], wmat[:, c, :], start=(c == 0), stop=(c == ec - 1 and bias is None))
                    if bias is not None:
                        ins = pe.matmul(o, onesf[0:1, :], bias, start=False, stop=True)
                    ins.then_inc(out_mm, 1)

            pe.wait_ge(ld_w0, 32)
            pe.wait_ge(ld_ctx, 32)
            for t in range(NCT):
                if t >= 2:
                    pe.wait_ge(kv0_ready, t - 1)
                for c in range(DC):
                    ins = pe.matmul(bank[4 + t % 2], ctxT[:, c, t * P:(t + 1) * P], a_w0kv[:, c, :], start=(c == 0), stop=(c == DC - 1))
                ins.then_inc(kv0_mm, 1)
            pe.wait_ge(consts_ready, 2)
            transposes(xn, xnT_mm, 0, D, xn_ready, 0)
            pe.wait_ge(ld_small, 16 * 8)
            pe.wait_ge(xnT_ready, 4)
            for c in range(DC):
                for h in range(2):
                    if c:
                        pe.wait_ge(qT0_ready, h + 1)
                    for i in range(DC):
                        ins = pe.matmul(bank[h], a_w0q[:, i, c * P:(c + 1) * P], xnT[:, i, h * CH:(h + 1) * CH], start=(i == 0), stop=(i == DC - 1))
                    ins.then_inc(qT0_mm, 1)
            pe.wait_ge(kv0_ready, NCT)
            for t in range(NT):
                if t >= 2:
                    pe.wait_ge(q0_ready, t - 1)
                for i in range(DC):
                    ins = pe.matmul(bank[4 + t % 2][:, 0:D], xnT[:, i, t * P:(t + 1) * P], a_w0q[:, i, :], start=(i == 0), stop=(i == DC - 1))
                ins.then_inc(q0_mm, 1)
            pe.wait_ge(qT0_ready, 4)
            for t in range(NT):
                o = bank[2 + t // QT][:, (t % QT) * HK:(t % QT + 1) * HK]
                for i in range(DC):
                    ins = pe.matmul(o, a_qT0[:, i, t * P:(t + 1) * P], a_woff[:, i, :], start=(i == 0), stop=(i == DC - 1))
                ins.then_inc(off_mm, 1)

            pe.wait_ge(cov_ready, 1)
            pe.matmul(bank[0][0:1, 0:1], onesf[:, 0:1], a_cov[:, 0:1], start=True, stop=True).then_inc(cov_mm, 1)

            n_mm = 0
            pe.wait_ge(ld_prep, 16 * 7)
            for l in ATT:
                n = min(P, EW[l])
                for j in range(PREP0[l + 1] - PREP0[l]):
                    c, q = j // (CT // CH), j % (CT // CH)
                    if n_mm >= 2:
                        pe.wait_ge(prep_evac, n_mm - 1)
                    for i in range(DC):
                        ins = pe.matmul(bank[6 + n_mm % 2][0:n, :], a_wkv[l][:, i, c * P:c * P + n], ctxT[:, i, q * CH:(q + 1) * CH], start=(i == 0), stop=(i == DC - 1))
                    ins.then_inc(prep_mm, 1)
                    n_mm += 1
                for t in range(NCT):
                    if n_mm >= 2:
                        pe.wait_ge(prep_evac, n_mm - 1)
                    o = bank[6 + n_mm % 2][:, 0:EW[l]]
                    for i in range(DC):
                        ins = pe.matmul(o, ctxT[:, i, t * P:(t + 1) * P], a_wkv[l][:, i, EW[l]:2 * EW[l]], start=(i == 0), stop=(i == DC - 1 and l == 1))
                    if l > 1:
                        ins = pe.matmul(o, onesf[0:1, :], a_bv[l][0:1, 0:EW[l]], start=False, stop=True)
                    ins.then_inc(prep_mm, 1)
                    n_mm += 1

            pe.wait_ge(ld_late, 16 * LATE_LOADS)
            transposes(ctx0, ctxT_mm, 0, D, ctxn_ready, 0)
            project_out(0, wo0, D, bo0[:], 0)

            pe.wait_ge(i8_wq, 1)
            for c in range(DC):
                for i in range(DC):
                    ins = pe.transpose(bank[c][:, 0:D // 2].bitcast(BF16)[:, i * P:(i + 1) * P], i8wq[:, i, c * P:(c + 1) * P], identb[:])
                ins.then_inc(i8_tr, 1)
            pe.wait_ge(x_ready, NT)
            for i in range(DC):
                ins = pe.matmul(bank[4][:, i * P:(i + 1) * P], bc(i8wsc[:, i:i + 1], [P, P]), ident[:], start=True, stop=True)
            ins.then_inc(i8_bc, 1)
            for t in range(NT):
                pe.wait_ge(i8_xq, t + 1)
                if t == 0:
                    pe.wait_ge(i8_qT, DC)
                for c in range(DC):
                    ins = pe.transpose(bank[(t // QT) * DC + c][:, 0:CH // 2].bitcast(BF16)[:, (t % QT) * P:(t % QT + 1) * P], i8xq[:, t, c * P:(c + 1) * P], identb[:])
                    if t % QT == QT - 1:
                        ins.then_inc(i8_tr, 1)
            for t in range(NT):
                if t % QT == 0:
                    pe.wait_ge(i8_qT, DC + 1 + (t // QT + 1) * DC)
                if t >= 2:
                    pe.wait_ge(x_ready, NT + t - 1)
                for c in range(DC):
                    ins = pe.matmul(bank[4 + t % 2][:, 0:D], i8xT[:, c, t * P:(t + 1) * P], i8wT[:, c, :], start=(c == 0), stop=(c == DC - 1))
                ins.then_inc(out_mm, 1)

            def attention(l):
                H, dh, _ = ATT[l]
                R = max(MIN_ROWS, SHIFT_ROWS + NPAIRS[l] * dh)
                n = min(P, EW[l])
                stage = 2 * l
                pe.wait_ge(xnT_ready, (LN_AT[stage] + 1) * 4)
                for j in range(QCH0[l + 1] - QCH0[l]):
                    k = QCH0[l] + j
                    c, q = j // 2, j % 2
                    if j >= 2:
                        pe.wait_ge(qp_evac, k - 1)
                    for i in range(DC):
                        ins = pe.matmul(bank[4 + k % 2][0:n, :], w[l]["q"][:, i, c * P:c * P + n], xnT[:, i, q * CH:(q + 1) * CH], start=(i == 0), stop=(i == DC - 1))
                    ins.then_inc(qp_mm, 1)
                pe.wait_ge(qp_evac, QCH0[l + 1])

                order = schedule(l)
                rotation = [step for step in order if step[0] in ("max", "turn", "context")]

                def bank_read(place):
                    kind, what, _ = rotation[place - len(TURN_BANKS)]
                    if kind == "max":
                        return max_red, GROUP0[l] * HALVES + what + 1
                    return max_lo if kind == "turn" else norm_ready, GROUP0[l] + what + 1

                def row_max(u, place):
                    g, hh, qt, half = u // HALVES, u // (2 * QT) % HG, u // 2 % QT, u % 2
                    gi = GROUP0[l] + g
                    if u % HALVES == 0:
                        pe.wait_ge(kq_ld[gi % 3], keys_and_queries(gi))
                    if place >= len(TURN_BANKS):
                        pe.wait_ge(*bank_read(place))
                    pe.matmul(bank[TURN_BANKS[place % 3]], Qc[gi % 3][0:R, hh, qt * P:(qt + 1) * P], Kc[gi % 3][0:R, hh, half * CH:(half + 1) * CH],
                              start=True, stop=True).then_inc(max_mm, 1)

                def turn_max(g, place):
                    gi = GROUP0[l] + g
                    pe.wait_ge(max_fin, gi + 1)
                    pe.wait_ge(*bank_read(place))
                    pe.transpose(bank[TURN_BANKS[place % 3]][0:HG * QT, 0:P], mxg[gi % 2], ident[:]).then_inc(max_tr, 1)

                def score(g, kt, pair):
                    gi = GROUP0[l] + g
                    sl = gi * KT + kt
                    if kt == 0 and pair == 0:
                        pe.wait_ge(shift_ld[gi % 3], 16 * SHIFT_ROWS * (gi // 3 + 1))
                    if sl >= 1:
                        pe.wait_ge(exp_ready, 2 * (sl - 1) + pair + 1)
                    for i in range(2):
                        hh = 2 * pair + i
                        ins = pe.matmul(st_bank[pair][:, i, :], Kc[gi % 3][0:R, hh, kt * P:(kt + 1) * P], Qc[gi % 3][0:R, hh, :], start=True, stop=True)
                    ins.then_inc(st_mm, 1)

                def values(g, kt):
                    gi = GROUP0[l] + g
                    sl = gi * KT + kt
                    b, h0 = g // (H // HG), (g % (H // HG)) * HG
                    pe.wait_ge(exp_ready, 2 * sl + 2)
                    if kt == 0:
                        pe.wait_ge(pv_evac, gi) if g else pe.wait_ge(pv_done, l)
                    for hh in range(HG):
                        ins = pe.matmul(bank[7][32 * hh:32 * hh + dh + 1, :], vaug[l][:, b * KT + kt, h0 + hh, :], prob[sl % 3][:, hh, :],
                                        start=(kt == 0), stop=(kt == KT - 1))
                    ins.then_inc(pv_mm, 1)

                def turn_context(g, place):
                    pe.wait_ge(pv_evac, GROUP0[l] + g + 1)
                    pe.wait_ge(*bank_read(place))
                    for qt in range(QT):
                        ins = pe.transpose(bank[TURN_BANKS[place % 3]][:, qt * P:(qt + 1) * P], pvs[:, qt * P:(qt + 1) * P], ident[:])
                    ins.then_inc(pv_tr, 1)

                if l == 1:
                    pe.wait_ge(prep_evac, PREP_MM)
                for step in order:
                    if step[0] == "max":
                        row_max(*step[1:])
                    elif step[0] == "turn":
                        turn_max(*step[1:])
                    elif step[0] == "score":
                        score(*step[1:])
                    elif step[0] == "values":
                        values(*step[1:])
                    elif step[0] == "context":
                        turn_context(*step[1:])
                pe.wait_ge(norm_ready, GROUP0[l + 1])
                transposes(xn, ctxT_mm, 0, EW[l], None, 0)
                project_out(stage, w[l]["o"], EW[l], w[l]["bo"][:] if w[l]["bo"] is not None else None, l)

            def ln_transposes(stage):
                transposes(xn, xnT_mm, 0, D, xn_ready, XN0[stage])

            ln_transposes(2)
            attention(1)

            ln_transposes(3)
            pe.wait_ge(xnT_ready, (LN_AT[3] + 1) * 4)
            pe.wait_ge(moe_small, 32)
            for t in range(NT):
                o = bank[6][:, t * E_MOE:(t + 1) * E_MOE]
                for i in range(DC):
                    pe.matmul(o, xnT[:, i, t * P:(t + 1) * P], wg[:, i, :], start=(i == 0), stop=False)
                ins = pe.matmul(o, onesf[0:1, :], bg[0:1, :], start=False, stop=True)
            ins.then_inc(lg_mm, 1)
            pe.wait_ge(onehot_ready, 1)
            pe.wait_ge(consts_ready, 6)
            pe.matmul(bank[7][:, 0:NT * E_MOE], before[:], lgs.rearrange("p t e -> p (t e)"), start=True, stop=False)
            for k in range(1, NT):
                pe.matmul(bank[7][:, k * E_MOE:NT * E_MOE], onesf[:], lgs[:, 0:NT - k].rearrange("p t e -> p (t e)"), start=False, stop=(k == NT - 1))
            for t in range(NT):
                ins = pe.matmul(bank[4][:, 0:E_MOE], onesf[:], lgs[:, t], start=(t == 0), stop=(t == NT - 1))
            ins.then_inc(rank_mm, 1)
            pe.wait_ge(mask_ready, 1)
            for t in range(NT):
                ins = pe.matmul(bank[5][:, 0:E_MOE], onesf[:], mskd[:, t, :], start=(t == 0), stop=(t == NT - 1))
            ins.then_inc(den_mm, 1)
            ups = FM // UP_PER_BANK

            def unit_transposes(n, src, done, read):
                if n >= 2:
                    pe.wait_ge(read, n - 1)
                for c in range(DC):
                    for i in range(2):
                        ins = pe.transpose(bank[6 + n % 2][:, c * CAP + i * SUB:c * CAP + (i + 1) * SUB], src[0:SUB, i, c * P:(c + 1) * P], ident[0:SUB, 0:SUB])
                ins.then_inc(done, 1)

            def unit_up_products(n, wbuf, up, ready, xT):
                pe.wait_ge(xT, n + 1)
                for f in range(FM):
                    i = f // UP_PER_BANK
                    if f % UP_PER_BANK == 0 and n:
                        pe.wait_ge(ready, (n - 1) * ups + i + 1)
                    for c in range(DC):
                        ins = pe.matmul(bank[i % 4][:, f % UP_PER_BANK * CAP:(f % UP_PER_BANK + 1) * CAP], mw1[wbuf][:, c, f * P:(f + 1) * P],
                                        unit_inT[n % 2][:, c, :], start=(c == 0), stop=(c == DC - 1))
                    if f % UP_PER_BANK == UP_PER_BANK - 1:
                        ins.then_inc(up, 1)

            def unit_down_products(n, wbuf, ready, down, y):
                pe.wait_ge(ready, (n + 1) * ups)
                if n >= 2:
                    pe.wait_ge(y, n - 1)
                for i in range(2):
                    for f in range(FM):
                        ins = pe.matmul(bank[4 + n % 2][0:SUB, i * D:(i + 1) * D], hid[n % 2][:, f, i * SUB:(i + 1) * SUB], mw2[wbuf][:, f, :],
                                        start=(f == 0), stop=(f == FM - 1))
                    ins.then_inc(down, 1)

            pe.wait_ge(slots_ready, 1)
            pe.wait_ge(gate_ready, 1)
            for e in range(E_MOE):
                if e == 0:
                    pe.wait_ge(unit_x, 16 * E_MOE)
                    unit_transposes(0, unit_in[:, 0], unit_tr, unit_xT)
                pe.wait_ge(unit_w[e % MOE_BUFS], 32 * (e // MOE_BUFS + 1))
                unit_up_products(e, e % MOE_BUFS, unit_up, unit_hid, unit_xT)
                if e + 1 < E_MOE:
                    unit_transposes(e + 1, unit_in[:, e + 1], unit_tr, unit_xT)
                unit_down_products(e, e % MOE_BUFS, unit_hid, unit_down, unit_y)
            pe.wait_ge(over_ready, 1)
            over = pe.value_load(over_i[0:1, OVER:OVER + 1], min_val=0, max_val=1)
            with pe.If(over):
                pe.wait_ge(unit_y, E_MOE)
                for j in range(OVER):
                    pe.wait_ge(over_w, 48 * (j + 1))
                    unit_transposes(j, unit_in[:, 0], over_tr, over_xT)
                    unit_up_products(j, 0, over_up, over_hid, over_xT)
                    unit_down_products(j, 0, over_hid, over_down, over_y)

            ln_transposes(4)
            attention(2)

            ln_transposes(5)
            pe.wait_ge(xnT_ready, (LN_AT[5] + 1) * 4)
            pe.wait_ge(glu_ld, 16 * 8)
            nf = F_GLU // P
            for h in range(2):
                for f in range(nf):
                    n = h * nf + f
                    if n >= 2:
                        pe.wait_ge(glu_h, n - 1)
                    for j, gw in enumerate((gw1, gw2)):
                        for i in range(DC):
                            ins = pe.matmul(bank[2 * j + n % 2], gw[:, i, f * P:(f + 1) * P], xnT[:, i, h * CH:(h + 1) * CH], start=(i == 0), stop=(i == DC - 1))
                        ins.then_inc(glu_mm, 1)
                pe.wait_ge(glu_h, (h + 1) * nf)
                for i, src in enumerate((ha, hb)):
                    if h == 0:
                        pe.wait_ge(h1_ld[i], 16)
                    if i:
                        pe.wait_ge(h1_act, (h * 2 + 1) * nf)
                    for f in range(nf):
                        n = (h * 2 + i) * nf + f
                        if n >= 2:
                            pe.wait_ge(h1_act, n - 1)
                        for j in range(nf):
                            ins = pe.matmul(bank[4 + n % 2], gh[i][:, j, f * P:(f + 1) * P], src[:, j, :], start=(j == 0), stop=(j == nf - 1))
                        ins.then_inc(h1_mm, 1)
                pe.wait_ge(h1_act, (h * 2 + 2) * nf)
                for q in range(QT):
                    t = h * QT + q
                    if t >= 2:
                        pe.wait_ge(x_ready, 5 * NT + t - 1)
                    for j in range(nf):
                        ins = pe.matmul(bank[6 + t % 2][:, 0:D], ha[:, j, q * P:(q + 1) * P], gw3[:, j, :], start=(j == 0), stop=(j == nf - 1))
                    ins.then_inc(out_mm, 1)

            ln_transposes(6)
            attention(3)

            ln_transposes(7)
            pe.wait_ge(fin_ld, 16 * 5)
            pe.wait_ge(mix_ready, 4)
            for t in range(NT):
                if t >= 2:
                    pe.wait_ge(rk_act, t - 1)
                for i in range(DC):
                    ins = pe.matmul(bank[t % 2][:, 0:D], xr[:, i, t * P:(t + 1) * P], mwr[:, i, :], start=(i == 0), stop=(i == DC - 1))
                ins.then_inc(rk_mm, 1)
            for j in range(2 * DC):
                c, h = j // 2, j % 2
                if j >= 2:
                    pe.wait_ge(rk_act, NT + j - 1)
                for i in range(DC):
                    ins = pe.matmul(bank[2 + j % 2], mwk[:, i, c * P:(c + 1) * P], xk[:, i, h * CH:(h + 1) * CH], start=(i == 0), stop=(i == DC - 1))
                ins.then_inc(rk_mm, 1)
            pe.wait_ge(rk_sq, 2 * DC)
            for t in range(NT):
                if t >= 2:
                    pe.wait_ge(rv_ready, t - 1)
                for i in range(DC):
                    ins = pe.matmul(bank[4 + t % 2][:, 0:D], kact[:, i, t * P:(t + 1) * P], mwv[:, i, :], start=(i == 0), stop=(i == DC - 1))
                ins.then_inc(fv_mm, 1)

        @block.vector
        def _(dve):
            ch = Chain(dve, chain_dve)

            def normalise(stage):
                if stage:
                    dve.wait_ge(x_ready, stage * NT)
                else:
                    dve.wait_ge(ld_x, 16)
                for t in range(NT):
                    ins = dve.bn_stats(bnst[:, t, :], x[:, t, :])
                ch.link(ins)
                for t in range(NT):
                    ins = dve.bn_aggr(mv[:, t, :], bnst[:, t, :])
                ins.then_inc(var_ready, 1)
                dve.wait_ge(var_ready, stage + 1)
                dve.wait_ge(rstd_ready, stage + 1)
                for t in range(NT):
                    dve.tensor_scalar(xn[:, t, :], x[:, t, :], mv[:, t, 0:1], rstd[:, t:t + 1], ALU.subtract, ALU.mult).then_inc(xn_ready, 1)

            def add_out(stage, tg, banks=4):
                for t in range(NT):
                    dve.wait_ge(out_mm, OUT_AT[stage] * NT + t + 1)
                    dve.scalar_tensor_tensor(x[:, t, :], bank[banks + t % 2][:, 0:D], tg, x[:, t, :], ALU.mult, ALU.add).then_inc(x_ready, 1)

            normalise(0)
            dve.wait_ge(ld_w0, 32)
            for t in range(NCT):
                dve.wait_ge(kv0_mm, t + 1)
                if t >= 4:
                    dve.wait_ge(table_written[t % 4], 16 * table_dmas(t - 4))
                dve.tensor_tensor(a_kv0[t % 4], bank[4 + t % 2], a_bkv, ALU.add).then_inc(kv0_ready, 1)
            dve.wait_ge(consts_ready, 5)
            dve.wait_ge(ld_small, 16 * 8)
            dve.tensor_copy(a_ref, a_iref)
            ch.link(dve.tensor_copy(a_pos.rearrange("p t j -> p (t j)"), a_ipos[:, 0:NT * WIN]))
            dve.tensor_scalar(a_wrap[:, 0:NT * WIN], a_pos.rearrange("p t j -> p (t j)"), 0.0, float(M), ALU.is_lt, ALU.mult)
            ch.link(dve.tensor_copy(a_loc, a_ipos[:, NT * WIN:]))
            ch.link(dve.tensor_tensor(a_pos.rearrange("p t j -> p (t j)"), a_pos.rearrange("p t j -> p (t j)"), a_wrap[:, 0:NT * WIN], ALU.add))
            mf = a_mask.rearrange("p j e -> p (j e)")
            ch.link(dve.tensor_scalar(mf, mf.bitcast(I32), -1.0, 1.0, ALU.mult, ALU.add))
            ch.link(dve.tensor_reduce(a_msum, mf.rearrange("p (b m) -> p b m", b=B), AX.X, ALU.add))
            ch.link(dve.tensor_scalar(a_msum, a_msum, -1.0, None, ALU.add))
            for t in range(NT):
                dve.wait_ge(q0_mm, t + 1)
                dve.tensor_tensor(a_q0[:, t, :], bank[4 + t % 2][:, 0:D], a_bq0, ALU.add).then_inc(q0_ready, 1)
            dve.wait_ge(off_mm, NT)
            u = a_u.rearrange("p t k -> p (t k)")
            tt = a_t.rearrange("p t k -> p (t k)")
            for b in range(B):
                ins = dve.tensor_tensor(a_u[:, b * QT:(b + 1) * QT, :], bank[2 + b][:, 0:QT * HK].rearrange("p (t k) -> p t k", t=QT),
                                        bc(a_boff.unsqueeze(1), [P, QT, HK]), ALU.add)
            ch.link(ins)
            ch.link(dve.tensor_tensor(u, u, a_ref, ALU.add))
            ch.link(dve.tensor_tensor(a_u, a_u, bc(a_loc.unsqueeze(2), [P, NT, HK]), ALU.add))
            half = QT * HK
            halves = [(b, slice(b * half, (b + 1) * half)) for b in range(B)]
            ch.link(dve.reciprocal(a_rlen, a_msum))
            for b, h in halves:
                ins = dve.tensor_scalar(tt[:, h], u[:, h], a_rlen[:, b:b + 1], MAGIC, ALU.mult, ALU.add)
            ch.link(ins)
            for b, h in halves:
                ins = dve.tensor_scalar(tt[:, h], tt[:, h], -MAGIC, a_msum[:, b:b + 1], ALU.add, ALU.mult)
            ch.link(ins)
            ch.link(dve.tensor_tensor(u, u, tt, ALU.subtract))
            for b, h in halves:
                ins = dve.tensor_scalar(tt[:, h], u[:, h], a_msum[:, b:b + 1], 0.0, ALU.mult, ALU.is_lt)
            ch.link(ins)
            for b, h in halves:
                ins = dve.scalar_tensor_tensor(u[:, h], tt[:, h], a_msum[:, b:b + 1], u[:, h], ALU.mult, ALU.add)
            ch.link(ins)
            ch.link(dve.tensor_scalar(u, u, 1.0 / float(M - 1), 2.0, ALU.mult, ALU.mult))
            ch.link(dve.tensor_scalar(u, u, -1.0, 1.0, ALU.add, ALU.add))
            ch.link(dve.tensor_scalar(u, u, float(M), -1.0, ALU.mult, ALU.add))
            ch.link(dve.tensor_scalar(u, u, 0.5, None, ALU.mult))
            ch.link(dve.tensor_tensor(a_t, a_u, bc(a_loc.unsqueeze(2), [P, NT, HK]), ALU.subtract))
            ch.link(dve.tensor_scalar(tt, tt, float(BACK), None, ALU.add))
            ch.link(dve.tensor_scalar(a_wrap, tt, float(M // 2), float(-M), ALU.is_ge, ALU.mult))
            ch.link(dve.tensor_tensor(tt, tt, a_wrap, ALU.add))
            ch.link(dve.tensor_scalar(a_wrap, tt, 0.0, None, ALU.is_ge))
            ch.link(dve.scalar_tensor_tensor(tt, tt, float(WIN - 1), a_wrap, ALU.is_le, ALU.mult))
            dve.tensor_reduce(a_cov[:, 0:1], tt, AX.X, ALU.add).then_inc(cov_ready, 1)
            dve.wait_ge(cov_mm, 1)
            dve.tensor_scalar(flag_i[:], bank[0][0:1, 0:1], float(P * NT * HK) - 0.5, None, ALU.is_lt).then_inc(flag_ready, 1)
            dve.wait_ge(flag_ready, 1)
            uncovered = dve.value_load(flag_i[0:1, 0:1], min_val=0, max_val=1)
            dve.wait_ge(cov_ready, 1)
            for t in range(NT):
                ins = dve.tensor_tensor(a_W[:, t], bc(a_u[:, t, :].unsqueeze(2), [P, HK, WIN]), bc(a_pos[:, t, :].unsqueeze(1), [P, HK, WIN]), ALU.subtract)
            ch.link(ins)
            Wf = a_W.rearrange("p t k j -> p (t k j)")
            ch.link(dve.scalar_tensor_tensor(Wf, Wf, -1.0, Wf, ALU.mult, ALU.min))
            ch.link(dve.tensor_scalar(Wf, Wf, 1.0, 0.0, ALU.add, ALU.max))

            def scores0(prod, S_out):
                return dve.tensor_reduce(S_out.rearrange("p h j -> p j h"), prod.rearrange("p j (h d) -> p j h d", h=H0), AX.X, ALU.add)

            def hkj(a):
                return a.rearrange("p (h k) j -> p h k j", h=H0)

            S_hj = a_S.rearrange("p j h -> p (j h)").rearrange("p (h j) -> p h j", h=H0)
            for t in range(NT):
                dve.wait_ge(prodK_ready, t + 1)
                ins = scores0(a_prod[t % 2], S_hj)
                ins.then_inc(prodK_used, 1)
                dve.wait_ge(prodK_used, t + 1)
                ch.link(dve.tensor_tensor(hkj(a_tmp), hkj(a_W[:, t]), bc(S_hj.unsqueeze(2), [P, H0, NK, WIN]), ALU.mult))
                ch.link(dve.tensor_reduce(a_sc[:, t, :], a_tmp, AX.X, ALU.add))

            gen_links = [0]

            def general(loop0, use):
                with dve.If(uncovered):
                    if loop0 == 0:
                        dve.sem_inc(gen_used, 1)
                    for t in range(NT):
                        def link(ins):
                            gen_links[0] += 1
                            ins.then_inc(gen_chain, 1)
                            dve.wait_ge(gen_chain, gen_links[0])

                        link(dve.tensor_copy(a_gpos, a_pos[:, t, :]))
                        first = gen_links[0]
                        with dve.Fori(1, M // WIN) as s:
                            done = [0]

                            def step(ins):
                                done[0] += 1
                                ins.then_inc(gen_chain, 1)
                                dve.wait_ge(gen_chain, (s - 1) * GEN_LINKS + (first + done[0]))

                            step(dve.tensor_scalar(a_gpos, a_gpos, float(WIN), None, ALU.add))
                            step(dve.tensor_scalar(a_gwrap, a_gpos, float(M), float(-M), ALU.is_ge, ALU.mult))
                            step(dve.tensor_tensor(a_gpos, a_gpos, a_gwrap, ALU.add))
                            step(dve.tensor_tensor(a_gW, bc(a_u[:, t, :].unsqueeze(2), [P, HK, WIN]), bc(a_gpos.unsqueeze(1), [P, HK, WIN]), ALU.subtract))
                            step(dve.scalar_tensor_tensor(a_gW, a_gW, -1.0, a_gW, ALU.mult, ALU.min))
                            step(dve.tensor_scalar(a_gW, a_gW, 1.0, 0.0, ALU.add, ALU.max))
                            use(t, step, lambda: dve.wait_ge(gen_ld, s * 16 + 16 * (loop0 + t) * GEN_STEPS),
                                lambda ins: (ins.then_inc(gen_used, 1), dve.wait_ge(gen_used, s + ((loop0 + t) * GEN_STEPS + 1))))
                            assert done[0] == GEN_LINKS, done
                        gen_links[0] += GEN_STEPS * GEN_LINKS

            def more_scores(t, step, loaded, used):
                loaded()
                step(dve.tensor_tensor(gwin, gwin, bc(a_q0[:, t, :].unsqueeze(1), [P, WIN, D]), ALU.mult))
                used(scores0(gwin, S_hj))
                step(dve.tensor_tensor(hkj(a_tmp), hkj(a_gW), bc(S_hj.unsqueeze(2), [P, H0, NK, WIN]), ALU.mult))
                step(dve.tensor_reduce(a_small[:, 0:HK], a_tmp, AX.X, ALU.add))
                step(dve.tensor_tensor(a_sc[:, t, :], a_sc[:, t, :], a_small[:, 0:HK], ALU.add))

            def more_context(t, step, loaded, used):
                step(dve.tensor_tensor(a_tmp, a_gW, bc(a_sc[:, t, :].unsqueeze(2), [P, HK, WIN]), ALU.mult))
                step(dve.tensor_reduce(a_A[0], a_tmp.rearrange("p (h k) j -> p h j k", h=H0), AX.X, ALU.add))
                loaded()
                step(dve.tensor_tensor(gwin.rearrange("p j (h d) -> p j h d", h=H0), gwin.rearrange("p j (h d) -> p j h d", h=H0),
                                       bc(a_A[0].rearrange("p h j -> p j h").unsqueeze(3), [P, WIN, H0, HD0]), ALU.mult))
                used(dve.tensor_reduce(a_small, gwin.rearrange("p j e -> p e j"), AX.X, ALU.add))
                step(dve.tensor_tensor(ctx0[:, t, :], ctx0[:, t, :], a_small, ALU.add))

            general(0, more_scores)
            sc = a_sc.rearrange("p t (h k) -> p (t h) k", h=H0)
            ch.link(dve.tensor_reduce(a_mx, sc, AX.X, ALU.max))
            dve.tensor_tensor(sc, sc, bc(a_mx.unsqueeze(2), [P, NT * H0, NK]), ALU.subtract).then_inc(sub0_ready, 1)
            dve.wait_ge(exp0_ready, 1)
            ch.link(dve.tensor_reduce(a_sm, sc, AX.X, ALU.add))
            ch.link(dve.reciprocal(a_sm, a_sm))
            ch.link(dve.scalar_tensor_tensor(sc, sc, 0.5, bc(a_sm.unsqueeze(2), [P, NT * H0, NK]), ALU.mult, ALU.mult))

            def sum_rows(t):
                dve.wait_ge(prodV_ready, t + 1)
                dve.tensor_reduce(ctx0[:, t, :], a_prod[t % 2].rearrange("p j e -> p e j"), AX.X, ALU.add).then_inc(prodV_used, 1)

            for t in range(NT):
                ch.link(dve.tensor_tensor(a_tmp, a_W[:, t], bc(a_sc[:, t, :].unsqueeze(2), [P, HK, WIN]), ALU.mult))
                if t >= 2:
                    dve.wait_ge(prodV_ready, t - 1)
                dve.tensor_reduce(a_A[t % 2], a_tmp.rearrange("p (h k) j -> p h j k", h=H0), AX.X, ALU.add).then_inc(attw_ready, 1)
                dve.wait_ge(attw_ready, t + 1)
                if t:
                    sum_rows(t - 1)
            sum_rows(NT - 1)
            dve.wait_ge(prodV_used, NT)
            general(NT, more_context)
            dve.sem_inc(ctxn_ready, NT)
            dve.wait_ge(tanh_ready, 2)
            add_out(0, tgx[:, 0:1])

            dve.wait_ge(i8_w, 16)
            ch.link(dve.tensor_reduce(i8wsc, i8w, AX.X, ALU.max, apply_absolute_value=True))
            ch.link(dve.tensor_scalar(i8wsc, i8wsc, 1e-12, 1.0 / 127.0, ALU.max, ALU.mult))
            ch.link(dve.reciprocal(i8wr, i8wsc))
            for i in range(DC):
                ch.link(dve.tensor_scalar(i8w[:, i], i8w[:, i], i8wr[:, i:i + 1], MAGIC, ALU.mult, ALU.add))
                ch.link(dve.tensor_scalar(i8w[:, i], i8w[:, i], -MAGIC, 127.0, ALU.add, ALU.min))
                ins = dve.tensor_scalar(i8wq[:, i], i8w[:, i], -127.0, None, ALU.max)
            ins.then_inc(i8_wq, 2)
            normalise(1)
            dve.wait_ge(xn_ready, 2 * NT)
            ch.link(dve.tensor_reduce(i8xsc, xn[:], AX.X, ALU.max, apply_absolute_value=True))
            ch.link(dve.tensor_scalar(i8xsc, i8xsc, 1e-12, 1.0 / 127.0, ALU.max, ALU.mult))
            ch.link(dve.reciprocal(i8xr, i8xsc))
            for t in range(NT):
                ins = dve.tensor_scalar(xn[:, t], xn[:, t], i8xr[:, t:t + 1], MAGIC, ALU.mult, ALU.add)
            ch.link(ins)
            ch.link(dve.tensor_scalar(xn[:], xn[:], -MAGIC, 127.0, ALU.add, ALU.min))
            for t in range(NT):
                dve.tensor_scalar(i8xq[:, t], xn[:, t], -127.0, None, ALU.max).then_inc(i8_xq, 1)
            dve.wait_ge(i8_qT, DC + 1)
            dve.wait_ge(i8_xq, NT)
            for t in range(NT):
                dve.wait_ge(out_mm, OUT_AT[1] * NT + t + 1)
                ch.link(dve.scalar_tensor_tensor(xn[:, t, :], bank[4 + t % 2][:, 0:D], i8xsc[:, t:t + 1], i8sc_bc, ALU.mult, ALU.mult))
                dve.scalar_tensor_tensor(x[:, t, :], xn[:, t, :], tgf[:, 0:1], x[:, t, :], ALU.mult, ALU.add).then_inc(x_ready, 1)

            def attention(l):
                H, dh, _ = ATT[l]
                n = min(P, EW[l])
                for j in range(QCH0[l + 1] - QCH0[l]):
                    k = QCH0[l] + j
                    dve.wait_ge(qp_evac, k + 1)
                    hi, mid, lo = qph[k % 2]
                    ch.link(dve.tensor_tensor(qr[k % 2][0:n], qf[k % 2][0:n], hi[0:n], ALU.subtract))
                    ch.link(dve.tensor_copy(mid[0:n], qr[k % 2][0:n]))
                    dve.tensor_tensor(lo[0:n], qr[k % 2][0:n], mid[0:n], ALU.subtract).then_inc(qp_split, 1)

                if l == 1:
                    dve.wait_ge(prep_evac, PREP_MM)
                dve.memset(bank[7], 0.0).then_inc(pv_done, 1)

                def reduce_half(uu, place):
                    g, col, hf = uu // HALVES, uu // 2 % (HG * QT), uu % 2
                    un = GROUP0[l] * HALVES + uu
                    gi = GROUP0[l] + g
                    dve.wait_ge(max_mm, un + 1)
                    if uu % HALVES == 0 and gi >= 2:
                        dve.wait_ge(max_fin, gi - 1)
                    dve.tensor_reduce(mxh[gi % 2][:, col, hf:hf + 1], bank[TURN_BANKS[place % 3]], AX.X, ALU.max).then_inc(max_red, 1)
                    if uu % HALVES == HALVES - 1:
                        dve.wait_ge(max_red, un + 1)
                        if gi >= 2:
                            dve.wait_ge(max_tr, gi - 1)
                        dve.tensor_reduce(mxg[gi % 2], mxh[gi % 2], AX.X, ALU.max).then_inc(max_fin, 1)

                def shift_low(g, place):
                    gi = GROUP0[l] + g
                    dve.wait_ge(max_hi, gi + 1)
                    dve.scalar_tensor_tensor(shp[gi % 2][1][0:HG * QT, :], bank[TURN_BANKS[place % 3]][0:HG * QT, 0:P], -1.0, shp[gi % 2][0][0:HG * QT, :],
                                             ALU.mult, ALU.subtract).then_inc(max_lo, 1)

                def normalise_context(g, place):
                    gi = GROUP0[l] + g
                    b, h0 = g // (H // HG), (g % (H // HG)) * HG
                    dve.wait_ge(pv_tr, gi + 1)
                    turned = bank[TURN_BANKS[place % 3]].rearrange("p (q h e) -> p q h e", q=QT, h=HG)
                    if gi:
                        dve.wait_ge(norm_ready, gi)
                    ch.link(dve.reciprocal(rsum, turned[:, :, :, dh]))
                    dst = xn[:, b * QT:(b + 1) * QT, h0 * dh:(h0 + HG) * dh].rearrange("p q (h e) -> p q h e", h=HG)
                    dve.tensor_tensor(dst, turned[:, :, :, 0:dh], bc(rsum.unsqueeze(3), [P, QT, HG, dh]), ALU.mult).then_inc(norm_ready, 1)

                for step in schedule(l):
                    if step[0] == "max":
                        reduce_half(*step[1:])
                    elif step[0] == "turn":
                        shift_low(*step[1:])
                    elif step[0] == "context":
                        normalise_context(*step[1:])
                add_out(2 * l, tgx[:, l:l + 1])

            normalise(2)
            attention(1)

            normalise(3)
            dve.wait_ge(lg_mm, 1)
            lg = bank[6][:, 0:NT * E_MOE].rearrange("p (t e) -> p t e", t=NT)
            ch.link(dve.tensor_reduce(lgm, lg, AX.X, ALU.max))
            dve.tensor_tensor(lgs, lg, bc(lgm, [P, NT, E_MOE]), ALU.subtract).then_inc(lg_exp_in, 1)
            for e in range(E_MOE):
                dve.memset(unit_base[:, e:e + 1], float(CAP * e))
                ins = dve.memset(first_best[:, e:e + 1], float(E_MOE - e))
            ch.link(ins)
            dve.wait_ge(lg_exp, 1)
            ch.link(dve.tensor_reduce(lgz, lge, AX.X, ALU.add))
            ch.link(dve.reciprocal(lgz, lgz))
            ch.link(dve.tensor_tensor(lge, lge, bc(lgz, [P, NT, E_MOE]), ALU.mult))
            ch.link(dve.tensor_reduce(lgm, lge, AX.X, ALU.max))
            ch.link(dve.tensor_tensor(lgs, lge, bc(lgm, [P, NT, E_MOE]), ALU.is_ge))
            ch.link(dve.tensor_tensor(lgs, lgs, bc(first_best.unsqueeze(1), [P, NT, E_MOE]), ALU.mult))
            ch.link(dve.tensor_reduce(idx2, lgs, AX.X, ALU.max))
            dve.tensor_tensor(lgs, lgs, bc(idx2, [P, NT, E_MOE]), ALU.is_equal).then_inc(onehot_ready, 1)
            dve.wait_ge(onehot_ready, 1)
            dve.tensor_tensor(mskd, lgs, lge, ALU.mult).then_inc(mask_ready, 1)
            dve.wait_ge(rank_mm, 1)
            ch.link(dve.tensor_copy(counts, bank[4][:, 0:E_MOE]))
            ch.link(dve.tensor_scalar(over_n, counts, CAP + 0.5, None, ALU.is_gt))
            for k in range(2, OVER + 1):
                ch.link(dve.scalar_tensor_tensor(over_n, counts, k * CAP + 0.5, over_n, ALU.is_gt, ALU.add))
            ch.link(dve.tensor_copy(over_end[:, 0:1], over_n[:, 0:1]))
            for e in range(1, E_MOE):
                ch.link(dve.tensor_tensor(over_end[:, e:e + 1], over_end[:, e - 1:e], over_n[:, e:e + 1], ALU.add))
            ch.link(dve.tensor_tensor(over_base, over_end, over_n, ALU.subtract))
            ch.link(dve.tensor_scalar(over_base, over_base, float(E_MOE - 1), float(CAP), ALU.add, ALU.mult))
            rank = bank[7][:, 0:NT * E_MOE].rearrange("p (t e) -> p t e", t=NT)
            for src, dst in ((rank, rank_tok), (bc(unit_base.unsqueeze(1), [P, NT, E_MOE]), base_tok), (bc(over_base.unsqueeze(1), [P, NT, E_MOE]), over_tok)):
                ch.link(dve.tensor_tensor(pick, lgs, src, ALU.mult))
                ch.link(dve.tensor_reduce(dst, pick, AX.X, ALU.add))
            ch.link(dve.tensor_scalar(is_over, rank_tok, CAP - 0.5, None, ALU.is_gt))
            ch.link(dve.tensor_tensor(over_tok, over_tok, base_tok, ALU.subtract))
            ch.link(dve.tensor_tensor(over_tok, over_tok, is_over, ALU.mult))
            ch.link(dve.tensor_tensor(base_tok, base_tok, rank_tok, ALU.add))
            ch.link(dve.tensor_tensor(base_tok, base_tok, over_tok, ALU.add))
            dve.tensor_copy(slot_i, base_tok).then_inc(slots_ready, 1)
            dve.wait_ge(den_mm, 1)
            ch.link(dve.tensor_scalar(den, bank[5][:, 0:E_MOE], 1e-6, None, ALU.add))
            ch.link(dve.reciprocal(den, den))
            ch.link(dve.tensor_tensor(gate, mskd, bc(den.unsqueeze(1), [P, NT, E_MOE]), ALU.mult))
            ch.link(dve.tensor_reduce(gate_tok, gate, AX.X, ALU.add))
            dve.tensor_scalar(gate_tok, gate_tok, float(T), tgf[:, 1:2], ALU.mult, ALU.mult).then_inc(gate_ready, 1)
            for j in range(OVER):
                ins = dve.tensor_scalar(over_cmp[:, j], over_end, j + 0.5, None, ALU.is_lt)
            ch.link(ins)
            ch.link(dve.tensor_reduce(over_f[:, 0:OVER], over_cmp, AX.X, ALU.add))
            ch.link(dve.tensor_scalar(over_f[:, 0:OVER], over_f[:, 0:OVER], float(E_MOE - 1), None, ALU.min))
            ch.link(dve.tensor_scalar(over_f[:, OVER:OVER + 1], over_end[:, E_MOE - 1:E_MOE], 0.5, None, ALU.is_gt))
            dve.tensor_copy(over_i, over_f).then_inc(over_ready, 1)

            def unit_copies(n, kind, tr, xT, up, down, y):
                if kind == "in":
                    dve.wait_ge(tr, n + 1)
                    if n >= 2:
                        dve.wait_ge(up, (n - 1) * (FM // UP_PER_BANK))
                    dve.tensor_copy(unit_inT[n % 2], bank[6 + n % 2][:, 0:DC * CAP].rearrange("p (c s) -> p c s", c=DC)).then_inc(xT, 1)
                else:
                    dve.wait_ge(down, 2 * (n + 1))
                    out = unit_out[n % 2] if kind == "out" else unit_out[0]
                    dve.tensor_copy(out[0:SUB], bank[4 + n % 2][0:SUB].rearrange("p (i d) -> p i d", i=2)).then_inc(y, 1)

            unit_copies(0, "in", unit_tr, unit_xT, unit_up, unit_down, unit_y)
            for e in range(E_MOE):
                if e + 1 < E_MOE:
                    unit_copies(e + 1, "in", unit_tr, unit_xT, unit_up, unit_down, unit_y)
                if e >= 2:
                    dve.wait_ge(unit_st[e % 2], 16 * (e // 2))
                unit_copies(e, "out", unit_tr, unit_xT, unit_up, unit_down, unit_y)
            dve.wait_ge(over_ready, 1)
            over = dve.value_load(over_i[0:1, OVER:OVER + 1], min_val=0, max_val=1)
            with dve.If(over):
                for i in range(2):
                    dve.wait_ge(unit_st[i], 16 * E_MOE // 2)
                for j in range(OVER):
                    unit_copies(j, "in", over_tr, over_xT, over_up, over_down, over_y)
                    if j:
                        dve.wait_ge(over_st, 16 * j)
                    unit_copies(j, "over", over_tr, over_xT, over_up, over_down, over_y)
            for t in range(NT):
                dve.wait_ge(gathered[t], 16)
                dve.scalar_tensor_tensor(x[:, t, :], xn[:, t, :], gate_tok[:, t:t + 1], x[:, t, :], ALU.mult, ALU.add).then_inc(x_ready, 1)

            normalise(4)
            attention(2)

            normalise(5)
            nf = F_GLU // P
            for h in range(2):
                for f in range(nf):
                    n = h * nf + f
                    dve.wait_ge(glu_mm, 2 * n + 2)
                    dve.wait_ge(glu_silu, n + 1)
                    if h and f == 0:
                        dve.wait_ge(out_mm, OUT_AT[5] * NT + QT)
                    dve.scalar_tensor_tensor(ha[:, f, :], bank[2 + n % 2], gsc[:, 1, f:f + 1], gtmp[n % 2], ALU.mult, ALU.mult).then_inc(glu_h, 1)
                for q in range(QT):
                    t = h * QT + q
                    dve.wait_ge(out_mm, OUT_AT[5] * NT + t + 1)
                    ch.link(dve.tensor_tensor(xn[:, t, :], bank[6 + t % 2][:, 0:D], gs3, ALU.mult))
                    dve.scalar_tensor_tensor(x[:, t, :], xn[:, t, :], tgf[:, 2:3], x[:, t, :], ALU.mult, ALU.add).then_inc(x_ready, 1)

            normalise(6)
            attention(3)

            normalise(7)
            dve.wait_ge(fin_ld, 16 * 5)
            ch.link(dve.tensor_scalar(mom, mmu, -1.0, 1.0, ALU.mult, ALU.add))
            dve.wait_ge(xnT_ready, (LN_AT[7] + 1) * 4)
            for c in range(DC):
                for i, dst in enumerate((xr, xk)):
                    ch.link(dve.tensor_scalar(dst[:, c, :], xnT[:, c, :], mmu[:, i, c:c + 1], None, ALU.mult))
                    for b in range(B):
                        lo, hi = b * S, (b + 1) * S
                        ins = dve.scalar_tensor_tensor(dst[:, c, lo + 1:hi], xnT[:, c, lo:hi - 1], mom[:, i, c:c + 1], dst[:, c, lo + 1:hi], ALU.mult, ALU.add)
                    ins.then_inc(mix_ready, 1)
            for i in range(2 * DC):
                c, h = i // 2, i % 2
                dve.wait_ge(rk_act, NT + i + 1)
                ka = kact[:, c, h * CH:(h + 1) * CH]
                dve.tensor_tensor(ka, ka, ka, ALU.mult).then_inc(rk_sq, 1)
            for t in range(NT):
                dve.wait_ge(fv_mm, t + 1)
                ch2 = dve.tensor_tensor(rv[:, t, :], rv[:, t, :], bank[4 + t % 2][:, 0:D], ALU.mult)
                ch2.then_inc(rv_ready, 1)
                dve.wait_ge(rv_ready, t + 1)
                dve.scalar_tensor_tensor(x[:, t, :], rv[:, t, :], tgf[:, 3:4], x[:, t, :], ALU.mult, ALU.add).then_inc(x_ready, 1)


def kernel(**inputs):
    import numpy as _np
    import concourse.bacc as _bacc
    from concourse import mybir as _mybir
    from concourse.bass_utils import run_bass_kernel_spmd as _run

    a = {k: _np.asarray(v) for k, v in inputs.items()}
    heads = lambda m: m.transpose(1, 0, 2).reshape(m.shape[1], -1)
    cat = lambda *m: _np.concatenate(m, axis=-1)
    cols = lambda v: v.reshape(-1, min(P, v.size)).T
    arrays = {
        "b0qT": cols(a["L0_xattn_bq"]),
        "x": a["x"].reshape(T, D), "ctxT": a["ctx_1024"].reshape(CT, D).T, "mask": a["mask_BxS2_if0"],
        "g_xattn": a["g_xattn"], "g_ffn": a["g_ffn"],
        "w0kv": cat(a["L0_xattn_Wk"].T, a["L0_xattn_Wv"].T), "b0kv": cat(a["L0_xattn_bk"], a["L0_xattn_bv"]),
        "w0q": a["L0_xattn_Wq"].T, "b0q": a["L0_xattn_bq"], "woff": a["L0_xattn_Woff"].T, "boff": a["L0_xattn_boff"],
        "w0o": a["L0_xattn_Wo"].T, "b0o": a["L0_xattn_bo"], "i8rhsT": a["L0_ffn_rhs"].T,
        "wq1": heads(a["L1_xattn_Wq"]), "wkv1": cat(heads(a["L1_xattn_Wk"]), heads(a["L1_xattn_Wv"])), "wo1": a["L1_xattn_Wo"],
        "wg": a["L1_ffn_Wg"], "bg": a["L1_ffn_bg"], "w1": a["L1_ffn_W1"], "w2": a["L1_ffn_W2"],
        "glu1": a["L2_ffn_w1_w"].T, "glu2": a["L2_ffn_w2_w"].T, "gluh1": a["L2_ffn_h1_w"].T, "gluh2": a["L2_ffn_h2_w"].T,
        "glu3": a["L2_ffn_w3_w"].T, "s1": cols(a["L2_ffn_w1_s"]), "s2": cols(a["L2_ffn_w2_s"]), "sh1": cols(a["L2_ffn_h1_s"]),
        "sh2": cols(a["L2_ffn_h2_s"]), "s3": a["L2_ffn_w3_s"],
        "w_r": a["L3_ffn_W_r"].T, "w_k": a["L3_ffn_W_k"].T, "w_v": a["L3_ffn_W_v"].T, "mu_r": cols(a["L3_ffn_mu_r"]), "mu_k": cols(a["L3_ffn_mu_k"]),
    }
    for l in (2, 3):
        p = f"L{l}_xattn_"
        arrays |= {f"wq{l}": a[p + "Wq"], f"wkv{l}": cat(a[p + "Wk"], a[p + "Wv"]), f"wo{l}": a[p + "Wo"], f"bq{l}": cols(a[p + "bq"]),
                   f"bk{l}": cols(a[p + "bk"]), f"bv{l}": a[p + "bv"], f"bo{l}": a[p + "bo"]}
    nc = _bacc.Bacc("TRN2", target_bir_lowering=False, num_devices=1)
    io, feed = {}, {}
    for name, v in arrays.items():
        feed[f"in_{name}"] = _np.ascontiguousarray(v)
        io[name] = nc.dram_tensor(f"in_{name}", feed[f"in_{name}"].shape, _mybir.dt.from_np(feed[f"in_{name}"].dtype), kind="ExternalInput").ap()
    io["out"] = nc.dram_tensor("out_0", (T, D), F32, kind="ExternalOutput").ap()
    build(nc, io)
    got = _run(nc, [feed], core_ids=[0]).results[0]["out_0"]
    return _np.asarray(got).reshape(B, S, D)
```

```python
from contextlib import ExitStack

import concourse.bass as bass
from concourse import mybir

F32 = mybir.dt.float32
BF16 = mybir.dt.bfloat16
F32R = mybir.dt.float32r
I32 = mybir.dt.int32
ALU = mybir.AluOpType
ACT = mybir.ActivationFunctionType
AX = mybir.AxisListType

P = 128
D = 256
DC = D // P
B = 2
S = 512
M = 1024
T = B * S
NT = T // P
QT = S // P
CT = B * M
NCT = CT // P
CH = 512
EPS_LN = 1e-5
MAGIC = 1.5 * 2.0**23

H0, HD0, NK = 16, 16, 5
HK = H0 * NK
LEFT = (-NK) // 2
WIN = 8
NWIN = 3
BACK = 5
ROWS = M + S + 8

ATT = {1: (16, 8, 256 ** -0.5), 2: (16, 16, 0.25), 3: (8, 4, 1.0 / float(32.0 ** 0.5))}
HG = 4
KT = M // P
PARTS = 3
K_PARTS = {1: (3, 3, 3), 2: (3, 2, 1), 3: (3, 3, 3)}
NPAIRS = {l: sum(n) for l, n in K_PARTS.items()}


def part_blocks(l):
    return [(j, c) for j, n in enumerate(K_PARTS[l]) for c in ([range(PARTS)] if n == PARTS else [range(c, c + 1) for c in range(n)])]


TWO_ONES = 1.0 + 127 * 2.0**-16
MIN_ROWS = 66
SHIFT_ROWS = 2

NGROUPS = {l: B * ATT[l][0] // HG for l in ATT}
GROUP0 = {l: sum(NGROUPS[i] for i in range(1, l)) for l in range(1, 5)}
EW = {l: ATT[l][0] * ATT[l][1] for l in ATT}
EC = {l: max(1, EW[l] // P) for l in ATT}
PREP0 = {l: sum(EC[i] * CT // CH for i in range(1, l)) for l in range(1, 5)}
QCH0 = {l: sum(EC[i] * T // CH for i in range(1, l)) for l in range(1, 5)}
GEN_STEPS = M // WIN - 1
GEN_LINKS = 10


def keys_and_queries(gi):
    layer = lambda i: next(l for l in ATT if i < GROUP0[l + 1])
    return sum(16 * 2 * len(part_blocks(layer(i))) for i in range(gi % 3, gi + 1, 3))


def zeroed(l, g):
    return GROUP0[l] + l + g + 1


def chunk_rows(k):
    return chunk_of(k)[1]


def chunk_of(k):
    l = next(l for l in ATT if k < PREP0[l + 1])
    j = k - PREP0[l]
    return l, min(P, EW[l]), j // (CT // CH), j % (CT // CH)


LN_AT = {0: 0, 2: 1, 3: 2, 4: 3, 5: 4, 6: 5, 7: 6}
OUT_AT = {0: 0, 1: 1, 2: 2, 4: 3, 5: 4, 6: 5}
CTX_BANKS0 = {0: 0, 1: 2 * DC, 2: 2 * DC + 2 * EC[1], 3: 2 * DC + 2 * EC[1] + 2 * EC[2]}
HALVES = HG * QT * 2
LEAD = HALVES + 8

TURN_LAG = 2
TURN_BANKS = (4, 5, 6)
NORMAL_LAG = 4
WEIGHTS_AT = 2
LN_HOLDS = {0: 10, 2: 7, 3: 8, 4: 60, 5: 22, 6: 12, 7: 16}
QUERY_HOLDS = {1: 30, 2: 20, 3: 22}
CTX_HOLD, UNIT_HOLD, MIX_HOLD = 20, 44, 22
CTX_SLOT = 4
XN0 = {s: s * NT for s in range(8)}
LATE_LOADS = 2 + 3 * 2 + 2 * 2
REST_LAG = 2
LOW_LAG = 4
STORE_LAG = 3
PBUFS = 4
KCHUNKS = PREP0[4]
QT_BANKS = (0, 1, 6, 7)
KV0_EARLY = 2
assert KCHUNKS == 2 * NT == NCT


def schedule(l):
    steps, turns, u, total = [], 0, 0, NGROUPS[l] * HALVES
    batch = NGROUPS[l] // B
    finish = {}
    for b in range(B - 1):
        first = (b + 1) * batch * KT + CTX_SLOT + 1
        for i, step in enumerate([("heads", (b, c)) for c in range(EC[l])] + [("out", (b, i)) for i in range(2)]):
            finish[first + i] = step
        finish[first + EC[l] + 2] = ("variance", b)
        finish[first + EC[l] + 2 + NORMAL_LAG] = ("normalise", b)

    def turn(kind, *what):
        nonlocal turns
        steps.append((kind, *what, turns))
        turns += 1

    def maxima(upto):
        nonlocal u
        while u < min(upto, total):
            turn("max", u)
            u += 1
            if u > HALVES and u % HALVES == TURN_LAG:
                turn("turn", u // HALVES - 1)
            if u == total:
                turn("turn", NGROUPS[l] - 1)

    for g in range(NGROUPS[l]):
        for kt in range(KT):
            sl = g * KT + kt
            maxima(LEAD + 4 * sl)
            steps.append(("score", g, kt, 0))
            maxima(LEAD + 4 * sl + 2)
            steps.append(("score", g, kt, 1))
            if sl:
                steps.append(("values", (sl - 1) // KT, (sl - 1) % KT))
            if kt == 0 and g:
                steps.append(("copy", g - 1))
            if kt == CTX_SLOT and g:
                turn("context", g - 1)
            if sl in finish and finish[sl][0] in ("heads", "out"):
                turn(*finish[sl])
            elif sl in finish:
                steps.append(finish[sl])
    steps += [("values", NGROUPS[l] - 1, KT - 1), ("copy", NGROUPS[l] - 1)]
    turn("context", NGROUPS[l] - 1)
    steps.append(("tokens", 0))
    for c in range(EC[l]):
        turn("heads", (B - 1, c))
    for i in range(2):
        turn("out", (B - 1, i))
    return steps


E_MOE, F_MOE = 8, 1024
FM = F_MOE // P
CAP = 176
SUB = CAP // 2
OVER = (T - 1) // CAP
SLOT_ROWS = -(-(E_MOE + OVER) * CAP // P) * P
UP_PER_BANK = CH // CAP
MOE_BUFS = 3
F_GLU = 1024
NF = F_GLU // P
GC = F_GLU
UP_FS = GC // (2 * DC * P)
UP_CHUNKS = NF // UP_FS
W3_CHUNKS = NF * D // GC
GLU_HALF = list(range(UP_CHUNKS + 2 * NF))
W3_FIRST = len(GLU_HALF)
GLU_ORDER = GLU_HALF[:-NF] + [W3_FIRST + i for i in range(W3_CHUNKS)] + GLU_HALF[-NF:] + GLU_HALF
GLU_RAW = 3
TOKENS_AT = NF // 2
GLU_CHUNKS = W3_FIRST + W3_CHUNKS
SCAN_EACH = -(-GLU_CHUNKS // E_MOE)
BF16_REST = 0xFFFF
BLOCKS = 3 * NF


def raw_loads(n):
    return len(range(n % GLU_RAW, GLU_CHUNKS, GLU_RAW)) + n // GLU_RAW + 1


def glu_half(n):
    return int(n >= len(GLU_HALF) + W3_CHUNKS)


def glu_blocks(n):
    c = GLU_ORDER[n]
    return glu_half(n) * BLOCKS + ((c + 1) * UP_FS if c < UP_CHUNKS else NF + c + 1 - UP_CHUNKS)


def glu_buffer(n):
    return sum(c < W3_FIRST for c in GLU_ORDER[:n]) % 2


def build(nc, io):
    with ExitStack() as ctx:
        def sb(name, shape, dt=F32):
            return ctx.enter_context(nc.sbuf_tensor(name, shape, dt))

        def sem(name):
            return ctx.enter_context(nc.semaphore(name))

        st_bank = [ctx.enter_context(nc.psum_tensor(f"st_bank{i}", [P, 2, CH], F32)) for i in range(2)]
        bank = [st_bank[i // 2][:, i % 2, :] for i in range(4)]
        bank += [ctx.enter_context(nc.psum_tensor(f"bank{i}", [P, CH], F32))[:, :] for i in range(4, 8)]

        kv_table = nc.dram_tensor("kv_table", [B, ROWS, 2 * D], F32).ap()
        kparts = {l: nc.dram_tensor(f"kparts{l}", [ATT[l][0] * ATT[l][1], PARTS, CT], BF16).ap() for l in ATT}
        qparts = {l: nc.dram_tensor(f"qparts{l}", [PARTS, ATT[l][0] * ATT[l][1], PARTS, T], BF16).ap() for l in ATT}

        slot_in = nc.dram_tensor("slot_in", [SLOT_ROWS, D], F32).ap()
        slot_out = nc.dram_tensor("slot_out", [SLOT_ROWS, D], F32).ap()

        x = sb("x", [P, NT, D])
        xn = sb("xn", [P, NT, D])
        xnT = sb("xnT", [P, DC, T])
        with nc.sbuf_tensor("ctxT", [P, DC, CT], F32) as ctxT:
            pass
        g_x = [sb(f"g_x{i}", [P, DC, T], F32R) for i in range(2)]
        scan_buf = [ctxT[:, i // 2, i % 2 * GC:(i % 2 + 1) * GC] for i in range(GLU_RAW)]
        scan_bits = ctxT[:, 1, GC:2 * GC].bitcast(I32)
        ident = sb("ident", [P, P])
        identb = sb("identb", [P, P], BF16)
        onesf = sb("onesf", [P, P])
        onesb = sb("onesb", [P, P], BF16)
        zero_row = sb("zero_row", [P, D // 2])
        before = sb("before", [P, P], BF16)
        bnst = sb("bnst", [P, NT, 6])
        mv = sb("mv", [P, NT, 2])
        rstd = sb("rstd", [P, NT])
        minus_half = sb("minus_half", [P, NT])
        tgx = sb("tgx", [P, 4])
        tgf = sb("tgf", [P, 4])
        gx = sb("gx", [P, 4])
        gf = sb("gf", [P, 4])
        ARENA = 31 * 1024
        with nc.sbuf_tensor("arena", [P, ARENA], F32) as arena:
            pass
        g_a = [[sb(f"g_a{i}{j}", [P, NF, CH], F32R) for j in range(2)] for i in range(2)]
        g_w = [[sb(f"g_w{i}{j}", [P, GC], F32R) for j in range(2)] for i in range(2)]
        g_w3 = [sb(f"g_w3{j}", [P, NF, D], F32R) for j in range(2)]
        GLU_WORDS = 4 * NF * CH + 4 * GC + 2 * NF * D
        arena_rest = sb("arena_rest", [P, ARENA - GLU_WORDS])

        class Region:
            def __init__(self, at=0):
                self.at = at

            def take(self, shape, dt=F32):
                n = 1
                for s in shape:
                    n *= s
                words = n if dt in (F32, I32) else (n + 1) // 2
                ap = arena[:, self.at:self.at + words]
                self.at += words
                assert self.at <= ARENA, self.at
                if dt != F32:
                    ap = ap.bitcast(dt)
                if len(shape) == 2:
                    ap = ap.rearrange("p (a b) -> p a b", a=shape[0])
                elif len(shape) == 3:
                    ap = ap.rearrange("p (a b c) -> p a b c", a=shape[0], b=shape[1])
                elif len(shape) == 4:
                    ap = ap.rearrange("p (a b c d) -> p a b c d", a=shape[0], b=shape[1], c=shape[2])
                return ap

        w = {}
        for l in ATT:
            e = ATT[l][0] * ATT[l][1]
            w[l] = dict(
                q=sb(f"wq{l}", [P, DC, e]), o=sb(f"wo{l}", [min(e, P), (e + P - 1) // P, D]),
                bq=sb(f"bq{l}", [min(e, P), (e + P - 1) // P]) if l > 1 else None,
                bo=sb(f"bo{l}", [1, D]) if l > 1 else None)
        vaug = {l: sb(f"vaug{l}", [P, NCT, ATT[l][0], ATT[l][1] + 1]) for l in ATT}
        wo0 = sb("wo0", [P, DC, D])
        bo0 = sb("bo0", [1, D])

        chain_dve, chain_act, chain_pool = sem("chain_dve"), sem("chain_act"), sem("chain_pool")
        ld_x, ld_w0, ld_bkv, ld_q0, ld_prep, ld_small, ld_late = (sem(n) for n in (
            "ld_x", "ld_w0", "ld_bkv", "ld_q0", "ld_prep", "ld_small", "ld_late"))
        ld_ctx = [sem(f"ld_ctx{b}") for b in range(B)]
        consts_ready, tanh_ready = sem("consts_ready"), sem("tanh_ready")
        kv0_mm, kv0_evac, kv0_ready = sem("kv0_mm"), sem("kv0_evac"), sem("kv0_ready")
        table_written = [sem(f"table_written{i}") for i in range(4)]
        xn_ready, xnT_mm, xnT_ready = sem("xn_ready"), sem("xnT_mm"), sem("xnT_ready")
        qT0_mm, qT0_ready, q0_mm, q0_ready, off_mm = (sem(n) for n in ("qT0_mm", "qT0_ready", "q0_mm", "q0_ready", "off_mm"))
        dist_ready, w_ready = sem("dist_ready"), sem("w_ready")
        sum_ready, sum_mm, flag_ready = sem("sum_ready"), sem("sum_mm"), sem("flag_ready")
        win_ld = [sem(f"win_ld{i}") for i in range(NWIN)]
        prod_ready, prodK_used, prodV_used = (sem(n) for n in ("prod_ready", "prodK_used", "prodV_used"))
        sub0_ready, exp0_ready, attw_ready = sem("sub0_ready"), sem("exp0_ready"), sem("attw_ready")
        gen_ld, gen_used, gen_chain = sem("gen_ld"), sem("gen_used"), sem("gen_chain")
        ctxn_ready, ctxT_mm, ctxT_ready = sem("ctxn_ready"), sem("ctxT_mm"), sem("ctxT_ready")
        out_mm, x_ready = sem("out_mm"), sem("x_ready")
        prepk_mm, prepk_hi, prepk_rest, prepk_mid, prepk_lo = (sem(n) for n in ("prepk_mm", "prepk_hi", "prepk_rest", "prepk_mid", "prepk_lo"))
        prepv_mm, prepv_evac = sem("prepv_mm"), sem("prepv_evac")
        prep_st = [sem(f"prep_st{i}") for i in range(PBUFS)]
        qp_mm, qp_evac, qp_split = sem("qp_mm"), sem("qp_evac"), sem("qp_split")
        qp_st = [sem(f"qp_st{i}") for i in range(2)]
        kq_zero, kq_ld, shift_ld = sem("kq_zero"), [sem(f"kq_ld{i}") for i in range(3)], [sem(f"shift_ld{i}") for i in range(3)]
        ones_rows = sem("ones_rows")
        max_mm, max_red, max_fin, max_tr, max_hi, max_lo = (sem(n) for n in ("max_mm", "max_red", "max_fin", "max_tr", "max_hi", "max_lo"))
        st_mm, exp_ready, pv_mm, pv_done = sem("st_mm"), sem("exp_ready"), sem("pv_mm"), sem("pv_done")
        pv_evac, pv_tr, norm_ready = sem("pv_evac"), sem("pv_tr"), sem("norm_ready")
        i8_tr, i8_bc, i8_qT, i8_w = sem("i8_tr"), sem("i8_bc"), sem("i8_qT"), sem("i8_w")
        i8_wq, i8_xq = sem("i8_wq"), sem("i8_xq")
        moe_small = sem("moe_small")
        lg_mm, lg_exp_in, lg_exp, mask_ready, den_mm, gate_ready = (sem(n) for n in (
            "lg_mm", "lg_exp_in", "lg_exp", "mask_ready", "den_mm", "gate_ready"))
        zero_ready, slots_zeroed = sem("zero_ready"), sem("slots_zeroed")
        onehot_ready, rank_mm, slots_ready, scattered, over_ready = (sem(n) for n in (
            "onehot_ready", "rank_mm", "slots_ready", "scattered", "over_ready"))
        units_done, gathered = sem("units_done"), [sem(f"gathered{b}") for b in range(B)]
        unit_w = [sem(f"unit_w{i}") for i in range(MOE_BUFS)]
        unit_x = [sem(f"unit_x{i}") for i in range(2)]
        unit_tr, unit_xT, unit_up, unit_hid, unit_down, unit_y = (sem(n) for n in (
            "unit_tr", "unit_xT", "unit_up", "unit_hid", "unit_down", "unit_y"))
        unit_yT, unit_turn, over_yT, over_turn = (sem(n) for n in ("unit_yT", "unit_turn", "over_yT", "over_turn"))
        unit_st = [sem(f"unit_st{i}") for i in range(2)]
        over_w, over_tr, over_xT, over_up, over_hid, over_down, over_y, over_st = (sem(n) for n in (
            "over_w", "over_tr", "over_xT", "over_up", "over_hid", "over_down", "over_y", "over_st"))
        glu_raw = [sem(f"glu_raw{i}") for i in range(GLU_RAW)]
        scan_done, tokens_split, gated_high = sem("scan_done"), sem("tokens_split"), sem("gated_high")
        glu_ld, glu_split, glu_mm, glu_act, act_split = (sem(n) for n in ("glu_ld", "glu_split", "glu_mm", "glu_act", "act_split"))
        fin_ld, mix_ready, rk_mm, rk_act, rk_sq, fv_mm, rv_ready = (sem(n) for n in (
            "fin_ld", "mix_ready", "rk_mm", "rk_act", "rk_sq", "fv_mm", "rv_ready"))
        stored = sem("stored")
        var_ready, rstd_ready = sem("var_ready"), sem("rstd_ready")

        r = Region()
        a_wkv = {l: r.take([DC, 2 * ATT[l][0] * ATT[l][1]]) for l in ATT}
        a_bk = {l: r.take([max(1, ATT[l][0] * ATT[l][1] // P)]) for l in (2, 3)}
        a_bv = {l: r.take([ATT[l][0] * ATT[l][1]]) for l in (2, 3)}
        a_pr = [r.take([CH]) for _ in range(PBUFS)]
        a_parts = [r.take([PARTS, CH], BF16) for _ in range(PBUFS)]
        a_ph = [[v[:, i] for i in range(PARTS)] for v in a_parts]
        w0kv_at = r.at
        a_w0kv = r.take([DC, 2 * D])
        a_bkv = r.take([2 * D])
        w0q_at = r.at
        a_w0q = r.take([DC, D])
        a_woff = r.take([DC, HK])
        a_boff = r.take([HK])
        a_bq0 = r.take([D])
        a_bq0T = r.take([DC])
        kv0_at = r.at
        a_kv0 = [r.take([2 * D]) for _ in range(4)]
        a_q0 = r.take([NT, D])
        a_qT0 = r.take([DC, T])
        a_u = r.take([NT, HK])
        a_t = r.take([NT, HK])
        a_sc = r.take([NT, HK])
        a_small = r.take([256])
        a_mx, a_sm = r.take([NT * H0]), r.take([NT * H0])
        a_loc, a_pos, a_msum = r.take([NT]), r.take([NT, WIN]), r.take([B])
        a_rlen = r.take([B])
        a_cov, a_gpos, a_gwrap = r.take([4]), r.take([WIN]), r.take([WIN])
        ctx0 = xn
        end_l0 = r.at
        r2 = Region(end_l0)
        a_win = [r2.take([WIN, D]) for _ in range(2)] + [a_qT0.rearrange("p c t -> p (c t)").rearrange("p (j e) -> p j e", j=WIN)]
        a_prod = [r2.take([WIN, D]) for _ in range(2)]
        a_W = r2.take([NT, HK, WIN])
        a_S = r2.take([WIN, H0])
        r3 = Region(w0kv_at)
        a_A = [r3.take([H0, WIN]) for _ in range(3)]
        a_tmp = Region(w0q_at).take([HK, WIN])
        assert HK * WIN <= DC * (D + HK)
        a_gW = Region(kv0_at).take([HK, WIN])
        gwin = xnT[:, :, :].rearrange("p c t -> p (c t)").rearrange("p (j e) -> p j e", j=WIN)
        a_mask = a_prod[0]
        a_iref = a_W[:, 0].rearrange("p a j -> p (a j)").bitcast(I32)
        a_ref = a_W[:, 1].rearrange("p a j -> p (a j)")
        a_ipos = a_W[:, 2].rearrange("p a j -> p (a j)")[:, 0:NT * WIN + NT].bitcast(I32)
        a_wrap = a_W[:, 3].rearrange("p a j -> p (a j)")
        flag_i = sb("flag_i", [1, 1], I32)
        low_flags = sb("low_flags", [1, 2], I32)

        r = Region()
        keys_bufs = [ctxT[:, 0, 0:HG * M // 2].bitcast(BF16).rearrange("p (h t) -> p h t", h=HG)] + [r.take([HG, M], BF16) for _ in range(2)]
        Kc = {l: [keys_bufs[(i - GROUP0[l]) % 3] for i in range(3)] for l in ATT}
        Qc = [r.take([HG, S], BF16) for _ in range(3)]
        prob = [r.take([HG, S]) for _ in range(3)]
        mxh = [r.take([HG * QT, 2]) for _ in range(2)]
        mxg = [r.take([HG * QT]) for _ in range(2)]
        shp = [[r.take([P], BF16) for _ in range(SHIFT_ROWS)] for _ in range(2)]
        pvs = xnT[:, 1, CH:2 * CH]
        rsum = r.take([QT, HG])
        qf = [r.take([CH]) for _ in range(2)]
        qr = [r.take([CH]) for _ in range(2)]
        qph = [[r.take([CH], BF16) for _ in range(3)] for _ in range(2)]
        after_att = r.at
        r = Region(after_att)
        mw1 = [r.take([DC, F_MOE]) for _ in range(MOE_BUFS)]
        mw2 = [r.take([FM, D]) for _ in range(MOE_BUFS)]
        r = Region()
        unit_in = r.take([E_MOE, 2, D])
        unit_inT = [r.take([DC, CAP]) for _ in range(2)]
        hid = [r.take([FM, CAP]) for _ in range(2)]
        unit_out = [r.take([2, D]) for _ in range(2)]
        unit_outT = [r.take([DC, CAP]) for _ in range(2)]
        wg, bg = r.take([DC, E_MOE]), r.take([E_MOE])
        lgs, lge, mskd, gate, pick = (r.take([NT, E_MOE]) for _ in range(5))
        lgm, lgz, idx2 = r.take([NT, 1]), r.take([NT, 1]), r.take([NT, 1])
        gate_tok, rank_tok, base_tok, over_tok, is_over = (r.take([NT]) for _ in range(5))
        first_best, den, unit_base, over_base, counts = (r.take([E_MOE]) for _ in range(5))
        sums = [r.take([2 * E_MOE]) for _ in range(4)]
        over_n, over_end = sums[0][:, E_MOE:], sums[3][:, E_MOE:]
        assert E_MOE == 2 ** 3
        onehot_b = r.take([NT, E_MOE], BF16)
        limits = r.take([OVER, E_MOE])
        low_sum = r.take([1])
        over_cmp, over_f = r.take([OVER, E_MOE]), r.take([OVER + 1])
        slot_i = r.take([NT], I32)
        over_i = r.take([OVER + 1], I32)
        assert r.at <= after_att
        r = Region(GLU_WORDS)
        assert r.at >= after_att
        g_raw = [r.take([GC]) for _ in range(GLU_RAW)]
        gsc = r.take([4, NF])
        gs3 = r.take([D])
        g_tmp = [r.take([CH]) for _ in range(2)]
        g_silu = [r.take([CH]) for _ in range(2)]
        r = Region()
        mwr, mwk, mwv = (r.take([DC, D]) for _ in range(3))
        mmu, mom = r.take([2, DC]), r.take([2, DC])
        xr, xk = r.take([DC, T]), r.take([DC, T])
        rv, kact = r.take([NT, D]), r.take([DC, T])

        def table_dmas(t):
            return sum(1 + (i % KT < QT) + (i % KT == KT - 1) for i in range(t % 4, t + 1, 4))

        r = Region(kv0_at + HK * WIN)
        i8w = r.take([DC, D])
        i8wq, i8wT = r.take([DC, D], BF16), r.take([DC, D], BF16)
        i8wr, i8wsc = r.take([DC]), r.take([DC])
        assert r.at <= kv0_at + 4 * 2 * D
        i8xq, i8xT = r.take([NT, D], BF16), r.take([DC, T], BF16)
        i8xr, i8xsc, i8sc_bc = r.take([NT]), r.take([NT]), r.take([D])
        assert r.at <= kv0_at + 4 * 2 * D + NT * D

        def q0_bank(t):
            return bank[QT_BANKS[t // 2]][:, t % 2 * D:(t % 2 + 1) * D]

        block = ctx.enter_context(nc.Block())

        class Chain:
            def __init__(self, eng, s):
                self.eng, self.s, self.n = eng, s, 0

            def link(self, ins):
                self.n += 1
                ins.then_inc(self.s, 1)
                self.eng.wait_ge(self.s, self.n)

        def bc(ap, shape):
            return ap.to_broadcast(shape)

        @block.sync
        def _(sp):
            def ld(dst, src, s):
                sp.dma_start(dst, src).then_inc(s, 16)

            def rows(a):
                return a.rearrange("(c p) n -> p c n", p=P)

            def spread(a, n=P):
                return a.partition_broadcast(n)

            ld(x[:], io["x"].rearrange("(t p) d -> p t d", p=P), ld_x)
            ld(a_w0kv, rows(io["w0kv"]), ld_w0)
            ld(ctxT[:, :, 0:M], rows(io["ctxT"])[:, :, 0:M], ld_ctx[0])
            ld(a_w0q, rows(io["w0q"]), ld_q0)
            ld(a_woff, rows(io["woff"]), ld_q0)
            ld(a_bq0T, io["b0qT"], ld_q0)
            ld(a_bkv, spread(io["b0kv"]), ld_bkv)
            ld(a_boff, spread(io["boff"]), ld_small)
            ld(a_bq0, spread(io["b0q"]), ld_small)
            ld(a_mask.rearrange("p a b -> p (a b)").bitcast(I32), spread(io["mask"].rearrange("b m -> (b m)")), ld_small)
            ld(gx[:], spread(io["g_xattn"]), ld_small)
            ld(gf[:], spread(io["g_ffn"]), ld_small)
            ld(ctxT[:, :, M:2 * M], rows(io["ctxT"])[:, :, M:2 * M], ld_ctx[1])
            for l in ATT:
                ld(a_wkv[l], rows(io[f"wkv{l}"]), ld_prep)
            for l in (2, 3):
                e = ATT[l][0] * ATT[l][1]
                n = min(e, P)
                ld(a_bk[l][0:n, 0:e // n], io[f"bk{l}"], ld_prep)
                ld(a_bv[l][0:1, 0:e], io[f"bv{l}"].rearrange("(o n) -> o n", o=1), ld_prep)

            def window(t, col, shift):
                b, i = t // QT, t % QT
                return bass.AP(tensor=kv_table.tensor, offset=kv_table.offset + (b * ROWS + i * P) * 2 * D + col * D + shift * WIN * 2 * D,
                               ap=[[2 * D, P], [2 * D, WIN], [1, D]])

            def window_load(n, t, col):
                if n >= NWIN:
                    sp.wait_ge(prod_ready, n - NWIN + 1)
                sp.dma_start(a_win[n % NWIN], window(t, col, 0)).then_inc(win_ld[n % NWIN], 16)

            for t in range(NT):
                if t % QT == 0:
                    for i in range(4):
                        sp.wait_ge(table_written[i], 16 * table_dmas(KT * (t // QT + 1) - 4 + i))
                if t == NWIN - 1:
                    sp.wait_ge(off_mm, NT)
                window_load(t, t, 0)
            ld(i8w, io["i8rhsT"].rearrange("(c p) n -> p c n", p=P), i8_w)
            ld(wo0[:], rows(io["w0o"]), ld_late)
            ld(bo0[:], io["b0o"].rearrange("(o n) -> o n", o=1), ld_late)
            for l in ATT:
                e = ATT[l][0] * ATT[l][1]
                n = min(e, P)
                ld(w[l]["q"][:], rows(io[f"wq{l}"]), ld_late)
                ld(w[l]["o"][:], io[f"wo{l}"].rearrange("(c p) n -> p c n", p=n), ld_late)
                if l > 1:
                    ld(w[l]["bq"][:], io[f"bq{l}"], ld_late)
                    ld(w[l]["bo"][:], io[f"bo{l}"].rearrange("(o n) -> o n", o=1), ld_late)
            for t in range(NWIN):
                window_load(NT + t, t, 1)
            sp.wait_ge(flag_ready, 1)
            uncovered = sp.value_load(flag_i[0:1, 0:1], min_val=0, max_val=1)

            def general_windows(col, loop0):
                with sp.If(uncovered):
                    for t in range(NT):
                        with sp.Fori(1, M // WIN) as s:
                            sp.wait_ge(gen_used, s + (loop0 + t) * GEN_STEPS)
                            sp.dma_start(gwin, window(t, col, s)).then_inc(gen_ld, 16)

            general_windows(0, 0)
            for t in range(NWIN, NT):
                window_load(NT + t, t, 1)
            general_windows(1, NT)
            def load_rows(l, g, dst, cols, source):
                H, dh, _ = ATT[l]
                gi, h0, at = GROUP0[l] + g, (g % (H // HG)) * HG, SHIFT_ROWS
                heads = slice(h0 * dh, (h0 + HG) * dh)
                for j, parts in part_blocks(l):
                    src = source(j, heads, parts)[:, :, cols].rearrange("(h d) c t -> (d c) h t", h=HG)
                    sp.dma_start(dst[at:at + len(parts) * dh], src).then_inc(kq_ld[gi % 3], 16)
                    at += len(parts) * dh

            def keys_load(l, g):
                gi, b = GROUP0[l] + g, g // (ATT[l][0] // HG)
                sp.wait_ge(kq_zero, zeroed(l, g) if g else zeroed(l, 0) - 1)
                load_rows(l, g, Kc[l][gi % 3], slice(b * M, (b + 1) * M), lambda j, heads, parts: kparts[l][heads, parts.start:parts.stop])

            def queries_load(l, g):
                gi, b = GROUP0[l] + g, g // (ATT[l][0] // HG)
                sp.wait_ge(kq_zero, zeroed(l, g))
                k = QCH0[l] + g % (ATT[l][0] // HG) * HG * ATT[l][1] // P * 2 + b
                sp.wait_ge(qp_st[k % 2], 16 * PARTS * (k // 2 + 1))
                load_rows(l, g, Qc[gi % 3], slice(b * S, (b + 1) * S), lambda j, heads, parts: qparts[l][j, heads, 0:len(parts)])

            def shift_load(l, g):
                gi = GROUP0[l] + g
                sp.wait_ge(max_hi, gi + 1)
                sp.wait_ge(max_lo, gi + 1)
                for i in range(SHIFT_ROWS):
                    sp.dma_start(Qc[gi % 3][i:i + 1].rearrange("o h (q n) -> o (h q) n", n=P), shp[gi % 2][i][0:HG * QT, :]).then_inc(shift_ld[gi % 3], 16)

            def first_keys_load(l):
                for i in range(PBUFS):
                    sp.wait_ge(prep_st[i], 16 * (PREP0[l + 1] // PBUFS))
                keys_load(l, 0)

            def attention_loads(l):
                ng = NGROUPS[l]
                for g in range(min(3, ng)):
                    if g:
                        keys_load(l, g)
                    queries_load(l, g)
                shift_load(l, 0)
                for g in range(ng):
                    if g == WEIGHTS_AT and l == 1:
                        for e in range(MOE_BUFS):
                            expert_load(e)
                    if g == WEIGHTS_AT and l == 2:
                        glu_first_loads()
                    if g + 1 < ng:
                        shift_load(l, g + 1)
                    if g + 3 < ng:
                        keys_load(l, g + 3)
                        queries_load(l, g + 3)

            def expert_load(e):
                i = e % MOE_BUFS
                ld(mw1[i], rows(io["w1"][e]), unit_w[i])
                ld(mw2[i], rows(io["w2"][e]), unit_w[i])

            def unit_rows(dram, n):
                return dram[n * CAP:(n + 1) * CAP, :].rearrange("(s p) d -> p s d", p=SUB)

            def moe_loads():
                sp.wait_ge(x_ready, 3 * NT)
                ld(wg, rows(io["wg"]), moe_small)
                ld(bg, spread(io["bg"]), moe_small)
                sp.wait_ge(slots_zeroed, 32)
                sp.wait_ge(scattered, 16 * NT)
                for e in range(E_MOE):
                    ld(unit_in[0:SUB, e], unit_rows(slot_in, e), unit_x[min(e, 1)])
                for e in range(E_MOE):
                    if e + MOE_BUFS < E_MOE:
                        sp.wait_ge(unit_down, e + 1)
                        expert_load(e + MOE_BUFS)
                    if e == E_MOE - 1:
                        first_keys_load(2)
                    sp.wait_ge(unit_y, e + 1)
                    sp.dma_start(unit_rows(slot_out, e), unit_out[e % 2][0:SUB]).then_inc(unit_st[e % 2], 16)
                for i in range(2):
                    sp.wait_ge(unit_st[i], 16 * E_MOE // 2)
                sp.wait_ge(over_ready, 1)
                over = sp.value_load(over_i[0:1, OVER:OVER + 1], min_val=0, max_val=1)
                with sp.If(over):
                    for j in range(OVER):
                        if j:
                            sp.wait_ge(over_y, j)
                        e = sp.value_load(over_i[0:1, j:j + 1], min_val=0, max_val=E_MOE - 1)
                        sp.dma_start(mw1[0], io["w1"][bass.ds(e, 1)].rearrange("o (c p) n -> p (o c) n", p=P)).then_inc(over_w, 16)
                        sp.dma_start(mw2[0], io["w2"][bass.ds(e, 1)].rearrange("o (c p) n -> p (o c) n", p=P)).then_inc(over_w, 16)
                        sp.dma_start(unit_in[0:SUB, 0], unit_rows(slot_in, E_MOE + j)).then_inc(over_w, 16)
                        sp.wait_ge(over_y, j + 1)
                        sp.dma_start(unit_rows(slot_out, E_MOE + j), unit_out[0][0:SUB]).then_inc(over_st, 16)
                        sp.wait_ge(over_st, 16 * (j + 1))
                sp.sem_inc(units_done, 1)

            def glu_chunk_load(n):
                sp.dma_start(g_raw[n % GLU_RAW], io["glu_w"][GLU_ORDER[n]]).then_inc(glu_raw[n % GLU_RAW], 16)

            def glu_first_loads():
                sp.wait_ge(x_ready, 4 * NT)
                for i, n in enumerate(("s1", "s2", "sh1", "sh2")):
                    ld(gsc[:, i], io[n], glu_ld)
                ld(gs3, spread(io["s3"]), glu_ld)
                for n in range(GLU_RAW):
                    glu_chunk_load(n)

            def glu_loads():
                for n in range(GLU_RAW, len(GLU_ORDER)):
                    sp.wait_ge(glu_split, n - GLU_RAW + 1)
                    glu_chunk_load(n)

            def mix_loads():
                sp.wait_ge(x_ready, 7 * NT)
                for dst, n in ((mwr, "w_r"), (mwk, "w_k"), (mwv, "w_v")):
                    ld(dst, rows(io[n]), fin_ld)
                ld(mmu[:, 0], io["mu_r"], fin_ld)
                ld(mmu[:, 1], io["mu_k"], fin_ld)

            first_keys_load(1)
            sp.wait_ge(x_ready, 2 * NT)
            attention_loads(1)
            sp.wait_ge(zero_ready, 1)
            for slots in (slot_in, slot_out):
                sp.dma_start(slots.rearrange("(p a) d -> p (a d)", p=P).rearrange("p (k d) -> p k d", d=D // 2),
                             bc(zero_row[:].unsqueeze(1), [P, SLOT_ROWS // P * 2, D // 2])).then_inc(slots_zeroed, 16)
            moe_loads()
            attention_loads(2)
            glu_loads()
            first_keys_load(3)
            attention_loads(3)
            mix_loads()
            for t in range(NT):
                sp.wait_ge(x_ready, 8 * NT - NT + t + 1)
                sp.dma_start(io["out"][t * P:(t + 1) * P, :], x[:, t, :]).then_inc(stored, 16)
            sp.wait_ge(stored, 16 * NT)

        @block.gpsimd
        def _(pool):
            ch = Chain(pool, chain_pool)
            ch.link(pool.memset(ident[:], 0.0))
            ch.link(pool.affine_select(out=ident[:], in_=ident[:], compare_op=ALU.not_equal, fill=1.0, base=0,
                                       pattern=[[-1, P]], channel_multiplier=1))
            pool.tensor_copy(identb[:], ident[:]).then_inc(consts_ready, 1)
            pool.memset(onesf[:], 1.0).then_inc(consts_ready, 1)
            pool.iota(a_iref, pattern=[[0, NT * H0], [1, NK]], base=LEFT, channel_multiplier=0).then_inc(consts_ready, 1)
            pool.iota(a_ipos[:, 0:NT * WIN], pattern=[[0, B], [P, QT], [1, WIN]], base=-BACK, channel_multiplier=1).then_inc(consts_ready, 1)
            pool.iota(a_ipos[:, NT * WIN:], pattern=[[0, B], [P, QT]], base=0, channel_multiplier=1).then_inc(consts_ready, 1)
            for l in ATT:
                pool.memset(vaug[l][:].rearrange("p t h e -> p (t h) e")[:, :, ATT[l][1]], 1.0).then_inc(ones_rows, 1)

            def inverse_deviation(stage):
                for b in range(B):
                    tiles = slice(b * QT, (b + 1) * QT)
                    pool.wait_ge(var_ready, B * stage + b + 1)
                    ch.link(pool.tensor_scalar(rstd[:, tiles], mv[:, tiles, 1], EPS_LN, None, ALU.add))
                    pool.tensor_tensor(rstd[:, tiles], rstd[:, tiles], minus_half[:, tiles], ALU.pow).then_inc(rstd_ready, 1)

            pool.memset(zero_row[:], 0.0).then_inc(zero_ready, 1)
            pool.wait_ge(consts_ready, 5)
            ch.link(pool.memset(onesb[:], 1.0))
            pool.affine_select(out=before[:], in_=onesb[:], compare_op=ALU.is_gt, fill=0.0, base=0,
                               pattern=[[1, P]], channel_multiplier=-1).then_inc(consts_ready, 1)
            ch.link(pool.memset(minus_half[:], -0.5))
            inverse_deviation(0)

            pool.wait_ge(ld_bkv, 16)
            for t in range(KT):
                pool.wait_ge(kv0_evac, t + 1)
                pool.tensor_tensor(a_kv0[t % 4], a_kv0[t % 4], a_bkv, ALU.add).then_inc(kv0_ready, 1)

            def low_part(k):
                n = chunk_rows(k)
                pool.wait_ge(prepk_mid, k + 1)
                pool.tensor_tensor(a_ph[k % PBUFS][2][0:n], a_pr[k % PBUFS][0:n], a_ph[k % PBUFS][1][0:n], ALU.subtract).then_inc(prepk_lo, 1)

            for t in range(NT):
                pool.wait_ge(win_ld[t % NWIN], 16 * (t // NWIN + 1))
                pool.wait_ge(q0_ready, t + 1)
                if t >= 2:
                    pool.wait_ge(prodK_used, t - 1)
                pool.tensor_tensor(a_prod[t % 2], a_win[t % NWIN], bc(a_q0[:, t, :].unsqueeze(1), [P, WIN, D]), ALU.mult).then_inc(prod_ready, 1)
                if t >= LOW_LAG:
                    low_part(t - LOW_LAG)
            for t in range(NT):
                n = NT + t
                pool.wait_ge(win_ld[n % NWIN], 16 * (n // NWIN + 1))
                pool.wait_ge(attw_ready, t + 1)
                pool.wait_ge(prodV_used, t - 1) if t >= 2 else pool.wait_ge(prodK_used, NT)
                pool.tensor_tensor(a_prod[t % 2].rearrange("p j (h d) -> p j h d", h=H0), a_win[n % NWIN].rearrange("p j (h d) -> p j h d", h=H0),
                                   bc(a_A[t % 3].rearrange("p h j -> p j h").unsqueeze(3), [P, WIN, H0, HD0]), ALU.mult).then_inc(prod_ready, 1)
                low_part(NT + t - LOW_LAG)
            for k in range(KCHUNKS - LOW_LAG, KCHUNKS):
                low_part(k)

            def few_rows(l):
                return SHIFT_ROWS + NPAIRS[l] * ATT[l][1] < MIN_ROWS

            def keys_rows(l, gi):
                if few_rows(l):
                    ch.link(pool.memset(Kc[l][gi % 3][0:MIN_ROWS].bitcast(F32), 0.0))
                return pool.memset(Kc[l][gi % 3][0:SHIFT_ROWS].bitcast(F32), TWO_ONES)

            def first_keys_rows(l):
                keys_rows(l, GROUP0[l]).then_inc(kq_zero, 1)

            def shift_rows(l):
                for g in range(NGROUPS[l]):
                    gi = GROUP0[l] + g
                    if g == 0:
                        pool.wait_ge(x_ready, 2 * l * NT)
                        if l == 1:
                            for i in range(PBUFS):
                                pool.wait_ge(prep_st[i], 16 * (PREP0[4] // PBUFS))
                    if g >= 3:
                        pool.wait_ge(st_mm, 2 * KT * (gi - 2))
                    if g < 3:
                        if few_rows(l):
                            ch.link(pool.memset(Qc[gi % 3][0:MIN_ROWS].bitcast(F32), 0.0))
                        if g:
                            ch.link(keys_rows(l, gi))
                    pool.memset(Qc[gi % 3][0:SHIFT_ROWS].bitcast(F32), 0.0).then_inc(kq_zero, 1)

            pool.wait_ge(prepk_mm, KCHUNKS)
            pool.wait_ge(prepv_mm, 3 * NCT)
            first_keys_rows(1)
            inverse_deviation(1)
            for l in ATT:
                inverse_deviation(2 * l)
                shift_rows(l)
                inverse_deviation(2 * l + 1)
                if l == 2:
                    for h in range(2):
                        for f in range(NF):
                            pool.wait_ge(gated_high, h * NF + f + 1)
                            pool.tensor_tensor(g_a[0][1][:, f, :], g_tmp[f % 2], g_a[0][0][:, f, :].bitcast(F32), ALU.subtract).then_inc(act_split, 1)
                    pool.wait_ge(glu_mm, BLOCKS + NF)
                    first_keys_rows(3)
                if l == 1:
                    pool.wait_ge(slots_zeroed, 32)
                    pool.wait_ge(xn_ready, XN0[3] + NT)
                    pool.wait_ge(slots_ready, 1)
                    for t in range(NT):
                        pool.indirect_dma_start(slot_in, bass.IndirectOffsetOnAxis(slot_i[:, t:t + 1], 0), xn[:, t, :], None).then_inc(scattered, 16)
                    pool.wait_ge(scan_done, GLU_CHUNKS)
                    first_keys_rows(2)
                    pool.wait_ge(units_done, 1)
                    for t in range(NT):
                        pool.indirect_dma_start(xn[:, t, :], None, slot_out, bass.IndirectOffsetOnAxis(slot_i[:, t:t + 1], 0)).then_inc(gathered[t // QT], 16)

        @block.scalar
        def _(act):
            ch = Chain(act, chain_act)
            def ln_evac(stage):
                for i in range(4):
                    c, h = i % 2, i // 2
                    act.wait_ge(xnT_mm, LN_AT[stage] * 4 + i + 1)
                    act.activation(xnT[:, c, h * CH:(h + 1) * CH], bank[i], ACT.Copy).then_inc(xnT_ready, 1)

            def ctx_evac(l, width):
                n, ec = min(P, width), max(1, width // P)
                for i in range(2 * ec):
                    c, h = i % ec, i // ec
                    act.wait_ge(ctxT_mm, CTX_BANKS0[l] + i + 1)
                    act.activation(xnT[0:n, c, h * CH:(h + 1) * CH], bank[i][0:n, :], ACT.Copy).then_inc(ctxT_ready, 1)

            def kv0_store(t):
                b, i = t // KT, t % KT
                act.wait_ge(kv0_ready, t + 1)
                src = a_kv0[t % 4]
                act.dma_start(kv_table[b, BACK + i * P:BACK + (i + 1) * P, :], src).then_inc(table_written[t % 4], 16)
                if i < QT:
                    n = min(P, ROWS - (BACK + M + i * P))
                    act.dma_start(kv_table[b, BACK + M + i * P:BACK + M + i * P + n, :], src[0:n]).then_inc(table_written[t % 4], 16)
                if i == KT - 1:
                    act.dma_start(kv_table[b, 0:BACK, :], src[P - BACK:P]).then_inc(table_written[t % 4], 16)

            def kv0_copies(first, last):
                for t in range(first, last):
                    act.wait_ge(kv0_mm, t + 1)
                    if t >= 4:
                        act.wait_ge(table_written[t % 4], 16 * table_dmas(t - 4))
                    act.activation(a_kv0[t % 4], bank[4 + t % 2], ACT.Copy).then_inc(kv0_evac, 1)
                    if t > first:
                        kv0_store(t - 1)
                kv0_store(last - 1)

            def row_weights(t):
                act.wait_ge(dist_ready, t + 1)
                act.activation(a_W[:, t], a_W[:, t], ACT.Relu, bias=onesf[:, 0:1]).then_inc(w_ready, 1)

            kv0_copies(0, KV0_EARLY)
            ln_evac(0)
            act.wait_ge(ld_q0, 16 * 3)
            for c in range(DC):
                for h in range(2):
                    act.wait_ge(qT0_mm, 2 * c + h + 1)
                    act.activation(a_qT0[:, c, h * CH:(h + 1) * CH], bank[QT_BANKS[2 * c + h]], ACT.Identity, bias=a_bq0T[:, c:c + 1]).then_inc(qT0_ready, 1)
            kv0_copies(KV0_EARLY, KT)
            row_weights(0)
            row_weights(1)
            for t in range(KT, NCT):
                kv0_store(t)
                if t in (KT + 3, KT + 5):
                    row_weights((t - KT + 1) // 2)
            act.wait_ge(ld_small, 16 * 5)
            act.activation(tgx[:], gx[:], ACT.Tanh).then_inc(tanh_ready, 1)
            act.activation(tgf[:], gf[:], ACT.Tanh).then_inc(tanh_ready, 1)

            act.wait_ge(ld_prep, 16 * 7)
            act.wait_ge(ones_rows, 3)

            def middle_part(k):
                n = chunk_rows(k)
                act.wait_ge(prepk_rest, k + 1)
                act.activation(a_ph[k % PBUFS][1][0:n], a_pr[k % PBUFS][0:n], ACT.Copy).then_inc(prepk_mid, 1)

            def store_parts(k):
                l, n, c, q = chunk_of(k)
                act.wait_ge(prepk_lo, k + 1)
                act.dma_start(kparts[l][c * P:c * P + n, :, q * CH:(q + 1) * CH], a_parts[k % PBUFS][0:n]).then_inc(prep_st[k % PBUFS], 16)

            def prepare(k):
                l, n, c, q = chunk_of(k)
                if k > STORE_LAG - 1:
                    store_parts(k - STORE_LAG)
                act.wait_ge(prepk_mm, k + 1)
                if k >= PBUFS:
                    act.wait_ge(prep_st[k % PBUFS], 16 * (k // PBUFS))
                src, dst = bank[2 + k % 2][0:n, :], a_ph[k % PBUFS][0][0:n]
                if l == 1:
                    ins = act.activation(dst, src, ACT.Copy)
                else:
                    ins = act.activation(dst, src, ACT.Identity, bias=a_bk[l][0:n, c:c + 1])
                ins.then_inc(prepk_hi, 1)
                for l in ATT:
                    n_mm = 3 * k + l - 1
                    act.wait_ge(prepv_mm, n_mm + 1)
                    act.activation(vaug[l][:, k, :, 0:ATT[l][1]], bank[QT_BANKS[n_mm % 4]][:, 0:EW[l]].rearrange("p (h d) -> p h d", h=ATT[l][0]),
                                   ACT.Copy).then_inc(prepv_evac, 1)
                if k >= 1:
                    middle_part(k - 1)

            for k in range(NT - REST_LAG):
                prepare(k)
                if k + 2 * REST_LAG < NT:
                    row_weights(k + 2 * REST_LAG)
            act.wait_ge(sub0_ready, 1)
            act.activation(a_sc[:], a_sc[:], ACT.Exp, scale=0.5 * HD0 ** -0.5).then_inc(exp0_ready, 1)
            for k in range(NT - REST_LAG, KCHUNKS):
                prepare(k)
            middle_part(KCHUNKS - 1)
            for k in range(KCHUNKS - STORE_LAG, KCHUNKS):
                store_parts(k)
            ctx_evac(0, D)

            act.wait_ge(i8_wq, 1)

            def i8_evac():
                for i in range(DC):
                    act.wait_ge(i8_tr, i + 1)
                    act.activation(i8wT[:, i, :], bank[i][:, 0:D // 2].bitcast(BF16), ACT.Copy).then_inc(i8_qT, 1)
                act.wait_ge(i8_bc, 1)
                act.activation(i8sc_bc, bank[4][:, 0:D], ACT.Copy).then_inc(i8_qT, 1)
                for i in range(4):
                    c, h = i % 2, i // 2
                    act.wait_ge(i8_tr, DC + i + 1)
                    act.activation(i8xT[:, c, h * CH:(h + 1) * CH], bank[i][:, 0:CH // 2].bitcast(BF16), ACT.Copy).then_inc(i8_qT, 1)

            i8_evac()

            def q_store(l, k, parts):
                n, j = min(P, EW[l]), k - QCH0[l]
                c, q = j // 2, j % 2
                for i in parts:
                    act.wait_ge(qp_split, k + 1) if i else act.wait_ge(qp_evac, k + 1)
                    copies = PARTS if K_PARTS[l][i] == PARTS else 1
                    act.dma_start(qparts[l][i, c * P:c * P + n, 0:copies, q * CH:(q + 1) * CH],
                                  bc(qph[k % 2][i][0:n].unsqueeze(1), [n, copies, CH])).then_inc(qp_st[k % 2], 16)

            def attention(l):
                H, dh, scale = ATT[l]
                n = min(P, EW[l])
                for j in range(QCH0[l + 1] - QCH0[l]):
                    k = QCH0[l] + j
                    act.wait_ge(qp_mm, k + 1)
                    if k >= 2:
                        act.wait_ge(qp_split, k - 1)
                        act.wait_ge(qp_st[k % 2], 16 * 3 * (k // 2))
                    if l == 1:
                        ins = act.activation(qf[k % 2][0:n], bank[j][0:n], ACT.Copy)
                    else:
                        ins = act.activation(qf[k % 2][0:n], bank[j][0:n], ACT.Identity, bias=w[l]["bq"][:, j // 2:j // 2 + 1])
                    ch.link(ins)
                    act.activation(qph[k % 2][0][0:n], qf[k % 2][0:n], ACT.Copy).then_inc(qp_evac, 1)
                    q_store(l, k, [0])
                    if j >= 1:
                        q_store(l, k - 1, [1, 2])
                q_store(l, QCH0[l + 1] - 1, [1, 2])

                for step in schedule(l):
                    if step[0] == "turn":
                        _, g, place = step
                        gi = GROUP0[l] + g
                        act.wait_ge(max_tr, gi + 1)
                        if gi >= 2:
                            act.wait_ge(shift_ld[(gi - 2) % 3], 16 * SHIFT_ROWS * ((gi - 2) // 3 + 1))
                        act.activation(shp[gi % 2][0][0:HG * QT, :], bank[TURN_BANKS[place % 3]][0:HG * QT, 0:P], ACT.Copy, scale=-1.0).then_inc(max_hi, 1)
                    elif step[0] == "score":
                        _, g, kt, pair = step
                        sl = (GROUP0[l] + g) * KT + kt
                        if sl >= 3:
                            act.wait_ge(pv_mm, sl - 2)
                        act.wait_ge(st_mm, 2 * sl + pair + 1)
                        act.activation(prob[sl % 3][:, 2 * pair:2 * pair + 2, :], st_bank[pair][:], ACT.Exp, scale=scale).then_inc(exp_ready, 1)
                    elif step[0] == "copy":
                        gi = GROUP0[l] + step[1]
                        act.wait_ge(pv_mm, KT * (gi + 1))
                        if gi:
                            act.wait_ge(pv_tr, gi)
                        act.activation(pvs, bank[7], ACT.Copy).then_inc(pv_evac, 1)
                    elif step[0] == "heads":
                        _, (b, c), place = step
                        act.wait_ge(ctxT_mm, CTX_BANKS0[l] + b * EC[l] + c + 1)
                        act.activation(xnT[0:n, c, b * CH:(b + 1) * CH], bank[TURN_BANKS[place % 3]][0:n, :], ACT.Copy).then_inc(ctxT_ready, 1)

            ln_evac(2)
            attention(1)

            ln_evac(3)
            act.wait_ge(lg_exp_in, 1)
            act.activation(lge, lgs, ACT.Exp).then_inc(lg_exp, 1)
            ups = FM // UP_PER_BANK

            def hidden(n, up, ready, down):
                for i in range(ups):
                    act.wait_ge(up, n * ups + i + 1)
                    if n >= 2 and i == 0:
                        act.wait_ge(down, n - 1)
                    act.activation(hid[n % 2][:, i * UP_PER_BANK:(i + 1) * UP_PER_BANK, :],
                                   bank[i % 4][:, 0:UP_PER_BANK * CAP].rearrange("p (f s) -> p f s", s=CAP), ACT.Relu).then_inc(ready, 1)

            def scan_loads(first, last):
                for n in range(first, min(last, GLU_CHUNKS)):
                    if n >= GLU_RAW:
                        act.wait_ge(scan_done, n - GLU_RAW + 1)
                    act.dma_start(scan_buf[n % GLU_RAW], io["glu_w"][n]).then_inc(glu_raw[n % GLU_RAW], 16)

            scan_loads(0, 1)
            for e in range(E_MOE):
                hidden(e, unit_up, unit_hid, unit_down)
                scan_loads(1 + e * SCAN_EACH, 1 + (e + 1) * SCAN_EACH)
            act.wait_ge(over_ready, 1)
            over = act.value_load(over_i[0:1, OVER:OVER + 1], min_val=0, max_val=1)
            with act.If(over):
                for j in range(OVER):
                    hidden(j, over_up, over_hid, over_down)

            ln_evac(4)
            attention(2)

            ln_evac(5)
            act.wait_ge(glu_ld, 16 * 5)
            for a in range(2 * BLOCKS):
                h, layer, f = a // BLOCKS, a // NF % 3, a % NF
                act.wait_ge(glu_mm, a + 1)
                if layer == 0 and h * NF + f >= 2:
                    act.wait_ge(gated_high, h * NF + f - 1)
                if layer > 0:
                    act.wait_ge(act_split, a - 1)
                if layer == 0:
                    ins = act.activation(g_silu[a % 2], bank[f % 2], ACT.Silu, scale=gsc[:, 0, f:f + 1])
                else:
                    ins = act.activation(g_tmp[a % 2], bank[4 + f % 2], ACT.Gelu, scale=gsc[:, 1 + layer, f:f + 1])
                ins.then_inc(glu_act, 1)

            ln_evac(6)
            attention(3)

            ln_evac(7)
            for i in range(B * DC):
                h, c = i // DC, i % DC
                act.wait_ge(rk_mm, i + 1)
                act.activation(kact[:, c, h * CH:(h + 1) * CH], bank[i], ACT.Relu).then_inc(rk_act, 1)
            for t in range(NT):
                act.wait_ge(rk_mm, B * DC + t + 1)
                act.activation(rv[:, t, :], bank[6 + t % 2][:, 0:D], ACT.Sigmoid).then_inc(rk_act, 1)

        @block.tensor
        def _(pe):
            def hold_clock(n, b):
                for _ in range(n):
                    pe.matmul(bank[b], identb[:], bc(identb[:].unsqueeze(1), [P, CH // P, P]), start=True, stop=True)

            def transposes(src, dst_sem, base, width, ready, ready0, batches=range(B)):
                n, ec = min(P, width), max(1, width // P)
                for t in (b * QT + q for b in batches for q in range(QT)):
                    if ready is not None:
                        pe.wait_ge(ready, ready0 + t + 1)
                    for c in range(ec):
                        ins = pe.transpose(bank[(t // QT) * ec + c][0:n, (t % QT) * P:(t % QT + 1) * P], src[:, t, c * P:c * P + n], ident[:])
                        if t % QT == QT - 1:
                            ins.then_inc(dst_sem, 1)

            def project_out(stage, wmat, width, bias, l):
                n, ec = min(P, width), max(1, width // P)
                for t in range(NT):
                    if t % QT == 0:
                        pe.wait_ge(ctxT_ready, CTX_BANKS0[l] + (t // QT + 1) * ec)
                    if t >= 2:
                        pe.wait_ge(x_ready, stage * NT + t - 1)
                    o = bank[4 + t % 2][:, 0:D]
                    for c in range(ec):
                        ins = pe.matmul(o, xnT[0:n, c, t * P:(t + 1) * P], wmat[:, c, :], start=(c == 0), stop=(c == ec - 1 and bias is None))
                    if bias is not None:
                        ins = pe.matmul(o, onesf[0:1, :], bias, start=False, stop=True)
                    ins.then_inc(out_mm, 1)

            def kv0_products(first, last):
                for t in range(first, last):
                    if t % KT == 0:
                        pe.wait_ge(ld_ctx[t // KT], 16)
                    if t >= 2:
                        pe.wait_ge(kv0_evac if t - 2 < KT else kv0_ready, t - 1)
                    for c in range(DC):
                        ins = pe.matmul(bank[4 + t % 2], ctxT[:, c, t * P:(t + 1) * P], a_w0kv[:, c, :], start=(c == 0), stop=(c == DC - 1))
                    ins.then_inc(kv0_mm, 1)

            pe.wait_ge(consts_ready, 1)
            hold_clock(CTX_HOLD, 3)
            pe.wait_ge(ld_w0, 16)
            kv0_products(0, KV0_EARLY)
            hold_clock(LN_HOLDS[0], 3)
            pe.wait_ge(consts_ready, 2)
            transposes(xn, xnT_mm, 0, D, xn_ready, 0)
            pe.wait_ge(ld_q0, 16 * 3)
            pe.wait_ge(xnT_ready, 4)
            for c in range(DC):
                for h in range(2):
                    for i in range(DC):
                        ins = pe.matmul(bank[QT_BANKS[2 * c + h]], a_w0q[:, i, c * P:(c + 1) * P], xnT[:, i, h * CH:(h + 1) * CH], start=(i == 0), stop=(i == DC - 1))
                    ins.then_inc(qT0_mm, 1)
            pe.wait_ge(qT0_ready, 4)
            for t in range(NT):
                o = bank[2 + t // QT][:, (t % QT) * HK:(t % QT + 1) * HK]
                for i in range(DC):
                    ins = pe.matmul(o, a_qT0[:, i, t * P:(t + 1) * P], a_woff[:, i, :], start=(i == 0), stop=(i == DC - 1))
                ins.then_inc(off_mm, 1)
            kv0_products(KV0_EARLY, KT)
            for t in range(NT):
                o = q0_bank(t)
                for i in range(DC):
                    ins = pe.matmul(o, xnT[:, i, t * P:(t + 1) * P], a_w0q[:, i, :], start=(i == 0), stop=(i == DC - 1))
                ins.then_inc(q0_mm, 1)
            kv0_products(KT, NCT)

            pe.wait_ge(sum_ready, 1)
            pe.wait_ge(kv0_ready, NCT)
            pe.matmul(bank[4][0:1, 0:1], onesf[:, 0:1], a_cov[:, 0:1], start=True, stop=True).then_inc(sum_mm, 1)

            pe.wait_ge(ld_prep, 16 * 7)
            pe.wait_ge(q0_ready, NT)
            for k in range(KCHUNKS):
                l, n, c, q = chunk_of(k)
                if k >= 2:
                    pe.wait_ge(prepk_rest, k - 1)
                for i in range(DC):
                    ins = pe.matmul(bank[2 + k % 2][0:n, :], a_wkv[l][:, i, c * P:c * P + n], ctxT[:, i, q * CH:(q + 1) * CH], start=(i == 0), stop=(i == DC - 1))
                ins.then_inc(prepk_mm, 1)
                for l in ATT:
                    n_mm = 3 * k + l - 1
                    if n_mm >= 4:
                        pe.wait_ge(prepv_evac, n_mm - 3)
                    o = bank[QT_BANKS[n_mm % 4]][:, 0:EW[l]]
                    for i in range(DC):
                        ins = pe.matmul(o, ctxT[:, i, k * P:(k + 1) * P], a_wkv[l][:, i, EW[l]:2 * EW[l]], start=(i == 0), stop=(i == DC - 1 and l == 1))
                    if l > 1:
                        ins = pe.matmul(o, onesf[0:1, :], a_bv[l][0:1, 0:EW[l]], start=False, stop=True)
                    ins.then_inc(prepv_mm, 1)

            pe.wait_ge(ld_late, 16 * LATE_LOADS)
            pe.wait_ge(prepk_rest, KCHUNKS)
            pe.wait_ge(prepv_evac, 3 * NCT)
            transposes(ctx0, ctxT_mm, 0, D, ctxn_ready, 0)
            project_out(0, wo0, D, bo0[:], 0)

            pe.wait_ge(i8_wq, 1)
            for c in range(DC):
                for i in range(DC):
                    ins = pe.transpose(bank[c][:, 0:D // 2].bitcast(BF16)[:, i * P:(i + 1) * P], i8wq[:, i, c * P:(c + 1) * P], identb[:])
                ins.then_inc(i8_tr, 1)
            pe.wait_ge(x_ready, NT)
            for i in range(DC):
                ins = pe.matmul(bank[4][:, i * P:(i + 1) * P], bc(i8wsc[:, i:i + 1], [P, P]), ident[:], start=True, stop=True)
            ins.then_inc(i8_bc, 1)
            for t in range(NT):
                pe.wait_ge(i8_xq, t + 1)
                if t == 0:
                    pe.wait_ge(i8_qT, DC)
                for c in range(DC):
                    ins = pe.transpose(bank[(t // QT) * DC + c][:, 0:CH // 2].bitcast(BF16)[:, (t % QT) * P:(t % QT + 1) * P], i8xq[:, t, c * P:(c + 1) * P], identb[:])
                    if t % QT == QT - 1:
                        ins.then_inc(i8_tr, 1)
            for t in range(NT):
                if t % QT == 0:
                    pe.wait_ge(i8_qT, DC + 1 + (t // QT + 1) * DC)
                if t >= 2:
                    pe.wait_ge(x_ready, NT + t - 1)
                for c in range(DC):
                    ins = pe.matmul(bank[4 + t % 2][:, 0:D], i8xT[:, c, t * P:(t + 1) * P], i8wT[:, c, :], start=(c == 0), stop=(c == DC - 1))
                ins.then_inc(out_mm, 1)

            def ln_transposes(stage, batches=range(B)):
                transposes(xn, xnT_mm, 0, D, xn_ready, XN0[stage], batches)

            def attention(l):
                H, dh, _ = ATT[l]
                R = max(MIN_ROWS, SHIFT_ROWS + NPAIRS[l] * dh)
                n = min(P, EW[l])
                stage = 2 * l
                for j in range(QCH0[l + 1] - QCH0[l]):
                    k = QCH0[l] + j
                    c, q = j // 2, j % 2
                    pe.wait_ge(xnT_ready, LN_AT[stage] * 4 + (2 if j == 0 else 4))
                    for i in range(DC):
                        ins = pe.matmul(bank[j][0:n, :], w[l]["q"][:, i, c * P:c * P + n], xnT[:, i, q * CH:(q + 1) * CH], start=(i == 0), stop=(i == DC - 1))
                    ins.then_inc(qp_mm, 1)

                hold_clock(QUERY_HOLDS[l], 4)
                order = schedule(l)
                rotation = [step for step in order if step[0] in ("max", "turn", "context", "heads", "out")]

                def bank_read(place):
                    kind, what, _ = rotation[place - len(TURN_BANKS)]
                    if kind == "max":
                        return max_red, GROUP0[l] * HALVES + what + 1
                    if kind == "heads":
                        return ctxT_ready, CTX_BANKS0[l] + what[0] * EC[l] + what[1] + 1
                    if kind == "out":
                        return x_ready, stage * NT + what[0] * QT + what[1] * 2 + 2
                    return max_lo if kind == "turn" else norm_ready, GROUP0[l] + what + 1

                def row_max(u, place):
                    g, hh, qt, half = u // HALVES, u // (2 * QT) % HG, u // 2 % QT, u % 2
                    gi = GROUP0[l] + g
                    if u % HALVES == 0:
                        pe.wait_ge(kq_ld[gi % 3], keys_and_queries(gi))
                    if place >= len(TURN_BANKS):
                        pe.wait_ge(*bank_read(place))
                    pe.matmul(bank[TURN_BANKS[place % 3]], Qc[gi % 3][0:R, hh, qt * P:(qt + 1) * P], Kc[l][gi % 3][0:R, hh, half * CH:(half + 1) * CH],
                              start=True, stop=True).then_inc(max_mm, 1)

                def turn_max(g, place):
                    gi = GROUP0[l] + g
                    pe.wait_ge(max_fin, gi + 1)
                    pe.wait_ge(*bank_read(place))
                    pe.transpose(bank[TURN_BANKS[place % 3]][0:HG * QT, 0:P], mxg[gi % 2], ident[:]).then_inc(max_tr, 1)

                def score(g, kt, pair):
                    gi = GROUP0[l] + g
                    sl = gi * KT + kt
                    if sl == GROUP0[l] * KT:
                        pe.wait_ge(qp_evac, QCH0[l + 1])
                    if kt == 0 and pair == 0:
                        pe.wait_ge(shift_ld[gi % 3], 16 * SHIFT_ROWS * (gi // 3 + 1))
                    if sl >= 1:
                        pe.wait_ge(exp_ready, 2 * (sl - 1) + pair + 1)
                    for i in range(2):
                        hh = 2 * pair + i
                        ins = pe.matmul(st_bank[pair][:, i, :], Kc[l][gi % 3][0:R, hh, kt * P:(kt + 1) * P], Qc[gi % 3][0:R, hh, :], start=True, stop=True)
                    ins.then_inc(st_mm, 1)

                def values(g, kt):
                    gi = GROUP0[l] + g
                    sl = gi * KT + kt
                    b, h0 = g // (H // HG), (g % (H // HG)) * HG
                    pe.wait_ge(exp_ready, 2 * sl + 2)
                    if kt == 0:
                        pe.wait_ge(pv_evac, gi) if g else pe.wait_ge(pv_done, l)
                    for hh in range(HG):
                        ins = pe.matmul(bank[7][32 * hh:32 * hh + dh + 1, :], vaug[l][:, b * KT + kt, h0 + hh, :], prob[sl % 3][:, hh, :],
                                        start=(kt == 0), stop=(kt == KT - 1))
                    ins.then_inc(pv_mm, 1)

                def turn_context(g, place):
                    pe.wait_ge(pv_evac, GROUP0[l] + g + 1)
                    pe.wait_ge(*bank_read(place))
                    for qt in range(QT):
                        ins = pe.transpose(bank[TURN_BANKS[place % 3]][:, qt * P:(qt + 1) * P], pvs[:, qt * P:(qt + 1) * P], ident[:])
                    ins.then_inc(pv_tr, 1)

                def turn_heads(which, place):
                    b, c = which
                    pe.wait_ge(norm_ready, GROUP0[l] + (b + 1) * NGROUPS[l] // B)
                    pe.wait_ge(*bank_read(place))
                    for q in range(QT):
                        ins = pe.transpose(bank[TURN_BANKS[place % 3]][0:n, q * P:(q + 1) * P], xn[:, b * QT + q, c * P:c * P + n], ident[:])
                    ins.then_inc(ctxT_mm, 1)

                def output(which, place):
                    b, i = which
                    pe.wait_ge(ctxT_ready, CTX_BANKS0[l] + (b + 1) * EC[l])
                    pe.wait_ge(*bank_read(place))
                    for j in range(2):
                        t = b * QT + 2 * i + j
                        o = bank[TURN_BANKS[place % 3]][:, j * D:(j + 1) * D]
                        for c in range(EC[l]):
                            ins = pe.matmul(o, xnT[0:n, c, t * P:(t + 1) * P], w[l]["o"][:, c, :], start=(c == 0), stop=(c == EC[l] - 1 and l == 1))
                        if l > 1:
                            ins = pe.matmul(o, onesf[0:1, :], w[l]["bo"][:], start=False, stop=True)
                        ins.then_inc(out_mm, 1)

                if l == 1:
                    pe.wait_ge(prepv_evac, 3 * NCT)
                for step in order:
                    if step[0] == "max":
                        row_max(*step[1:])
                    elif step[0] == "turn":
                        turn_max(*step[1:])
                    elif step[0] == "score":
                        score(*step[1:])
                    elif step[0] == "values":
                        values(*step[1:])
                    elif step[0] == "context":
                        turn_context(*step[1:])
                    elif step[0] == "tokens":
                        ln_transposes(2 * l + 1, [step[1]])
                    elif step[0] == "heads":
                        turn_heads(*step[1:])
                    elif step[0] == "out":
                        output(*step[1:])

            hold_clock(LN_HOLDS[2], 2)
            ln_transposes(2)
            attention(1)

            hold_clock(LN_HOLDS[3], 2)
            ln_transposes(3, [1])
            pe.wait_ge(xnT_ready, (LN_AT[3] + 1) * 4)
            pe.wait_ge(moe_small, 32)
            for t in range(NT):
                o = bank[6][:, t * E_MOE:(t + 1) * E_MOE]
                for i in range(DC):
                    ins = pe.matmul(o, xnT[:, i, t * P:(t + 1) * P], wg[:, i, :], start=(i == 0), stop=(i == DC - 1))
            ins.then_inc(lg_mm, 1)
            pe.wait_ge(onehot_ready, 1)
            pe.wait_ge(consts_ready, 6)
            hots = onehot_b.rearrange("p t e -> p (t e)")
            pe.matmul(bank[7][:, 0:NT * E_MOE], before[:], hots, start=True, stop=False)
            for k in range(1, NT):
                pe.matmul(bank[7][:, k * E_MOE:NT * E_MOE], onesb[:], hots[:, 0:(NT - k) * E_MOE], start=False, stop=(k == NT - 1))
            pe.matmul(bank[4][:, 0:NT * E_MOE], onesb[:], hots, start=True, stop=True).then_inc(rank_mm, 1)
            pe.wait_ge(mask_ready, 1)
            pe.matmul(bank[5][:, 0:NT * E_MOE], onesf[:], mskd.rearrange("p t e -> p (t e)"), start=True, stop=True).then_inc(den_mm, 1)
            ups = FM // UP_PER_BANK

            def unit_transposes(n, src, done, read):
                if n:
                    pe.wait_ge(read, n)
                for c in range(DC):
                    for i in range(2):
                        ins = pe.transpose(bank[6][:, c * CAP + i * SUB:c * CAP + (i + 1) * SUB], src[0:SUB, i, c * P:(c + 1) * P], ident[0:SUB, 0:SUB])
                ins.then_inc(done, 1)

            def unit_up_products(n, wbuf, up, ready, xT):
                pe.wait_ge(xT, n + 1)
                for f in range(FM):
                    i = f // UP_PER_BANK
                    if f % UP_PER_BANK == 0 and n:
                        pe.wait_ge(ready, (n - 1) * ups + i + 1)
                    for c in range(DC):
                        ins = pe.matmul(bank[i % 4][:, f % UP_PER_BANK * CAP:(f % UP_PER_BANK + 1) * CAP], mw1[wbuf][:, c, f * P:(f + 1) * P],
                                        unit_inT[n % 2][:, c, :], start=(c == 0), stop=(c == DC - 1))
                    if f % UP_PER_BANK == UP_PER_BANK - 1:
                        ins.then_inc(up, 1)

            def unit_down_products(n, wbuf, ready, down, yT):
                pe.wait_ge(ready, (n + 1) * ups)
                if n >= 2:
                    pe.wait_ge(yT, n - 1)
                for c in range(DC):
                    for f in range(FM):
                        ins = pe.matmul(bank[4 + n % 2][:, c * CAP:(c + 1) * CAP], mw2[wbuf][:, f, c * P:(c + 1) * P], hid[n % 2][:, f, :],
                                        start=(f == 0), stop=(f == FM - 1))
                ins.then_inc(down, 1)

            def unit_turn_back(n, yT, done, y):
                pe.wait_ge(yT, n + 1)
                if n:
                    pe.wait_ge(y, n)
                for i in range(2):
                    for c in range(DC):
                        ins = pe.transpose(bank[7][0:SUB, i * D + c * P:i * D + (c + 1) * P], unit_outT[n % 2][:, c, i * SUB:(i + 1) * SUB], ident[:])
                ins.then_inc(done, 1)

            pe.wait_ge(slots_ready, 1)
            pe.wait_ge(gate_ready, 1)
            hold_clock(UNIT_HOLD, 2)
            for e in range(E_MOE):
                if e == 0:
                    pe.wait_ge(unit_x[0], 16)
                    unit_transposes(0, unit_in[:, 0], unit_tr, unit_xT)
                pe.wait_ge(unit_w[e % MOE_BUFS], 32 * (e // MOE_BUFS + 1))
                unit_up_products(e, e % MOE_BUFS, unit_up, unit_hid, unit_xT)
                if e:
                    unit_turn_back(e - 1, unit_yT, unit_turn, unit_y)
                if e + 1 < E_MOE:
                    pe.wait_ge(unit_x[1], 16 * (E_MOE - 1))
                    unit_transposes(e + 1, unit_in[:, e + 1], unit_tr, unit_xT)
                unit_down_products(e, e % MOE_BUFS, unit_hid, unit_down, unit_yT)
            unit_turn_back(E_MOE - 1, unit_yT, unit_turn, unit_y)
            pe.wait_ge(over_ready, 1)
            over = pe.value_load(over_i[0:1, OVER:OVER + 1], min_val=0, max_val=1)
            with pe.If(over):
                pe.wait_ge(unit_y, E_MOE)
                for j in range(OVER):
                    pe.wait_ge(over_w, 48 * (j + 1))
                    unit_transposes(j, unit_in[:, 0], over_tr, over_xT)
                    unit_up_products(j, 0, over_up, over_hid, over_xT)
                    unit_down_products(j, 0, over_hid, over_down, over_yT)
                    unit_turn_back(j, over_yT, over_turn, over_y)
            pe.wait_ge(sum_ready, 2)
            pe.matmul(bank[6][0:1, 0:1], onesf[:, 0:1], low_sum, start=True, stop=True).then_inc(sum_mm, 1)
            pe.wait_ge(flag_ready, 3)

            hold_clock(LN_HOLDS[4], 2)
            ln_transposes(4)
            attention(2)

            hold_clock(LN_HOLDS[5], 2)
            ln_transposes(5, [1])
            pe.wait_ge(xnT_ready, (LN_AT[5] + 1) * 4)

            def gated_unit(low_weights):
                def split_products(out, weights, tokens, weights_stay, first, last):
                    pairs = [(0, 0), (0, 1)] + [(1, 0)] * low_weights
                    for i, (a, b) in enumerate(pairs):
                        stationary, moving = (weights[a], tokens[b]) if weights_stay else (tokens[b], weights[a])
                        ins = pe.matmul(out, stationary, moving, start=(first and i == 0), stop=(last and i == len(pairs) - 1))
                    return ins

                for n, c in enumerate(GLU_ORDER):
                    if c >= W3_FIRST:
                        continue
                    h = glu_half(n)
                    pe.wait_ge(glu_split, n + 1)
                    wbuf = g_w[glu_buffer(n)]
                    if c < UP_CHUNKS:
                        pe.wait_ge(tokens_split, (h + 1) * DC)
                        for i in range(UP_FS):
                            f = c * UP_FS + i
                            a = h * BLOCKS + f
                            if h * NF + f >= 2:
                                pe.wait_ge(gated_high, h * NF + f - 1)
                            for j in range(2):
                                for k in range(DC):
                                    at = (j * DC + k) * UP_FS * P + i * P
                                    ins = split_products(bank[2 * j + f % 2], [v[:, at:at + P] for v in wbuf], [v[:, k, h * CH:(h + 1) * CH] for v in g_x], True,
                                                         k == 0, k == DC - 1)
                            ins.then_inc(glu_mm, 1)
                    else:
                        layer, f = 1 + (c - UP_CHUNKS) // NF, (c - UP_CHUNKS) % NF
                        if (h, layer, f) == (1, 2, TOKENS_AT):
                            ln_transposes(6, [0])
                        a = h * BLOCKS + layer * NF + f
                        src = g_a[(layer - 1) % 2]
                        pe.wait_ge(glu_act, a - 1)
                        for j in range(NF):
                            if f == 0:
                                pe.wait_ge(act_split, a - NF + j + 1)
                            ins = split_products(bank[4 + f % 2], [v[:, j * P:(j + 1) * P] for v in wbuf], [v[:, j, :] for v in src], True, j == 0, j == NF - 1)
                        ins.then_inc(glu_mm, 1)
                    if c == len(GLU_HALF) - 1:
                        if h == 0:
                            pe.wait_ge(glu_split, GLU_ORDER.index(W3_FIRST + W3_CHUNKS - 1) + 1)
                        for q in range(QT):
                            t = h * QT + q
                            if t >= 2:
                                pe.wait_ge(x_ready, 5 * NT + t - 1)
                            for j in range(NF):
                                if q == 0:
                                    pe.wait_ge(act_split, (h + 1) * BLOCKS - NF + j + 1)
                                ins = split_products(bank[6 + t % 2][:, 0:D], [v[:, j, :] for v in g_w3], [v[:, j, q * P:(q + 1) * P] for v in g_a[0]], False, j == 0, j == NF - 1)
                            ins.then_inc(out_mm, 1)

            low, no_low = (pe.value_load(low_flags[0:1, i:i + 1], min_val=0, max_val=1) for i in range(2))
            with pe.If(no_low):
                gated_unit(False)
            with pe.If(low):
                gated_unit(True)

            hold_clock(LN_HOLDS[6], 2)
            ln_transposes(6, [1])
            attention(3)

            hold_clock(LN_HOLDS[7], 2)
            ln_transposes(7, [1])
            hold_clock(MIX_HOLD, 4)
            pe.wait_ge(fin_ld, 16 * 5)
            for i in range(B * DC):
                h, c = i // DC, i % DC
                pe.wait_ge(mix_ready, (h + 1) * DC)
                pe.wait_ge(xnT_ready, (LN_AT[7] + 1) * 4)
                for k in range(DC):
                    ins = pe.matmul(bank[i], mwk[:, k, c * P:(c + 1) * P], xk[:, k, h * CH:(h + 1) * CH], start=(k == 0), stop=(k == DC - 1))
                ins.then_inc(rk_mm, 1)
            for t in range(NT):
                pe.wait_ge(mix_ready, B * DC + (t // QT + 1) * DC)
                if t >= 2:
                    pe.wait_ge(rk_act, B * DC + t - 1)
                for k in range(DC):
                    ins = pe.matmul(bank[6 + t % 2][:, 0:D], xr[:, k, t * P:(t + 1) * P], mwr[:, k, :], start=(k == 0), stop=(k == DC - 1))
                ins.then_inc(rk_mm, 1)
            pe.wait_ge(rk_sq, 2 * DC)
            for t in range(NT):
                if t >= 2:
                    pe.wait_ge(rv_ready, t - 1)
                for i in range(DC):
                    ins = pe.matmul(bank[4 + t % 2][:, 0:D], kact[:, i, t * P:(t + 1) * P], mwv[:, i, :], start=(i == 0), stop=(i == DC - 1))
                ins.then_inc(fv_mm, 1)

        @block.vector
        def _(dve):
            ch = Chain(dve, chain_dve)

            def statistics(stage, t):
                dve.wait_ge(x_ready, (stage - 1) * NT + t + 1)
                return dve.bn_stats(bnst[:, t, :], x[:, t, :])

            def variances(stage, b):
                for t in range(b * QT, (b + 1) * QT):
                    ins = dve.bn_aggr(mv[:, t, :], bnst[:, t, :])
                ins.then_inc(var_ready, 1)

            def tile_statistics(stage, t):
                ins = statistics(stage, t)
                if t % QT == QT - 1:
                    ch.link(ins)
                    variances(stage, t // QT)

            def normalise_batch(stage, b):
                dve.wait_ge(var_ready, B * stage + b + 1)
                dve.wait_ge(rstd_ready, B * stage + b + 1)
                for t in range(b * QT, (b + 1) * QT):
                    dve.tensor_scalar(xn[:, t, :], x[:, t, :], mv[:, t, 0:1], rstd[:, t:t + 1], ALU.subtract, ALU.mult).then_inc(xn_ready, 1)

            def normalise(stage, first=0):
                if stage:
                    tile_statistics(stage, NT - 1)
                else:
                    dve.wait_ge(ld_x, 16)
                    for t in range(NT):
                        ins = dve.bn_stats(bnst[:, t, :], x[:, t, :])
                    ch.link(ins)
                    for b in range(B):
                        variances(0, b)
                for b in range(first, B):
                    normalise_batch(stage, b)

            def add_out(stage, tg, banks=4):
                for t in range(NT):
                    dve.wait_ge(out_mm, OUT_AT[stage] * NT + t + 1)
                    dve.scalar_tensor_tensor(x[:, t, :], bank[banks + t % 2][:, 0:D], tg, x[:, t, :], ALU.mult, ALU.add).then_inc(x_ready, 1)
                    if t:
                        tile_statistics(stage + 1, t - 1)

            normalise(0)
            dve.wait_ge(consts_ready, 5)
            dve.wait_ge(ld_small, 16 * 5)
            dve.tensor_copy(a_ref, a_iref)
            ch.link(dve.tensor_copy(a_pos.rearrange("p t j -> p (t j)"), a_ipos[:, 0:NT * WIN]))
            dve.tensor_scalar(a_wrap[:, 0:NT * WIN], a_pos.rearrange("p t j -> p (t j)"), 0.0, float(M), ALU.is_lt, ALU.mult)
            ch.link(dve.tensor_copy(a_loc, a_ipos[:, NT * WIN:]))
            ch.link(dve.tensor_tensor(a_pos.rearrange("p t j -> p (t j)"), a_pos.rearrange("p t j -> p (t j)"), a_wrap[:, 0:NT * WIN], ALU.add))
            mf = a_mask.rearrange("p j e -> p (j e)")
            ch.link(dve.tensor_scalar(mf, mf.bitcast(I32), -1.0, 1.0, ALU.mult, ALU.add))
            ch.link(dve.tensor_reduce(a_msum, mf.rearrange("p (b m) -> p b m", b=B), AX.X, ALU.add))
            ch.link(dve.tensor_scalar(a_msum, a_msum, -1.0, None, ALU.add))
            dve.wait_ge(off_mm, NT)
            u = a_u.rearrange("p t k -> p (t k)")
            tt = a_t.rearrange("p t k -> p (t k)")
            for b in range(B):
                ins = dve.tensor_tensor(a_u[:, b * QT:(b + 1) * QT, :], bank[2 + b][:, 0:QT * HK].rearrange("p (t k) -> p t k", t=QT),
                                        bc(a_boff.unsqueeze(1), [P, QT, HK]), ALU.add)
            ch.link(ins)
            ch.link(dve.tensor_tensor(u, u, a_ref, ALU.add))
            ch.link(dve.tensor_tensor(a_u, a_u, bc(a_loc.unsqueeze(2), [P, NT, HK]), ALU.add))
            half = QT * HK
            halves = [(b, slice(b * half, (b + 1) * half)) for b in range(B)]
            ch.link(dve.reciprocal(a_rlen, a_msum))
            for b, h in halves:
                ins = dve.tensor_scalar(tt[:, h], u[:, h], a_rlen[:, b:b + 1], MAGIC, ALU.mult, ALU.add)
            ch.link(ins)
            for b, h in halves:
                ins = dve.tensor_scalar(tt[:, h], tt[:, h], -MAGIC, a_msum[:, b:b + 1], ALU.add, ALU.mult)
            ch.link(ins)
            ch.link(dve.tensor_tensor(u, u, tt, ALU.subtract))
            for b, h in halves:
                ins = dve.tensor_scalar(tt[:, h], u[:, h], a_msum[:, b:b + 1], 0.0, ALU.mult, ALU.is_lt)
            ch.link(ins)
            for b, h in halves:
                ins = dve.scalar_tensor_tensor(u[:, h], tt[:, h], a_msum[:, b:b + 1], u[:, h], ALU.mult, ALU.add)
            ch.link(ins)
            ch.link(dve.tensor_scalar(u, u, 1.0 / float(M - 1), 2.0, ALU.mult, ALU.mult))
            ch.link(dve.tensor_scalar(u, u, -1.0, 1.0, ALU.add, ALU.add))
            ch.link(dve.tensor_scalar(u, u, float(M), -1.0, ALU.mult, ALU.add))
            ch.link(dve.tensor_scalar(u, u, 0.5, None, ALU.mult))
            ch.link(dve.tensor_tensor(a_t, a_u, bc(a_loc.unsqueeze(2), [P, NT, HK]), ALU.subtract))
            ch.link(dve.tensor_scalar(tt, tt, float(BACK), None, ALU.add))
            ch.link(dve.tensor_scalar(a_wrap, tt, float(M // 2), float(-M), ALU.is_ge, ALU.mult))
            ch.link(dve.tensor_tensor(tt, tt, a_wrap, ALU.add))
            ch.link(dve.tensor_scalar(a_wrap, tt, 0.0, None, ALU.is_ge))
            ch.link(dve.scalar_tensor_tensor(tt, tt, float(WIN - 1), a_wrap, ALU.is_le, ALU.mult))
            dve.tensor_reduce(a_cov[:, 0:1], tt, AX.X, ALU.add).then_inc(sum_ready, 1)
            dve.wait_ge(sum_ready, 1)
            def row_weights(t):
                W = a_W[:, t]
                ch.link(dve.tensor_tensor(W, bc(a_u[:, t, :].unsqueeze(2), [P, HK, WIN]), bc(a_pos[:, t, :].unsqueeze(1), [P, HK, WIN]), ALU.subtract))
                dve.scalar_tensor_tensor(W, W, -1.0, W, ALU.mult, ALU.min).then_inc(dist_ready, 1)

            def scores0(prod, S_out):
                return dve.tensor_reduce(S_out.rearrange("p h j -> p j h"), prod.rearrange("p j (h d) -> p j h d", h=H0), AX.X, ALU.add)

            def hkj(a):
                return a.rearrange("p (h k) j -> p h k j", h=H0)

            S_hj = a_S.rearrange("p j h -> p (j h)").rearrange("p (h j) -> p h j", h=H0)
            for t in range(NT):
                dve.wait_ge(q0_mm, NT)
                dve.tensor_tensor(a_q0[:, t, :], q0_bank(t), a_bq0, ALU.add).then_inc(q0_ready, 1)

            def rest(k):
                l, n, c, q = chunk_of(k)
                dve.wait_ge(prepk_hi, k + 1)
                if k >= PBUFS:
                    dve.wait_ge(prepk_lo, k - PBUFS + 1)
                src, dst, hi = bank[2 + k % 2][0:n, :], a_pr[k % PBUFS][0:n], a_ph[k % PBUFS][0][0:n]
                if l == 1:
                    ins = dve.tensor_tensor(dst, src, hi, ALU.subtract)
                else:
                    ins = dve.scalar_tensor_tensor(dst, src, a_bk[l][0:n, c:c + 1], hi, ALU.add, ALU.subtract)
                ins.then_inc(prepk_rest, 1)

            def kv0_rows(first, last):
                for t in range(first, last):
                    dve.wait_ge(kv0_mm, t + 1)
                    dve.wait_ge(table_written[t % 4], 16 * table_dmas(t - 4))
                    dve.tensor_tensor(a_kv0[t % 4], bank[4 + t % 2], a_bkv, ALU.add).then_inc(kv0_ready, 1)

            row_weights(0)
            row_weights(1)
            dve.wait_ge(kv0_ready, KT)
            dve.wait_ge(ld_bkv, 16)
            kv0_rows(KT, KT + 2)
            for t in range(NT):
                dve.wait_ge(prod_ready, t + 1)
                ins = scores0(a_prod[t % 2], S_hj)
                ins.then_inc(prodK_used, 1)
                dve.wait_ge(prodK_used, t + 1)
                dve.wait_ge(w_ready, t + 1)
                ch.link(dve.tensor_tensor(hkj(a_tmp), hkj(a_W[:, t]), bc(S_hj.unsqueeze(2), [P, H0, NK, WIN]), ALU.mult))
                ch.link(dve.tensor_reduce(a_sc[:, t, :], a_tmp, AX.X, ALU.add))
                kv0_rows(min(NCT, KT + 2 + 2 * t), min(NCT, KT + 4 + 2 * t))
                if t >= REST_LAG:
                    rest(t - REST_LAG)
                if t + 2 < NT:
                    row_weights(t + 2)
            dve.wait_ge(sum_mm, 1)
            dve.tensor_scalar(flag_i[:], bank[4][0:1, 0:1], float(P * NT * HK) - 0.5, None, ALU.is_lt).then_inc(flag_ready, 1)
            dve.wait_ge(flag_ready, 1)
            uncovered = dve.value_load(flag_i[0:1, 0:1], min_val=0, max_val=1)

            gen_links = [0]

            def general(loop0, use):
                with dve.If(uncovered):
                    for i in range(4):
                        dve.wait_ge(table_written[i], 16 * table_dmas(NCT - 4 + i))
                    if loop0 == 0:
                        dve.sem_inc(gen_used, 1)
                    for t in range(NT):
                        def link(ins):
                            gen_links[0] += 1
                            ins.then_inc(gen_chain, 1)
                            dve.wait_ge(gen_chain, gen_links[0])

                        link(dve.tensor_copy(a_gpos, a_pos[:, t, :]))
                        first = gen_links[0]
                        with dve.Fori(1, M // WIN) as s:
                            done = [0]

                            def step(ins):
                                done[0] += 1
                                ins.then_inc(gen_chain, 1)
                                dve.wait_ge(gen_chain, (s - 1) * GEN_LINKS + (first + done[0]))

                            step(dve.tensor_scalar(a_gpos, a_gpos, float(WIN), None, ALU.add))
                            step(dve.tensor_scalar(a_gwrap, a_gpos, float(M), float(-M), ALU.is_ge, ALU.mult))
                            step(dve.tensor_tensor(a_gpos, a_gpos, a_gwrap, ALU.add))
                            step(dve.tensor_tensor(a_gW, bc(a_u[:, t, :].unsqueeze(2), [P, HK, WIN]), bc(a_gpos.unsqueeze(1), [P, HK, WIN]), ALU.subtract))
                            step(dve.scalar_tensor_tensor(a_gW, a_gW, -1.0, a_gW, ALU.mult, ALU.min))
                            step(dve.tensor_scalar(a_gW, a_gW, 1.0, 0.0, ALU.add, ALU.max))
                            use(t, step, lambda: dve.wait_ge(gen_ld, s * 16 + 16 * (loop0 + t) * GEN_STEPS),
                                lambda ins: (ins.then_inc(gen_used, 1), dve.wait_ge(gen_used, s + ((loop0 + t) * GEN_STEPS + 1))))
                            assert done[0] == GEN_LINKS, done
                        gen_links[0] += GEN_STEPS * GEN_LINKS

            def more_scores(t, step, loaded, used):
                loaded()
                step(dve.tensor_tensor(gwin, gwin, bc(a_q0[:, t, :].unsqueeze(1), [P, WIN, D]), ALU.mult))
                used(scores0(gwin, S_hj))
                step(dve.tensor_tensor(hkj(a_tmp), hkj(a_gW), bc(S_hj.unsqueeze(2), [P, H0, NK, WIN]), ALU.mult))
                step(dve.tensor_reduce(a_small[:, 0:HK], a_tmp, AX.X, ALU.add))
                step(dve.tensor_tensor(a_sc[:, t, :], a_sc[:, t, :], a_small[:, 0:HK], ALU.add))

            def more_context(t, step, loaded, used):
                step(dve.tensor_tensor(a_tmp, a_gW, bc(a_sc[:, t, :].unsqueeze(2), [P, HK, WIN]), ALU.mult))
                step(dve.tensor_reduce(a_A[0], a_tmp.rearrange("p (h k) j -> p h j k", h=H0), AX.X, ALU.add))
                loaded()
                step(dve.tensor_tensor(gwin.rearrange("p j (h d) -> p j h d", h=H0), gwin.rearrange("p j (h d) -> p j h d", h=H0),
                                       bc(a_A[0].rearrange("p h j -> p j h").unsqueeze(3), [P, WIN, H0, HD0]), ALU.mult))
                used(dve.tensor_reduce(a_small, gwin.rearrange("p j e -> p e j"), AX.X, ALU.add))
                step(dve.tensor_tensor(ctx0[:, t, :], ctx0[:, t, :], a_small, ALU.add))

            general(0, more_scores)
            sc = a_sc.rearrange("p t (h k) -> p (t h) k", h=H0)
            ch.link(dve.tensor_reduce(a_mx, sc, AX.X, ALU.max))
            dve.tensor_tensor(sc, sc, bc(a_mx.unsqueeze(2), [P, NT * H0, NK]), ALU.subtract).then_inc(sub0_ready, 1)
            dve.wait_ge(exp0_ready, 1)
            ch.link(dve.tensor_reduce(a_sm, sc, AX.X, ALU.add))
            ch.link(dve.reciprocal(a_sm, a_sm))
            ch.link(dve.scalar_tensor_tensor(sc, sc, 0.5, bc(a_sm.unsqueeze(2), [P, NT * H0, NK]), ALU.mult, ALU.mult))

            def sum_rows(t):
                dve.wait_ge(prod_ready, NT + t + 1)
                dve.tensor_reduce(ctx0[:, t, :], a_prod[t % 2].rearrange("p j e -> p e j"), AX.X, ALU.add).then_inc(prodV_used, 1)

            dve.wait_ge(kv0_mm, NCT)

            def window_weights(t):
                if t:
                    dve.wait_ge(attw_ready, t)
                ch.link(dve.tensor_tensor(a_tmp, a_W[:, t], bc(a_sc[:, t, :].unsqueeze(2), [P, HK, WIN]), ALU.mult))
                if t >= 3:
                    dve.wait_ge(prod_ready, NT + t - 2)
                dve.tensor_reduce(a_A[t % 3], a_tmp.rearrange("p (h k) j -> p h j k", h=H0), AX.X, ALU.add).then_inc(attw_ready, 1)

            window_weights(0)
            window_weights(1)
            for t in range(NT):
                rest(NT + t - REST_LAG)
                if t + 2 < NT:
                    window_weights(t + 2)
                if t < NT - 1:
                    sum_rows(t)
            for k in range(KCHUNKS - REST_LAG, KCHUNKS):
                rest(k)
            sum_rows(NT - 1)
            dve.wait_ge(prodV_used, NT)
            general(NT, more_context)
            dve.sem_inc(ctxn_ready, NT)
            dve.wait_ge(i8_w, 16)
            ch.link(dve.tensor_reduce(i8wsc, i8w, AX.X, ALU.max, apply_absolute_value=True))
            ch.link(dve.tensor_scalar(i8wsc, i8wsc, 1e-12, 1.0 / 127.0, ALU.max, ALU.mult))
            ch.link(dve.reciprocal(i8wr, i8wsc))
            for i in range(DC):
                ch.link(dve.tensor_scalar(i8w[:, i], i8w[:, i], i8wr[:, i:i + 1], MAGIC, ALU.mult, ALU.add))
                ch.link(dve.tensor_scalar(i8w[:, i], i8w[:, i], -MAGIC, 127.0, ALU.add, ALU.min))
                ins = dve.tensor_scalar(i8wq[:, i], i8w[:, i], -127.0, None, ALU.max)
            ins.then_inc(i8_wq, 2)
            dve.wait_ge(tanh_ready, 2)
            add_out(0, tgx[:, 0:1])

            normalise(1)
            dve.wait_ge(xn_ready, 2 * NT)
            ch.link(dve.tensor_reduce(i8xsc, xn[:], AX.X, ALU.max, apply_absolute_value=True))
            ch.link(dve.tensor_scalar(i8xsc, i8xsc, 1e-12, 1.0 / 127.0, ALU.max, ALU.mult))
            ch.link(dve.reciprocal(i8xr, i8xsc))
            for t in range(NT):
                ins = dve.tensor_scalar(xn[:, t], xn[:, t], i8xr[:, t:t + 1], MAGIC, ALU.mult, ALU.add)
            ch.link(ins)
            ch.link(dve.tensor_scalar(xn[:], xn[:], -MAGIC, 127.0, ALU.add, ALU.min))
            for t in range(NT):
                dve.tensor_scalar(i8xq[:, t], xn[:, t], -127.0, None, ALU.max).then_inc(i8_xq, 1)
            dve.wait_ge(i8_qT, DC + 1)
            dve.wait_ge(i8_xq, NT)
            for t in range(NT):
                dve.wait_ge(out_mm, OUT_AT[1] * NT + t + 1)
                ch.link(dve.scalar_tensor_tensor(xn[:, t, :], bank[4 + t % 2][:, 0:D], i8xsc[:, t:t + 1], i8sc_bc, ALU.mult, ALU.mult))
                dve.scalar_tensor_tensor(x[:, t, :], xn[:, t, :], tgf[:, 0:1], x[:, t, :], ALU.mult, ALU.add).then_inc(x_ready, 1)
                if t:
                    tile_statistics(2, t - 1)

            def attention(l):
                H, dh, _ = ATT[l]
                n = min(P, EW[l])
                def split_queries(first, last):
                    for k in range(QCH0[l] + first, QCH0[l] + last):
                        dve.wait_ge(qp_evac, k + 1)
                        hi, mid, lo = qph[k % 2]
                        ch.link(dve.tensor_tensor(qr[k % 2][0:n], qf[k % 2][0:n], hi[0:n], ALU.subtract))
                        ch.link(dve.tensor_copy(mid[0:n], qr[k % 2][0:n]))
                        dve.tensor_tensor(lo[0:n], qr[k % 2][0:n], mid[0:n], ALU.subtract).then_inc(qp_split, 1)

                if l == 1:
                    dve.wait_ge(prepv_evac, 3 * NCT)
                dve.memset(bank[7], 0.0).then_inc(pv_done, 1)
                split_queries(0, 2)

                def reduce_half(uu, place):
                    g, col, hf = uu // HALVES, uu // 2 % (HG * QT), uu % 2
                    un = GROUP0[l] * HALVES + uu
                    gi = GROUP0[l] + g
                    dve.wait_ge(max_mm, un + 1)
                    if uu % HALVES == 0 and gi >= 2:
                        dve.wait_ge(max_fin, gi - 1)
                    dve.tensor_reduce(mxh[gi % 2][:, col, hf:hf + 1], bank[TURN_BANKS[place % 3]], AX.X, ALU.max).then_inc(max_red, 1)
                    if uu % HALVES == HALVES - 1:
                        dve.wait_ge(max_red, un + 1)
                        if gi >= 2:
                            dve.wait_ge(max_tr, gi - 1)
                        dve.tensor_reduce(mxg[gi % 2], mxh[gi % 2], AX.X, ALU.max).then_inc(max_fin, 1)

                def shift_low(g, place):
                    gi = GROUP0[l] + g
                    dve.wait_ge(max_hi, gi + 1)
                    dve.scalar_tensor_tensor(shp[gi % 2][1][0:HG * QT, :], bank[TURN_BANKS[place % 3]][0:HG * QT, 0:P], -1.0, shp[gi % 2][0][0:HG * QT, :],
                                             ALU.mult, ALU.subtract).then_inc(max_lo, 1)

                def normalise_context(g, place):
                    gi = GROUP0[l] + g
                    b, h0 = g // (H // HG), (g % (H // HG)) * HG
                    dve.wait_ge(pv_tr, gi + 1)
                    turned = bank[TURN_BANKS[place % 3]].rearrange("p (q h e) -> p q h e", q=QT, h=HG)
                    if gi:
                        dve.wait_ge(norm_ready, gi)
                    ch.link(dve.reciprocal(rsum, turned[:, :, :, dh]))
                    dst = xn[:, b * QT:(b + 1) * QT, h0 * dh:(h0 + HG) * dh].rearrange("p q (h e) -> p q h e", h=HG)
                    dve.tensor_tensor(dst, turned[:, :, :, 0:dh], bc(rsum.unsqueeze(3), [P, QT, HG, dh]), ALU.mult).then_inc(norm_ready, 1)

                for step in schedule(l):
                    if step[0] == "max":
                        if step[1] == 8:
                            split_queries(2, QCH0[l + 1] - QCH0[l])
                        reduce_half(*step[1:])
                    elif step[0] == "turn":
                        shift_low(*step[1:])
                    elif step[0] == "context":
                        normalise_context(*step[1:])
                    elif step[0] == "out":
                        _, (b, i), place = step
                        t = b * QT + 2 * i
                        dve.wait_ge(out_mm, OUT_AT[2 * l] * NT + t + 2)
                        dve.scalar_tensor_tensor(x[:, t:t + 2, :], bank[TURN_BANKS[place % 3]].rearrange("p (j d) -> p j d", j=2), tgx[:, l:l + 1],
                                                 x[:, t:t + 2, :], ALU.mult, ALU.add).then_inc(x_ready, 2)
                        for k in range(t - i, t + 1):
                            statistics(2 * l + 1, k)
                    elif step[0] == "variance":
                        tile_statistics(2 * l + 1, (step[1] + 1) * QT - 1)
                    elif step[0] == "normalise":
                        normalise_batch(2 * l + 1, step[1])

            normalise(2)
            attention(1)

            normalise(3, first=1)
            dve.wait_ge(lg_mm, 1)
            lg = bank[6][:, 0:NT * E_MOE].rearrange("p (t e) -> p t e", t=NT)
            dve.wait_ge(moe_small, 32)
            ch.link(dve.tensor_tensor(lgs, lg, bc(bg.unsqueeze(1), [P, NT, E_MOE]), ALU.add))
            ch.link(dve.tensor_reduce(lgm, lgs, AX.X, ALU.max))
            dve.tensor_tensor(lgs, lgs, bc(lgm, [P, NT, E_MOE]), ALU.subtract).then_inc(lg_exp_in, 1)
            for e in range(E_MOE):
                dve.memset(unit_base[:, e:e + 1], float(CAP * e))
                dve.memset(first_best[:, e:e + 1], float(E_MOE - e))
            for k in range(OVER):
                dve.memset(limits[:, k], (k + 1) * CAP + 0.5)
            for i in range(3):
                ins = dve.memset(sums[i][:, 0:E_MOE], 0.0)
            ch.link(ins)
            dve.wait_ge(lg_exp, 1)
            ch.link(dve.tensor_reduce(lgz, lge, AX.X, ALU.add))
            ch.link(dve.reciprocal(lgz, lgz))
            ch.link(dve.tensor_tensor(lge, lge, bc(lgz, [P, NT, E_MOE]), ALU.mult))
            ch.link(dve.tensor_reduce(lgm, lge, AX.X, ALU.max))
            ch.link(dve.tensor_tensor(lgs, lge, bc(lgm, [P, NT, E_MOE]), ALU.is_ge))
            ch.link(dve.tensor_tensor(lgs, lgs, bc(first_best.unsqueeze(1), [P, NT, E_MOE]), ALU.mult))
            ch.link(dve.tensor_reduce(idx2, lgs, AX.X, ALU.max))
            dve.tensor_tensor(onehot_b, lgs, bc(idx2, [P, NT, E_MOE]), ALU.is_equal).then_inc(onehot_ready, 1)
            ch.link(dve.tensor_tensor(lgs, lgs, bc(idx2, [P, NT, E_MOE]), ALU.is_equal))
            dve.tensor_tensor(mskd, lgs, lge, ALU.mult).then_inc(mask_ready, 1)
            dve.wait_ge(rank_mm, 1)
            ch.link(dve.tensor_reduce(counts, bank[4][:, 0:NT * E_MOE].rearrange("p (t e) -> p e t", t=NT), AX.X, ALU.add))
            ch.link(dve.tensor_tensor(over_cmp, bc(counts.unsqueeze(1), [P, OVER, E_MOE]), limits, ALU.is_gt))
            ch.link(dve.tensor_reduce(over_n, over_cmp.rearrange("p k e -> p e k"), AX.X, ALU.add))
            for i in range(3):
                src = sums[i][:, E_MOE - 2 ** i:2 * E_MOE - 2 ** i]
                ch.link(dve.tensor_tensor(sums[i + 1][:, E_MOE:], sums[i][:, E_MOE:], src, ALU.add))
            ch.link(dve.tensor_tensor(over_base, over_end, over_n, ALU.subtract))
            ch.link(dve.tensor_scalar(over_base, over_base, float(E_MOE - 1), float(CAP), ALU.add, ALU.mult))
            rank = bank[7][:, 0:NT * E_MOE].rearrange("p (t e) -> p t e", t=NT)
            for src, dst in ((rank, rank_tok), (bc(unit_base.unsqueeze(1), [P, NT, E_MOE]), base_tok), (bc(over_base.unsqueeze(1), [P, NT, E_MOE]), over_tok)):
                ch.link(dve.tensor_tensor(pick, lgs, src, ALU.mult))
                ch.link(dve.tensor_reduce(dst, pick, AX.X, ALU.add))
            ch.link(dve.tensor_scalar(is_over, rank_tok, CAP - 0.5, None, ALU.is_gt))
            ch.link(dve.tensor_tensor(over_tok, over_tok, base_tok, ALU.subtract))
            ch.link(dve.tensor_tensor(over_tok, over_tok, is_over, ALU.mult))
            ch.link(dve.tensor_tensor(base_tok, base_tok, rank_tok, ALU.add))
            ch.link(dve.tensor_tensor(base_tok, base_tok, over_tok, ALU.add))
            dve.tensor_copy(slot_i, base_tok).then_inc(slots_ready, 1)
            dve.wait_ge(den_mm, 1)
            ch.link(dve.tensor_reduce(den, bank[5][:, 0:NT * E_MOE].rearrange("p (t e) -> p e t", t=NT), AX.X, ALU.add))
            ch.link(dve.tensor_scalar(den, den, 1e-6, None, ALU.add))
            ch.link(dve.reciprocal(den, den))
            ch.link(dve.tensor_tensor(gate, mskd, bc(den.unsqueeze(1), [P, NT, E_MOE]), ALU.mult))
            ch.link(dve.tensor_reduce(gate_tok, gate, AX.X, ALU.add))
            dve.tensor_scalar(gate_tok, gate_tok, float(T), tgf[:, 1:2], ALU.mult, ALU.mult).then_inc(gate_ready, 1)
            for j in range(OVER):
                ins = dve.tensor_scalar(over_cmp[:, j], over_end, j + 0.5, None, ALU.is_lt)
            ch.link(ins)
            ch.link(dve.tensor_reduce(over_f[:, 0:OVER], over_cmp, AX.X, ALU.add))
            ch.link(dve.tensor_scalar(over_f[:, 0:OVER], over_f[:, 0:OVER], float(E_MOE - 1), None, ALU.min))
            ch.link(dve.tensor_scalar(over_f[:, OVER:OVER + 1], over_end[:, E_MOE - 1:E_MOE], 0.5, None, ALU.is_gt))
            dve.tensor_copy(over_i, over_f).then_inc(over_ready, 1)

            def copy_in(n, tr, xT, up):
                dve.wait_ge(tr, n + 1)
                if n >= 2:
                    dve.wait_ge(up, (n - 1) * (FM // UP_PER_BANK))
                dve.tensor_copy(unit_inT[n % 2], bank[6][:, 0:DC * CAP].rearrange("p (c s) -> p c s", c=DC)).then_inc(xT, 1)

            def copy_returned(n, down, yT, turn):
                dve.wait_ge(down, n + 1)
                if n >= 2:
                    dve.wait_ge(turn, n - 1)
                dve.tensor_copy(unit_outT[n % 2], bank[4 + n % 2][:, 0:DC * CAP].rearrange("p (c s) -> p c s", c=DC)).then_inc(yT, 1)

            def copy_out(n, out, turn, y):
                dve.wait_ge(turn, n + 1)
                dve.tensor_copy(out[0:SUB], bank[7][0:SUB].rearrange("p (i d) -> p i d", i=2)).then_inc(y, 1)

            def scan(n):
                dve.wait_ge(glu_raw[n % GLU_RAW], 16 * (n // GLU_RAW + 1))
                chunk = scan_buf[n % GLU_RAW].bitcast(I32)
                if n == 0:
                    dve.tensor_copy(scan_bits, chunk).then_inc(scan_done, 1)
                else:
                    dve.wait_ge(scan_done, n)
                    dve.tensor_tensor(scan_bits, scan_bits, chunk, ALU.bitwise_or).then_inc(scan_done, 1)

            scan(0)
            copy_in(0, unit_tr, unit_xT, unit_up)
            for e in range(E_MOE + 1):
                if e:
                    if e - 1 >= 2:
                        dve.wait_ge(unit_st[(e - 1) % 2], 16 * ((e - 1) // 2))
                    copy_out(e - 1, unit_out[(e - 1) % 2], unit_turn, unit_y)
                if e + 1 < E_MOE:
                    copy_in(e + 1, unit_tr, unit_xT, unit_up)
                if e < E_MOE:
                    copy_returned(e, unit_down, unit_yT, unit_turn)
                    for n in range(1 + e * SCAN_EACH, min(1 + (e + 1) * SCAN_EACH, GLU_CHUNKS)):
                        scan(n)
            dve.wait_ge(over_ready, 1)
            over = dve.value_load(over_i[0:1, OVER:OVER + 1], min_val=0, max_val=1)
            with dve.If(over):
                for i in range(2):
                    dve.wait_ge(unit_st[i], 16 * E_MOE // 2)
                for j in range(OVER):
                    copy_in(j, over_tr, over_xT, over_up)
                    copy_returned(j, over_down, over_yT, over_turn)
                    if j:
                        dve.wait_ge(over_st, 16 * j)
                    copy_out(j, unit_out[0], over_turn, over_y)
            dve.wait_ge(scan_done, GLU_CHUNKS)
            ch.link(dve.tensor_scalar(scan_bits, scan_bits, BF16_REST, None, ALU.bitwise_and))
            dve.tensor_reduce(low_sum, scan_bits, AX.X, ALU.max).then_inc(sum_ready, 1)
            dve.wait_ge(sum_mm, 2)
            dve.tensor_scalar(low_flags[:, 0:1], bank[6][0:1, 0:1], 0.5, None, ALU.is_gt).then_inc(flag_ready, 1)
            dve.tensor_scalar(low_flags[:, 1:2], bank[6][0:1, 0:1], 0.5, None, ALU.is_lt).then_inc(flag_ready, 1)
            for t in range(NT):
                dve.wait_ge(gathered[t // QT], 16 * QT)
                dve.scalar_tensor_tensor(x[:, t, :], xn[:, t, :], gate_tok[:, t:t + 1], x[:, t, :], ALU.mult, ALU.add).then_inc(x_ready, 1)
                if t:
                    tile_statistics(4, t - 1)

            normalise(4)
            attention(2)

            def split(src, hi, lo):
                ch.link(dve.tensor_copy(hi, src))
                return dve.tensor_tensor(lo, src, hi.bitcast(F32), ALU.subtract)

            def split_tokens(h):
                dve.wait_ge(xnT_ready, LN_AT[5] * 4 + 2 * (h + 1))
                cols = slice(h * CH, (h + 1) * CH)
                for c in range(DC):
                    split(xnT[:, c, cols], *(v[:, c, cols] for v in g_x)).then_inc(tokens_split, 1)

            def split_weights(n, low_weights):
                c = GLU_ORDER[n]
                dve.wait_ge(glu_raw[n % GLU_RAW], 16 * raw_loads(n))
                if c >= W3_FIRST:
                    rows3 = slice((c - W3_FIRST) * NF // W3_CHUNKS, (c - W3_FIRST + 1) * NF // W3_CHUNKS)
                    hi, lo = (v[:, rows3].rearrange("p f d -> p (f d)") for v in g_w3)
                else:
                    hi, lo = (v[:] for v in g_w[glu_buffer(n)])
                    before = [i for i in range(n) if GLU_ORDER[i] < W3_FIRST]
                    if len(before) >= 2:
                        dve.wait_ge(glu_mm, glu_blocks(before[-2]))
                if low_weights:
                    split(g_raw[n % GLU_RAW], hi, lo).then_inc(glu_split, 1)
                else:
                    dve.tensor_copy(hi, g_raw[n % GLU_RAW]).then_inc(glu_split, 1)

            def add_glu(h):
                for q in range(QT):
                    t = h * QT + q
                    dve.wait_ge(out_mm, OUT_AT[5] * NT + t + 1)
                    ch.link(dve.tensor_tensor(xn[:, t, :], bank[6 + t % 2][:, 0:D], gs3, ALU.mult))
                    dve.scalar_tensor_tensor(x[:, t, :], xn[:, t, :], tgf[:, 2:3], x[:, t, :], ALU.mult, ALU.add).then_inc(x_ready, 1)
                    if q:
                        tile_statistics(6, t - 1)
                if h == 0:
                    tile_statistics(6, QT - 1)

            def gated_unit(low_weights):
                split_weights(0, low_weights)
                split_weights(1, low_weights)
                normalise(5, first=1)
                split_tokens(0)
                split_tokens(1)
                dve.wait_ge(glu_ld, 16 * 5)
                a = 0
                for n, c in enumerate(GLU_ORDER):
                    if c < W3_FIRST:
                        for _ in range(UP_FS if c < UP_CHUNKS else 1):
                            layer, f = a // NF % 3, a % NF
                            if a == BLOCKS + 2 * NF:
                                normalise_batch(6, 0)
                            dve.wait_ge(glu_act, a + 1)
                            if layer == 0:
                                if a >= 2:
                                    dve.wait_ge(act_split, a - 1)
                                ch.link(dve.scalar_tensor_tensor(g_tmp[a % 2], bank[2 + f % 2], gsc[:, 1, f:f + 1], g_silu[a % 2], ALU.mult, ALU.mult))
                            if layer == 0:
                                dve.tensor_copy(g_a[0][0][:, f, :], g_tmp[a % 2]).then_inc(gated_high, 1)
                            else:
                                split(g_tmp[a % 2], *(v[:, f, :] for v in g_a[layer % 2])).then_inc(act_split, 1)
                            a += 1
                    if n + 2 < len(GLU_ORDER):
                        split_weights(n + 2, low_weights)
                    if c == len(GLU_HALF) - 1:
                        add_glu(glu_half(n))

            links = ch.n
            low, no_low = (dve.value_load(low_flags[0:1, i:i + 1], min_val=0, max_val=1) for i in range(2))
            with dve.If(no_low):
                gated_unit(False)
                dve.sem_inc(chain_dve, len(GLU_ORDER))
            links_without = ch.n
            ch.n = links
            with dve.If(low):
                gated_unit(True)
            assert ch.n == links_without + len(GLU_ORDER)

            normalise(6, first=1)
            attention(3)

            normalise(7, first=1)
            dve.wait_ge(fin_ld, 16 * 5)
            ch.link(dve.tensor_scalar(mom, mmu, -1.0, 1.0, ALU.mult, ALU.add))
            dve.wait_ge(xnT_ready, (LN_AT[7] + 1) * 4)
            for i, dst in ((1, xk), (0, xr)):
                for b in range(B):
                    lo, hi = b * S, (b + 1) * S
                    for c in range(DC):
                        ch.link(dve.tensor_scalar(dst[:, c, lo:hi], xnT[:, c, lo:hi], mmu[:, i, c:c + 1], None, ALU.mult))
                        dve.scalar_tensor_tensor(dst[:, c, lo + 1:hi], xnT[:, c, lo:hi - 1], mom[:, i, c:c + 1], dst[:, c, lo + 1:hi],
                                                 ALU.mult, ALU.add).then_inc(mix_ready, 1)
            for i in range(B * DC):
                h, c = i // DC, i % DC
                dve.wait_ge(rk_act, i + 1)
                ka = kact[:, c, h * CH:(h + 1) * CH]
                dve.tensor_tensor(ka, ka, ka, ALU.mult).then_inc(rk_sq, 1)
            for t in range(NT):
                dve.wait_ge(fv_mm, t + 1)
                dve.wait_ge(rk_act, B * DC + t + 1)
                ch2 = dve.tensor_tensor(rv[:, t, :], rv[:, t, :], bank[4 + t % 2][:, 0:D], ALU.mult)
                ch2.then_inc(rv_ready, 1)
                dve.wait_ge(rv_ready, t + 1)
                dve.scalar_tensor_tensor(x[:, t, :], rv[:, t, :], tgf[:, 3:4], x[:, t, :], ALU.mult, ALU.add).then_inc(x_ready, 1)


def kernel(**inputs):
    import numpy as _np
    import concourse.bacc as _bacc
    from concourse import mybir as _mybir
    from concourse.bass_utils import run_bass_kernel_spmd as _run

    a = {k: _np.asarray(v) for k, v in inputs.items()}
    heads = lambda m: m.transpose(1, 0, 2).reshape(m.shape[1], -1)
    cat = lambda *m: _np.concatenate(m, axis=-1)
    cols = lambda v: v.reshape(-1, min(P, v.size)).T
    up = _np.stack([a["L2_ffn_w1_w"].T, a["L2_ffn_w2_w"].T]).reshape(2, DC, P, UP_CHUNKS, UP_FS * P).transpose(3, 2, 0, 1, 4)
    hidden = [a[f"L2_ffn_h{i}_w"].T.reshape(NF, P, NF, P).transpose(2, 1, 0, 3) for i in (1, 2)]
    last = a["L2_ffn_w3_w"].T.reshape(W3_CHUNKS, NF // W3_CHUNKS, P, D).transpose(0, 2, 1, 3)
    chunks = _np.concatenate([m.reshape(-1, P, GC) for m in (up, *hidden, last)])
    arrays = {
        "b0qT": cols(a["L0_xattn_bq"]),
        "x": a["x"].reshape(T, D), "ctxT": a["ctx_1024"].reshape(CT, D).T, "mask": a["mask_BxS2_if0"],
        "g_xattn": a["g_xattn"], "g_ffn": a["g_ffn"],
        "w0kv": cat(a["L0_xattn_Wk"].T, a["L0_xattn_Wv"].T), "b0kv": cat(a["L0_xattn_bk"], a["L0_xattn_bv"]),
        "w0q": a["L0_xattn_Wq"].T, "b0q": a["L0_xattn_bq"], "woff": a["L0_xattn_Woff"].T, "boff": a["L0_xattn_boff"],
        "w0o": a["L0_xattn_Wo"].T, "b0o": a["L0_xattn_bo"], "i8rhsT": a["L0_ffn_rhs"].T,
        "wq1": heads(a["L1_xattn_Wq"]), "wkv1": cat(heads(a["L1_xattn_Wk"]), heads(a["L1_xattn_Wv"])), "wo1": a["L1_xattn_Wo"],
        "wg": a["L1_ffn_Wg"], "bg": a["L1_ffn_bg"], "w1": a["L1_ffn_W1"], "w2": a["L1_ffn_W2"],
        "glu_w": chunks, "s1": cols(a["L2_ffn_w1_s"]), "s2": cols(a["L2_ffn_w2_s"]), "sh1": cols(a["L2_ffn_h1_s"]),
        "sh2": cols(a["L2_ffn_h2_s"]), "s3": a["L2_ffn_w3_s"],
        "w_r": a["L3_ffn_W_r"].T, "w_k": a["L3_ffn_W_k"].T, "w_v": a["L3_ffn_W_v"].T, "mu_r": cols(a["L3_ffn_mu_r"]), "mu_k": cols(a["L3_ffn_mu_k"]),
    }
    for l in (2, 3):
        p = f"L{l}_xattn_"
        arrays |= {f"wq{l}": a[p + "Wq"], f"wkv{l}": cat(a[p + "Wk"], a[p + "Wv"]), f"wo{l}": a[p + "Wo"], f"bq{l}": cols(a[p + "bq"]),
                   f"bk{l}": cols(a[p + "bk"]), f"bv{l}": a[p + "bv"], f"bo{l}": a[p + "bo"]}
    nc = _bacc.Bacc("TRN2", target_bir_lowering=False, num_devices=1)
    io, feed = {}, {}
    for name, v in arrays.items():
        feed[f"in_{name}"] = _np.ascontiguousarray(v)
        io[name] = nc.dram_tensor(f"in_{name}", feed[f"in_{name}"].shape, _mybir.dt.from_np(feed[f"in_{name}"].dtype), kind="ExternalInput").ap()
    io["out"] = nc.dram_tensor("out_0", (T, D), F32, kind="ExternalOutput").ap()
    build(nc, io)
    got = _run(nc, [feed], core_ids=[0]).results[0]["out_0"]
    return _np.asarray(got).reshape(B, S, D)
```
